# Optimizing a Trainium2 kernel written in Bass

```python
import numpy as np
import jax
import jax.numpy as jnp

def _softmax(x, axis=-1):
    return jax.nn.softmax(x, axis=axis)

def _gelu(x):
    return jax.nn.gelu(x, approximate=True)

def _silu(x):
    return jax.nn.silu(x)

def _sigmoid(x):
    return jax.nn.sigmoid(x)

def _layernorm(x, axis=-1, eps=1e-05):
    m = jnp.mean(x, axis=axis, keepdims=True)
    v = jnp.var(x, axis=axis, keepdims=True)
    return (x - m) / jnp.sqrt(v + eps)

def _scatter_add(tgt, idx, src, axis=0):
    return tgt.at[idx].add(src)

def _segment_sum(src, seg, n):
    return jax.ops.segment_sum(src, seg, n)
kernel_name = 'mk_lm_tower_d2_tok_ids512_r4_0f3d0c'

def setup_inputs(seed: int=0):
    np.random.seed(seed)
    _w = jnp.asarray

    def _rec_inputs():
        import jax
        import jax.numpy as jnp
        _rk = jax.random.key(seed)
        x = jax.random.randint(jax.random.fold_in(_rk, 1), (4, 512), 0, 16, jnp.int32)
        return x
    x = _rec_inputs()

    def _L0_tok_setup():
        import jax, jax.numpy as jnp
        import numpy as np
        VOCAB = 16
        D_MODEL = 128
        D_EMB = int(D_MODEL * 0.7)
        D_STFT = D_MODEL - D_EMB
        N_FFT = 64
        HOP = 64
        N_FREQ = N_FFT // 2 + 1
        B, L = (4, 2048)

        def _stft_mag(signal):
            pad = N_FFT // 2
            padded = jnp.pad(signal, ((0, 0), (pad, pad)), mode='reflect')
            n_frames = signal.shape[1] // HOP + 1
            idx = jnp.arange(n_frames)[:, None] * HOP + jnp.arange(N_FFT)[None, :]
            window = 0.5 - 0.5 * jnp.cos(2.0 * jnp.pi * jnp.arange(N_FFT) / N_FFT)
            frames = padded[:, idx] * window.astype(signal.dtype)
            return jnp.abs(jnp.fft.rfft(frames, axis=-1))
        key = jax.random.key(seed)
        k1, k2, k3, k4 = jax.random.split(key, 4)
        input_ids = jax.random.randint(k1, (B, L), 0, VOCAB)
        emb_table = jax.random.normal(k2, (VOCAB, D_EMB), dtype=jnp.float32) * 0.02
        proj_w = jax.random.normal(k3, (VOCAB * N_FREQ, D_STFT), dtype=jnp.float32) * 0.02
        proj_b = jnp.zeros((D_STFT,), dtype=jnp.float32)
        return {'input_ids': input_ids, 'emb_table': emb_table, 'proj_w': proj_w, 'proj_b': proj_b}
    _L0_tok_all = _L0_tok_setup()
    _L0_tok_in = {k: v for k, v in _L0_tok_all.items() if k in ('emb_table', 'proj_w', 'proj_b')}
    del _L0_tok_all

    def _L0_attn_setup():
        import jax, jax.numpy as jnp
        import numpy as np
        import math
        key = jax.random.key(seed)
        k_x, k_q, k_k, k_v, k_o = jax.random.split(key, 5)
        B, S, D_IN, H, D_K, D_V, D_OUT = (1, 1024, 128, 8, 64, 64, 128)
        scale = 0.02
        return {'x': jax.random.normal(k_x, (B, S, D_IN), dtype=jnp.float32), 'W_q': jax.random.uniform(k_q, (H, D_IN, D_K), dtype=jnp.float32) * scale, 'W_k': jax.random.uniform(k_k, (H, D_IN, D_K), dtype=jnp.float32) * scale, 'W_v': jax.random.uniform(k_v, (H, D_IN, D_V), dtype=jnp.float32) * scale, 'W_o': jax.random.uniform(k_o, (H, D_V, D_OUT), dtype=jnp.float32) * scale}
    _L0_attn_all = _L0_attn_setup()
    _L0_attn_in = {k: v for k, v in _L0_attn_all.items() if k in ('W_q', 'W_k', 'W_v', 'W_o')}
    del _L0_attn_all

    def _L0_ffn_setup():
        import jax, jax.numpy as jnp
        import numpy as np
        from jax import lax
        B, S, IN, D, E, NH = (8, 128, 128, 256, 4, 16)
        DH = D // NH
        EPS = 1e-05
        SCALE = np.float32(1.0 / np.sqrt(DH))

        def _ln(x, g, b):
            m = x.mean(-1, keepdims=True)
            v = ((x - m) ** 2).mean(-1, keepdims=True)
            return (x - m) * lax.rsqrt(v + EPS) * g + b

        def _lstm_dir(x, Wi, Wh, b):
            bsz = x.shape[0]
            h0 = jnp.zeros((bsz, Wh.shape[0]), x.dtype)

            def step(carry, xt):
                h, c = carry
                zg = xt @ Wi + h @ Wh + b
                i, f, g, o = jnp.split(zg, 4, axis=-1)
                c = jax.nn.sigmoid(f) * c + jax.nn.sigmoid(i) * jnp.tanh(g)
                h = jax.nn.sigmoid(o) * jnp.tanh(c)
                return ((h, c), h)
            _, hs = lax.scan(step, (h0, h0), jnp.swapaxes(x, 0, 1))
            return jnp.swapaxes(hs, 0, 1)

        def _expert(x, p):
            ew1, eb1, ew2, eb2, eg, ebeta, aiw, aib, aow, aob, wif, whf, bf, wibk, whbk, bbk, sw1, sb1, sw2, sb2, tw1, tb1, tw2, tb2, dw1, db1, dw2, db2, dg, dbeta = p
            h = _ln(jax.nn.relu(x @ ew1 + eb1) @ ew2 + eb2, eg, ebeta)
            qkv = h @ aiw + aib
            q, k, v = jnp.split(qkv, 3, axis=-1)

            def heads(t):
                return t.reshape(t.shape[0], t.shape[1], NH, DH).transpose(0, 2, 1, 3)
            q, k, v = (heads(q), heads(k), heads(v))
            attn = jax.nn.softmax(jnp.einsum('bhqd,bhkd->bhqk', q, k) * SCALE, axis=-1)
            o = jnp.einsum('bhqk,bhkd->bhqd', attn, v).transpose(0, 2, 1, 3).reshape(h.shape)
            h = o @ aow + aob
            hf = _lstm_dir(h, wif, whf, bf)
            hb = _lstm_dir(h[:, ::-1], wibk, whbk, bbk)[:, ::-1]
            mem = jnp.concatenate([hf, hb], axis=-1)
            gate_s = jax.nn.sigmoid(jax.nn.relu(mem @ sw1 + sb1) @ sw2 + sb2)
            gate_t = jnp.tanh(jax.nn.relu(mem @ tw1 + tb1) @ tw2 + tb2)
            g = gate_s * gate_t
            return _ln(jax.nn.relu(g @ dw1 + db1) @ dw2 + db2, dg, dbeta)

        def _forward(x, router_w, router_b, *p):
            outs = jax.vmap(lambda pe: _expert(x, pe))(tuple(p))
            w = jax.nn.softmax(x @ router_w + router_b, axis=-1)
            return jnp.einsum('ebsd,bse->bsd', outs, w)
        key = jax.random.key(seed)
        ks = iter(jax.random.split(key, 64))

        def rn(shape, scale=0.02):
            return jax.random.normal(next(ks), shape, dtype=jnp.float32) * scale
        z = lambda shape: jnp.zeros(shape, dtype=jnp.float32)
        return {'x': jax.random.normal(next(ks), (B, S, IN), dtype=jnp.float32), 'router_w': rn((IN, E)), 'router_b': z((E,)), 'enc_w1': rn((E, IN, D)), 'enc_b1': z((E, D)), 'enc_w2': rn((E, D, D)), 'enc_b2': z((E, D)), 'enc_g': jnp.ones((E, D), jnp.float32), 'enc_beta': z((E, D)), 'attn_in_w': rn((E, D, 3 * D)), 'attn_in_b': z((E, 3 * D)), 'attn_out_w': rn((E, D, D)), 'attn_out_b': z((E, D)), 'lstm_wi_f': rn((E, D, 4 * D)), 'lstm_wh_f': rn((E, D, 4 * D)), 'lstm_b_f': z((E, 4 * D)), 'lstm_wi_b': rn((E, D, 4 * D)), 'lstm_wh_b': rn((E, D, 4 * D)), 'lstm_b_b': z((E, 4 * D)), 'sig_w1': rn((E, 2 * D, D)), 'sig_b1': z((E, D)), 'sig_w2': rn((E, D, D)), 'sig_b2': z((E, D)), 'tan_w1': rn((E, 2 * D, D)), 'tan_b1': z((E, D)), 'tan_w2': rn((E, D, D)), 'tan_b2': z((E, D)), 'dec_w1': rn((E, D, D)), 'dec_b1': z((E, D)), 'dec_w2': rn((E, D, IN)), 'dec_b2': z((E, IN)), 'dec_g': jnp.ones((E, IN), jnp.float32), 'dec_beta': z((E, IN))}
    _L0_ffn_all = _L0_ffn_setup()
    _L0_ffn_in = {k: v for k, v in _L0_ffn_all.items() if k in ('router_w', 'router_b', 'enc_w1', 'enc_b1', 'enc_w2', 'enc_b2', 'enc_g', 'enc_beta', 'attn_in_w', 'attn_in_b', 'attn_out_w', 'attn_out_b', 'lstm_wi_f', 'lstm_wh_f', 'lstm_b_f', 'lstm_wi_b', 'lstm_wh_b', 'lstm_b_b', 'sig_w1', 'sig_b1', 'sig_w2', 'sig_b2', 'tan_w1', 'tan_b1', 'tan_w2', 'tan_b2', 'dec_w1', 'dec_b1', 'dec_w2', 'dec_b2', 'dec_g', 'dec_beta')}
    del _L0_ffn_all

    def _L1_attn_setup():
        import jax, jax.numpy as jnp
        import numpy as np
        BATCH, SEQ, D_MODEL, D_STATE = (64, 512, 128, 64)
        DT_MIN, DT_MAX = (0.001, 0.1)
        LN_EPS = 1e-05
        key = jax.random.key(seed)
        ks = jax.random.split(key, 6)
        x = jax.random.normal(ks[0], (BATCH, SEQ, D_MODEL), dtype=jnp.float32)
        A_log = jnp.log(jnp.linspace(1.0, 0.1, D_STATE)).astype(jnp.float32)
        xav = np.sqrt(2.0 / (D_STATE + D_MODEL)).astype(np.float32)
        B_mat = jax.random.normal(ks[1], (D_STATE, D_MODEL), dtype=jnp.float32) * xav
        C_mat = jax.random.normal(ks[2], (D_MODEL, D_STATE), dtype=jnp.float32) * xav
        D_vec = jax.random.normal(ks[3], (D_MODEL,), dtype=jnp.float32)
        dt_w = jax.random.uniform(ks[4], (1, D_MODEL), minval=-0.1, maxval=0.1, dtype=jnp.float32)
        dt_b = jax.random.uniform(ks[5], (1,), minval=-0.1, maxval=0.1, dtype=jnp.float32)
        gamma = jnp.ones((D_MODEL,), dtype=jnp.float32)
        beta = jnp.zeros((D_MODEL,), dtype=jnp.float32)
        return {'x': x, 'A_log': A_log, 'B_mat': B_mat, 'C_mat': C_mat, 'D_vec': D_vec, 'dt_w': dt_w, 'dt_b': dt_b, 'gamma': gamma, 'beta': beta}
    _L1_attn_all = _L1_attn_setup()
    _L1_attn_in = {k: v for k, v in _L1_attn_all.items() if k in ('A_log', 'B_mat', 'C_mat', 'D_vec', 'dt_w', 'dt_b', 'gamma', 'beta')}
    del _L1_attn_all

    def _L1_ffn_setup():
        import jax, jax.numpy as jnp
        import numpy as np
        T = 128
        B = 64
        C = 256

        def _triu_apply(x, W, b):
            Wm = jnp.tril(W)
            return jnp.einsum('bct,st->bcs', x, Wm) + b
        key = jax.random.key(seed)
        ks = jax.random.split(key, 5)
        x = jax.random.normal(ks[0], (B, C, T), dtype=jnp.float32)
        scale = 1.0 / jnp.sqrt(jnp.arange(1, T + 1, dtype=jnp.float32))[:, None]
        W1 = jax.random.uniform(ks[1], (T, T), jnp.float32, -1.0, 1.0) * scale
        b1 = jax.random.uniform(ks[2], (T,), jnp.float32, -1.0, 1.0) * scale[:, 0]
        W2 = jax.random.uniform(ks[3], (T, T), jnp.float32, -1.0, 1.0) * scale
        b2 = jax.random.uniform(ks[4], (T,), jnp.float32, -1.0, 1.0) * scale[:, 0]
        return {'x': x, 'W1': W1, 'b1': b1, 'W2': W2, 'b2': b2}
    _L1_ffn_all = _L1_ffn_setup()
    _L1_ffn_in = {k: v for k, v in _L1_ffn_all.items() if k in ('W1', 'b1', 'W2', 'b2')}
    del _L1_ffn_all
    return {'x': x, 'L0_tok_emb_table': _L0_tok_in['emb_table'], 'L0_tok_proj_w': _L0_tok_in['proj_w'], 'L0_tok_proj_b': _L0_tok_in['proj_b'], 'L0_attn_W_q': _L0_attn_in['W_q'], 'L0_attn_W_k': _L0_attn_in['W_k'], 'L0_attn_W_v': _L0_attn_in['W_v'], 'L0_attn_W_o': _L0_attn_in['W_o'], 'L0_ffn_router_w': _L0_ffn_in['router_w'], 'L0_ffn_router_b': _L0_ffn_in['router_b'], 'L0_ffn_enc_w1': _L0_ffn_in['enc_w1'], 'L0_ffn_enc_b1': _L0_ffn_in['enc_b1'], 'L0_ffn_enc_w2': _L0_ffn_in['enc_w2'], 'L0_ffn_enc_b2': _L0_ffn_in['enc_b2'], 'L0_ffn_enc_g': _L0_ffn_in['enc_g'], 'L0_ffn_enc_beta': _L0_ffn_in['enc_beta'], 'L0_ffn_attn_in_w': _L0_ffn_in['attn_in_w'], 'L0_ffn_attn_in_b': _L0_ffn_in['attn_in_b'], 'L0_ffn_attn_out_w': _L0_ffn_in['attn_out_w'], 'L0_ffn_attn_out_b': _L0_ffn_in['attn_out_b'], 'L0_ffn_lstm_wi_f': _L0_ffn_in['lstm_wi_f'], 'L0_ffn_lstm_wh_f': _L0_ffn_in['lstm_wh_f'], 'L0_ffn_lstm_b_f': _L0_ffn_in['lstm_b_f'], 'L0_ffn_lstm_wi_b': _L0_ffn_in['lstm_wi_b'], 'L0_ffn_lstm_wh_b': _L0_ffn_in['lstm_wh_b'], 'L0_ffn_lstm_b_b': _L0_ffn_in['lstm_b_b'], 'L0_ffn_sig_w1': _L0_ffn_in['sig_w1'], 'L0_ffn_sig_b1': _L0_ffn_in['sig_b1'], 'L0_ffn_sig_w2': _L0_ffn_in['sig_w2'], 'L0_ffn_sig_b2': _L0_ffn_in['sig_b2'], 'L0_ffn_tan_w1': _L0_ffn_in['tan_w1'], 'L0_ffn_tan_b1': _L0_ffn_in['tan_b1'], 'L0_ffn_tan_w2': _L0_ffn_in['tan_w2'], 'L0_ffn_tan_b2': _L0_ffn_in['tan_b2'], 'L0_ffn_dec_w1': _L0_ffn_in['dec_w1'], 'L0_ffn_dec_b1': _L0_ffn_in['dec_b1'], 'L0_ffn_dec_w2': _L0_ffn_in['dec_w2'], 'L0_ffn_dec_b2': _L0_ffn_in['dec_b2'], 'L0_ffn_dec_g': _L0_ffn_in['dec_g'], 'L0_ffn_dec_beta': _L0_ffn_in['dec_beta'], 'L1_attn_A_log': _L1_attn_in['A_log'], 'L1_attn_B_mat': _L1_attn_in['B_mat'], 'L1_attn_C_mat': _L1_attn_in['C_mat'], 'L1_attn_D_vec': _L1_attn_in['D_vec'], 'L1_attn_dt_w': _L1_attn_in['dt_w'], 'L1_attn_dt_b': _L1_attn_in['dt_b'], 'L1_attn_gamma': _L1_attn_in['gamma'], 'L1_attn_beta': _L1_attn_in['beta'], 'L1_ffn_W1': _L1_ffn_in['W1'], 'L1_ffn_b1': _L1_ffn_in['b1'], 'L1_ffn_W2': _L1_ffn_in['W2'], 'L1_ffn_b2': _L1_ffn_in['b2']}

def reference(x, L0_tok_emb_table, L0_tok_proj_w, L0_tok_proj_b, L0_attn_W_q, L0_attn_W_k, L0_attn_W_v, L0_attn_W_o, L0_ffn_router_w, L0_ffn_router_b, L0_ffn_enc_w1, L0_ffn_enc_b1, L0_ffn_enc_w2, L0_ffn_enc_b2, L0_ffn_enc_g, L0_ffn_enc_beta, L0_ffn_attn_in_w, L0_ffn_attn_in_b, L0_ffn_attn_out_w, L0_ffn_attn_out_b, L0_ffn_lstm_wi_f, L0_ffn_lstm_wh_f, L0_ffn_lstm_b_f, L0_ffn_lstm_wi_b, L0_ffn_lstm_wh_b, L0_ffn_lstm_b_b, L0_ffn_sig_w1, L0_ffn_sig_b1, L0_ffn_sig_w2, L0_ffn_sig_b2, L0_ffn_tan_w1, L0_ffn_tan_b1, L0_ffn_tan_w2, L0_ffn_tan_b2, L0_ffn_dec_w1, L0_ffn_dec_b1, L0_ffn_dec_w2, L0_ffn_dec_b2, L0_ffn_dec_g, L0_ffn_dec_beta, L1_attn_A_log, L1_attn_B_mat, L1_attn_C_mat, L1_attn_D_vec, L1_attn_dt_w, L1_attn_dt_b, L1_attn_gamma, L1_attn_beta, L1_ffn_W1, L1_ffn_b1, L1_ffn_W2, L1_ffn_b2):
    import jax
    import jax.numpy as jnp

    def _L0_tok_ref(input_ids, emb_table, proj_w, proj_b):
        import jax, jax.numpy as jnp
        import numpy as np
        VOCAB = 16
        D_MODEL = 128
        D_EMB = int(D_MODEL * 0.7)
        D_STFT = D_MODEL - D_EMB
        N_FFT = 64
        HOP = 64
        N_FREQ = N_FFT // 2 + 1
        B, L = (4, 2048)

        def _stft_mag(signal):
            pad = N_FFT // 2
            padded = jnp.pad(signal, ((0, 0), (pad, pad)), mode='reflect')
            n_frames = signal.shape[1] // HOP + 1
            idx = jnp.arange(n_frames)[:, None] * HOP + jnp.arange(N_FFT)[None, :]
            window = 0.5 - 0.5 * jnp.cos(2.0 * jnp.pi * jnp.arange(N_FFT) / N_FFT)
            frames = padded[:, idx] * window.astype(signal.dtype)
            return jnp.abs(jnp.fft.rfft(frames, axis=-1))
        b, seq_len = input_ids.shape
        word_embeds = emb_table[input_ids]
        onehot = jax.nn.one_hot(input_ids, VOCAB, dtype=jnp.float32)
        signal = onehot.transpose(0, 2, 1).reshape(b * VOCAB, seq_len)
        spec = _stft_mag(signal)
        n_frames = spec.shape[1]
        stft_mag = spec.reshape(b, VOCAB, n_frames, N_FREQ).transpose(0, 1, 3, 2)
        stft_to_up = stft_mag.transpose(0, 2, 1, 3).reshape(b, N_FREQ * VOCAB, n_frames)
        up_idx = jnp.arange(seq_len) * n_frames // seq_len
        stft_up = stft_to_up[:, :, up_idx]
        feats = stft_up.transpose(0, 2, 1)
        stft_enc = jnp.einsum('bli,io->blo', feats, proj_w) + proj_b
        return jnp.concatenate([word_embeds, stft_enc], axis=-1)

    def _L0_attn_ref(x, W_q, W_k, W_v, W_o):
        import jax, jax.numpy as jnp
        import numpy as np
        import math
        S = x.shape[-2]
        d_key = W_k.shape[-1]
        Q = jnp.einsum('hjk,blj->bhlk', W_q, x)
        K = jnp.einsum('hjk,blj->bhlk', W_k, x)
        V = jnp.einsum('hjk,blj->bhlk', W_v, x)
        mask = jnp.triu(jnp.ones((S, S), dtype=bool), k=1)
        scores = jnp.einsum('bhik,bhjk->bhij', Q, K)
        scores = jnp.where(mask, -jnp.inf, scores)
        weights = jax.nn.softmax(scores / math.sqrt(d_key), axis=-1)
        weights = jnp.where(mask, 0.0, weights)
        values = jnp.einsum('bhij,bhjv->bhiv', weights, V)
        return jnp.einsum('hvk,bhlv->blk', W_o, values)

    def _L0_ffn_ref(x, router_w, router_b, enc_w1, enc_b1, enc_w2, enc_b2, enc_g, enc_beta, attn_in_w, attn_in_b, attn_out_w, attn_out_b, lstm_wi_f, lstm_wh_f, lstm_b_f, lstm_wi_b, lstm_wh_b, lstm_b_b, sig_w1, sig_b1, sig_w2, sig_b2, tan_w1, tan_b1, tan_w2, tan_b2, dec_w1, dec_b1, dec_w2, dec_b2, dec_g, dec_beta):
        import jax, jax.numpy as jnp
        import numpy as np
        from jax import lax
        B, S, IN, D, E, NH = (8, 128, 128, 256, 4, 16)
        DH = D // NH
        EPS = 1e-05
        SCALE = np.float32(1.0 / np.sqrt(DH))

        def _ln(x, g, b):
            m = x.mean(-1, keepdims=True)
            v = ((x - m) ** 2).mean(-1, keepdims=True)
            return (x - m) * lax.rsqrt(v + EPS) * g + b

        def _lstm_dir(x, Wi, Wh, b):
            bsz = x.shape[0]
            h0 = jnp.zeros((bsz, Wh.shape[0]), x.dtype)

            def step(carry, xt):
                h, c = carry
                zg = xt @ Wi + h @ Wh + b
                i, f, g, o = jnp.split(zg, 4, axis=-1)
                c = jax.nn.sigmoid(f) * c + jax.nn.sigmoid(i) * jnp.tanh(g)
                h = jax.nn.sigmoid(o) * jnp.tanh(c)
                return ((h, c), h)
            _, hs = lax.scan(step, (h0, h0), jnp.swapaxes(x, 0, 1))
            return jnp.swapaxes(hs, 0, 1)

        def _expert(x, p):
            ew1, eb1, ew2, eb2, eg, ebeta, aiw, aib, aow, aob, wif, whf, bf, wibk, whbk, bbk, sw1, sb1, sw2, sb2, tw1, tb1, tw2, tb2, dw1, db1, dw2, db2, dg, dbeta = p
            h = _ln(jax.nn.relu(x @ ew1 + eb1) @ ew2 + eb2, eg, ebeta)
            qkv = h @ aiw + aib
            q, k, v = jnp.split(qkv, 3, axis=-1)

            def heads(t):
                return t.reshape(t.shape[0], t.shape[1], NH, DH).transpose(0, 2, 1, 3)
            q, k, v = (heads(q), heads(k), heads(v))
            attn = jax.nn.softmax(jnp.einsum('bhqd,bhkd->bhqk', q, k) * SCALE, axis=-1)
            o = jnp.einsum('bhqk,bhkd->bhqd', attn, v).transpose(0, 2, 1, 3).reshape(h.shape)
            h = o @ aow + aob
            hf = _lstm_dir(h, wif, whf, bf)
            hb = _lstm_dir(h[:, ::-1], wibk, whbk, bbk)[:, ::-1]
            mem = jnp.concatenate([hf, hb], axis=-1)
            gate_s = jax.nn.sigmoid(jax.nn.relu(mem @ sw1 + sb1) @ sw2 + sb2)
            gate_t = jnp.tanh(jax.nn.relu(mem @ tw1 + tb1) @ tw2 + tb2)
            g = gate_s * gate_t
            return _ln(jax.nn.relu(g @ dw1 + db1) @ dw2 + db2, dg, dbeta)

        def _forward(x, router_w, router_b, *p):
            outs = jax.vmap(lambda pe: _expert(x, pe))(tuple(p))
            w = jax.nn.softmax(x @ router_w + router_b, axis=-1)
            return jnp.einsum('ebsd,bse->bsd', outs, w)
        return _forward(x, router_w, router_b, enc_w1, enc_b1, enc_w2, enc_b2, enc_g, enc_beta, attn_in_w, attn_in_b, attn_out_w, attn_out_b, lstm_wi_f, lstm_wh_f, lstm_b_f, lstm_wi_b, lstm_wh_b, lstm_b_b, sig_w1, sig_b1, sig_w2, sig_b2, tan_w1, tan_b1, tan_w2, tan_b2, dec_w1, dec_b1, dec_w2, dec_b2, dec_g, dec_beta)

    def _L1_attn_ref(x, A_log, B_mat, C_mat, D_vec, dt_w, dt_b, gamma, beta):
        import jax, jax.numpy as jnp
        import numpy as np
        BATCH, SEQ, D_MODEL, D_STATE = (64, 512, 128, 64)
        DT_MIN, DT_MAX = (0.001, 0.1)
        LN_EPS = 1e-05
        dt = jax.nn.sigmoid(jnp.einsum('bsd,od->bso', x, dt_w) + dt_b)
        dt = dt * (DT_MAX - DT_MIN) + DT_MIN
        A = -jnp.exp(A_log)
        dA = jnp.exp(dt * A)
        dBu = dt * jnp.einsum('nd,bsd->bsn', B_mat, x)

        def step(h, inp):
            a_t, bu_t = inp
            h = a_t * h + bu_t
            return (h, h)
        h0 = jnp.zeros((x.shape[0], A_log.shape[0]), dtype=x.dtype)
        _, hs = jax.lax.scan(step, h0, (jnp.swapaxes(dA, 0, 1), jnp.swapaxes(dBu, 0, 1)))
        hs = jnp.swapaxes(hs, 0, 1)
        y = jnp.einsum('dn,bsn->bsd', C_mat, hs) + D_vec * x
        mu = jnp.mean(y, axis=-1, keepdims=True)
        var = jnp.var(y, axis=-1, keepdims=True)
        y = (y - mu) * jax.lax.rsqrt(var + LN_EPS) * gamma + beta
        return y

    def _L1_ffn_ref(x, W1, b1, W2, b2):
        import jax, jax.numpy as jnp
        import numpy as np
        T = 128
        B = 64
        C = 256

        def _triu_apply(x, W, b):
            Wm = jnp.tril(W)
            return jnp.einsum('bct,st->bcs', x, Wm) + b
        h = _triu_apply(x, W1, b1)
        h = jax.nn.gelu(h, approximate=False)
        return _triu_apply(h, W2, b2)
    h = _L0_tok_ref(x, L0_tok_emb_table, L0_tok_proj_w, L0_tok_proj_b)
    h = h + _L0_attn_ref(_layernorm(h, axis=-1), L0_attn_W_q, L0_attn_W_k, L0_attn_W_v, L0_attn_W_o)
    h = h + _L0_ffn_ref(_layernorm(h, axis=-1), L0_ffn_router_w, L0_ffn_router_b, L0_ffn_enc_w1, L0_ffn_enc_b1, L0_ffn_enc_w2, L0_ffn_enc_b2, L0_ffn_enc_g, L0_ffn_enc_beta, L0_ffn_attn_in_w, L0_ffn_attn_in_b, L0_ffn_attn_out_w, L0_ffn_attn_out_b, L0_ffn_lstm_wi_f, L0_ffn_lstm_wh_f, L0_ffn_lstm_b_f, L0_ffn_lstm_wi_b, L0_ffn_lstm_wh_b, L0_ffn_lstm_b_b, L0_ffn_sig_w1, L0_ffn_sig_b1, L0_ffn_sig_w2, L0_ffn_sig_b2, L0_ffn_tan_w1, L0_ffn_tan_b1, L0_ffn_tan_w2, L0_ffn_tan_b2, L0_ffn_dec_w1, L0_ffn_dec_b1, L0_ffn_dec_w2, L0_ffn_dec_b2, L0_ffn_dec_g, L0_ffn_dec_beta)
    h = h + _L1_attn_ref(_layernorm(h, axis=-1), L1_attn_A_log, L1_attn_B_mat, L1_attn_C_mat, L1_attn_D_vec, L1_attn_dt_w, L1_attn_dt_b, L1_attn_gamma, L1_attn_beta)
    h = h + _L1_ffn_ref(_layernorm(h, axis=-1), L1_ffn_W1, L1_ffn_b1, L1_ffn_W2, L1_ffn_b2)
    return h

_drawn_inputs = setup_inputs


def setup_inputs(seed=0):
    import zlib

    import numpy as np

    out = dict(_drawn_inputs(seed))
    spreads = {'L0_tok_proj_b': (0.0, 0.1),
     'L0_ffn_router_b': (0.0, 0.291),
     'L0_ffn_enc_b1': (0.0, 0.8),
     'L0_ffn_enc_b2': (0.0, 0.8),
     'L0_ffn_enc_g': (1.0, 0.6),
     'L0_ffn_enc_beta': (0.0, 0.8),
     'L0_ffn_attn_in_b': (0.0, 0.8),
     'L0_ffn_attn_out_b': (0.0, 0.8),
     'L0_ffn_lstm_b_f': (0.0, 0.8),
     'L0_ffn_lstm_b_b': (0.0, 0.8),
     'L0_ffn_sig_b1': (0.0, 0.8),
     'L0_ffn_sig_b2': (0.0, 0.8),
     'L0_ffn_tan_b1': (0.0, 0.8),
     'L0_ffn_tan_b2': (0.0, 0.707),
     'L0_ffn_dec_b1': (0.0, 0.1),
     'L0_ffn_dec_b2': (0.0, 0.1),
     'L0_ffn_dec_g': (1.0, 0.2),
     'L0_ffn_dec_beta': (0.0, 0.1),
     'L1_attn_gamma': (1.0, 0.2),
     'L1_attn_beta': (0.0, 0.1)}
    factors = {'L0_tok_emb_table': 2.832,
     'L0_attn_W_q': 8.0,
     'L0_attn_W_k': 8.0,
     'L0_attn_W_v': 2.85,
     'L0_attn_W_o': 4.052,
     'L0_ffn_enc_w1': 8.0,
     'L0_ffn_enc_w2': 8.0,
     'L0_ffn_attn_in_w': 8.0,
     'L0_ffn_attn_out_w': 8.0,
     'L0_ffn_lstm_wi_f': 8.0,
     'L0_ffn_lstm_wh_f': 8.0,
     'L0_ffn_lstm_wi_b': 8.0,
     'L0_ffn_lstm_wh_b': 8.0,
     'L0_ffn_sig_w1': 8.0,
     'L0_ffn_sig_w2': 8.0,
     'L0_ffn_tan_w1': 8.0,
     'L0_ffn_tan_w2': 8.0}
    for name, (base, spread) in spreads.items():
        noise = np.random.default_rng([zlib.crc32(name.encode()), seed]).standard_normal(out[name].shape)
        drawn = base * np.exp(spread * noise) if base else spread * noise
        out[name] = jnp.asarray(drawn.astype(out[name].dtype))
    for name, factor in factors.items():
        out[name] = (out[name] * factor).astype(out[name].dtype)
    return out
```

```python
import concourse.bass as bass
from concourse import mybir
from contextlib import ExitStack
import numpy as np

F32 = mybir.dt.float32
I32 = mybir.dt.int32
ALU = mybir.AluOpType
ACT = mybir.ActivationFunctionType
AX = mybir.AxisListType

P = 128
B, S, D = 4, 512, 128
TOK = B * S
TILES = TOK // P
BT = S // P
EPS = 1e-5

VOCAB, D_EMB = 16, 89
D_STFT = D - D_EMB
N_FFT = 64
N_FREQ = N_FFT // 2 + 1
N_FRAMES = S // N_FFT + 1
BF = B * N_FRAMES

AH, ADK = 8, 64
E, DM, NH, DH = 4, 256, 16, 16
KH = DM // P
G4 = 4 * DM
NST = 64

PRE = {}
_at = 0
for _n, _w in (("ew1", DM), ("ew2", KH * DM), ("qkv", KH * 3 * DM), ("aow", 4 * DM), ("wi", 2 * KH * G4)):
    PRE[_n] = _at
    _at += _w
PRE_W = _at
POST = {}
_at = 0
for _n, _w in (("sw1", 2 * KH * DM), ("sw2", KH * DM), ("tw1", 2 * KH * DM), ("tw2", KH * DM),
               ("dw1", KH * DM), ("dw2", KH * D)):
    POST[_n] = _at
    _at += _w
POST_W = _at
COLS = {n: KH * i for i, n in enumerate(("eb1", "eg", "ebeta", "qb", "kb", "aob", "sb1", "tb1", "sb2", "tb2", "db1"))}
COLS_W = KH * len(COLS)
ROWS = {}
_at = 0
for _n, _w in (("eb2", DM), ("vb", DM), ("lb", 2 * G4), ("db2", D), ("dg", D), ("dbeta", D)):
    ROWS[_n] = _at
    _at += _w
ROWS_W = _at


def clear_signals(nc, signals):
    with nc.Block() as block:
        @block.vector
        def _(dve):
            for s in signals:
                dve.sem_clear(s)


class Core:

    def __init__(self, nc, ctx):
        self.nc, self.ctx = nc, ctx
        self.bank = [ctx.enter_context(nc.psum_tensor(f"bank{i}", [P, 512], F32)) for i in range(8)]
        self.h = self.sb(ctx, "h", [P, TILES, D])
        self.xn = self.sb(ctx, "xn", [P, TILES, D])
        self.xT = self.sb(ctx, "xT", [P, TOK])
        self.ident = self.sb(ctx, "ident", [P, P])
        self.route = self.sb(ctx, "route", [P, TILES, E])

    def sb(self, ctx, name, shape, dt=F32):
        return ctx.enter_context(self.nc.sbuf_tensor(name, shape, dt))

    def sems(self, tag, names):
        made = [self.stage.enter_context(self.nc.semaphore(f"{tag}_{n}")) for n in names.split()]
        self.made += made
        return made

    def run(self, stage, d):
        self.made = []
        with ExitStack() as self.stage:
            stage(self, d)
            clear_signals(self.nc, self.made)


def embed(core, d):
    nc = core.nc
    half = BF // 2 * VOCAB
    with ExitStack() as ctx:
        ids_fr = core.sb(ctx, "ids_fr", [N_FFT, BF], I32)
        ids_tok = core.sb(ctx, "ids_tok", [VOCAB, TOK], I32)
        idf_fr = core.sb(ctx, "idf_fr", [N_FFT, BF])
        idf_tok = core.sb(ctx, "idf_tok", [VOCAB, TOK])
        vocab_row = core.sb(ctx, "vocab_row", [N_FFT, VOCAB])
        vocab_col = core.sb(ctx, "vocab_col", [VOCAB, 1])
        dft = core.sb(ctx, "dft", [N_FFT, 2, N_FREQ])
        hot_fr = core.sb(ctx, "hot_fr", [N_FFT, BF, VOCAB])
        hot_tok = core.sb(ctx, "hot_tok", [VOCAB, TOK])
        sq = core.sb(ctx, "sq", [N_FREQ, 2, BF * VOCAB])
        power = core.sb(ctx, "power", [N_FREQ, BF * VOCAB])
        mag = core.sb(ctx, "mag", [N_FREQ, BF, VOCAB])
        proj = core.sb(ctx, "proj", [N_FREQ, VOCAB, D_STFT])
        table = core.sb(ctx, "table", [VOCAB, D])
        enc = core.sb(ctx, "enc", [BF, D])
        bias = core.sb(ctx, "bias", [1, D])
        up = core.sb(ctx, "up", [BF, TOK])
        ones = core.sb(ctx, "ones", [1, P])
        loaded, zeroed, placed, cast, hot, dft_done, squared, summed, mag_ready, enc_done, enc_ready, h_done, h_kept = \
            core.sems("em", "loaded zeroed placed cast hot dft squared summed mag enc encr h kept")
        with nc.Block() as block:
            @block.sync
            def _(sp):
                for dst, src in ((ids_fr, d["ids_frames"]), (vocab_row, d["vocab_row"]), (dft, d["dft"]),
                                 (vocab_col, d["vocab_col"]), (proj, d["proj_w"]), (up, d["upsample"]),
                                 (core.ident, d["ident"])):
                    sp.dma_start(dst[:], src).then_inc(loaded, 16)
                sp.dma_start(ids_tok[:], d["ids"].partition_broadcast(VOCAB)).then_inc(loaded, 16)
                sp.wait_ge(zeroed, 3)
                sp.dma_start(table[:, 0:D_EMB], d["emb_table"]).then_inc(placed, 16)
                sp.dma_start(bias[:, D_EMB:D], d["proj_b"].unsqueeze(0)).then_inc(placed, 16)

            @block.vector
            def _(dve):
                nc.vector.memset(table[:], 0.0).then_inc(zeroed, 1)
                nc.vector.memset(bias[:], 0.0).then_inc(zeroed, 1)
                nc.vector.memset(enc[:], 0.0).then_inc(zeroed, 1)
                nc.vector.memset(ones[:], 1.0).then_inc(zeroed, 1)
                dve.wait_ge(loaded, 8 * 16)
                nc.vector.tensor_copy(idf_fr[:], ids_fr[:]).then_inc(cast, 1)
                nc.vector.tensor_copy(idf_tok[:], ids_tok[:]).then_inc(cast, 1)
                dve.wait_ge(cast, 2)
                nc.vector.tensor_tensor(hot_fr[:], idf_fr[:].unsqueeze(2).broadcast_to([N_FFT, BF, VOCAB]),
                                        vocab_row[:].unsqueeze(1).broadcast_to([N_FFT, BF, VOCAB]),
                                        ALU.is_equal).then_inc(hot, 1)
                nc.vector.tensor_scalar(hot_tok[:], idf_tok[:], vocab_col[:, 0:1], None,
                                        ALU.is_equal).then_inc(hot, 1)
                dve.wait_ge(squared, 4)
                nc.vector.tensor_tensor(power[:], sq[:, 0], sq[:, 1], ALU.add).then_inc(summed, 1)
                dve.wait_ge(enc_done, 1)
                nc.vector.tensor_copy(enc[:, D_EMB:D], core.bank[4][0:BF, 0:D_STFT]).then_inc(enc_ready, 1)
                for g in range(4):
                    dve.wait_ge(h_done, g + 1)
                    nc.vector.tensor_copy(core.h[:, 4 * g:4 * g + 4],
                                          core.bank[g][:].rearrange("p (t d) -> p t d", d=D)).then_inc(h_kept, 1)

            @block.tensor
            def _(pe):
                pe.wait_ge(hot, 2)
                frames = hot_fr[:].rearrange("p f v -> p (f v)")
                for part in range(2):
                    for n in range(2):
                        nc.tensor.matmul(core.bank[2 * part + n][0:N_FREQ, 0:half], dft[:, part],
                                         frames[:, n * half:(n + 1) * half], start=True,
                                         stop=True).then_inc(dft_done, 1)
                pe.wait_ge(mag_ready, 1)
                for v in range(VOCAB):
                    last = nc.tensor.matmul(core.bank[4][0:BF, 0:D_STFT], mag[:, :, v], proj[:, v],
                                            start=v == 0, stop=v == VOCAB - 1)
                last.then_inc(enc_done, 1)
                pe.wait_ge(enc_ready, 1)
                pe.wait_ge(placed, 32)
                pe.wait_ge(zeroed, 4)
                for t in range(TILES):
                    out = core.bank[t // 4][:, (t % 4) * D:(t % 4 + 1) * D]
                    tok = slice(t * P, (t + 1) * P)
                    nc.tensor.matmul(out, hot_tok[:, tok], table[:], start=True, stop=False)
                    nc.tensor.matmul(out, up[:, tok], enc[:], start=False, stop=False)
                    last = nc.tensor.matmul(out, ones[:], bias[:], start=False, stop=True)
                    if t % 4 == 3:
                        last.then_inc(h_done, 1)

            @block.scalar
            def _(act):
                for part in range(2):
                    for n in range(2):
                        act.wait_ge(dft_done, 2 * part + n + 1)
                        nc.scalar.activation(sq[:, part, n * half:(n + 1) * half],
                                             core.bank[2 * part + n][0:N_FREQ, 0:half],
                                             ACT.Square).then_inc(squared, 1)
                act.wait_ge(summed, 1)
                nc.scalar.activation(mag[:].rearrange("p f v -> p (f v)"), power[:], ACT.Sqrt).then_inc(mag_ready, 1)


def layer_norm(core, tag):
    nc = core.nc
    with ExitStack() as ctx:
        stats = core.sb(ctx, f"{tag}_stats", [P, TILES, 6])
        mv = core.sb(ctx, f"{tag}_mv", [P, TILES, 2])
        var = core.sb(ctx, f"{tag}_var", [P, TILES])
        std = core.sb(ctx, f"{tag}_std", [P, TILES])
        rstd = core.sb(ctx, f"{tag}_rstd", [P, TILES])
        stats_done, mv_done, var_done, std_done, rstd_done, normed, turned, kept = \
            core.sems(tag, "stats mv var std rstd normed turned kept")
        with nc.Block() as block:
            @block.vector
            def _(dve):
                for t in range(TILES):
                    nc.vector.bn_stats(stats[:, t], core.h[:, t]).then_inc(stats_done, 1)
                for t in range(TILES):
                    dve.wait_ge(stats_done, t + 1)
                    nc.vector.bn_aggr(mv[:, t], stats[:, t]).then_inc(mv_done, 1)
                dve.wait_ge(mv_done, TILES)
                nc.vector.tensor_scalar(var[:], mv[:, :, 1], EPS, None, ALU.add).then_inc(var_done, 1)
                dve.wait_ge(std_done, 1)
                nc.vector.reciprocal(rstd[:], std[:]).then_inc(rstd_done, 1)
                dve.wait_ge(rstd_done, 1)
                for t in range(TILES):
                    nc.vector.tensor_scalar(core.xn[:, t], core.h[:, t], mv[:, t, 0:1], rstd[:, t:t + 1],
                                            ALU.subtract, ALU.mult).then_inc(normed, 1)

            @block.scalar
            def _(act):
                act.wait_ge(var_done, 1)
                nc.scalar.activation(std[:], var[:], ACT.Sqrt).then_inc(std_done, 1)
                for g in range(4):
                    act.wait_ge(turned, g + 1)
                    nc.scalar.activation(core.xT[:, g * 512:(g + 1) * 512], core.bank[g][:], ACT.Copy).then_inc(kept, 1)

            @block.tensor
            def _(pe):
                for t in range(TILES):
                    pe.wait_ge(normed, t + 1)
                    last = nc.tensor.transpose(core.bank[t // 4][:, (t % 4) * P:(t % 4 + 1) * P], core.xn[:, t],
                                               core.ident[:])
                    if t % 4 == 3:
                        last.then_inc(turned, 1)


class Attention:

    def __init__(self, core, ctx, tag, heads, causal, per_bank, rows):
        self.core, self.heads, self.causal, self.per_bank, self.rows = core, heads, causal, per_bank, rows
        self.p = core.sb(ctx, f"{tag}_p", [P, 2, BT, S])
        self.pT = core.sb(ctx, f"{tag}_pT", [P, 2, BT, S])
        self.negmax = core.sb(ctx, f"{tag}_negmax", [P, heads, BT])
        self.total = core.sb(ctx, f"{tag}_total", [P, heads, BT])
        self.inv = core.sb(ctx, f"{tag}_inv", [P, heads, BT])
        self.oT = core.sb(ctx, f"{tag}_oT", [P, heads // per_bank, S])
        (self.scored, self.maxed, self.exped, self.inverted, self.normed, self.turned, self.kept_v, self.kept_a,
         self.valued, self.out_kept) = core.sems(
            tag, "scored maxed exped inverted normed turned keptv kepta valued outkept")
        self.signals = [self.scored, self.maxed, self.exped, self.inverted, self.normed, self.turned, self.kept_v,
                        self.kept_a, self.valued, self.out_kept]

    def width(self, qt):
        return (qt + 1) * P if self.causal else S

    def low(self, kt):
        return kt * P if self.causal else 0

    def tensor(self, pe, query, key, value, key_wait, mask):
        nc, bank = self.core.nc, self.core.bank

        def score(h, qt):
            if qt == 0:
                key_wait(pe, h)
            if h > 0:
                pe.wait_ge(self.exped, BT * (h - 1) + qt + 1)
            w = self.width(qt)
            last = nc.tensor.matmul(bank[qt][:, 0:w], query(h, qt), key(h)[:, 0:w], start=True, stop=not self.causal)
            if self.causal:
                last = nc.tensor.matmul(bank[qt][:, qt * P:w], self.core.ident[:], mask, start=False, stop=True)
            last.then_inc(self.scored, 1)

        def turn(h, kt):
            n = BT * h + kt
            if kt == 0:
                pe.wait_ge(self.normed, BT * (h + 1))
            if n >= 2:
                pe.wait_ge(*((self.kept_a, (n - 2) // 2 + 1) if kt % 2 else (self.kept_v, (n - 2) // 2 + 1)))
            for qt in range(kt if self.causal else 0, BT):
                last = nc.tensor.transpose(bank[4 + kt % 2][:, qt * P:(qt + 1) * P],
                                           self.p[:, h % 2, qt, kt * P:(kt + 1) * P], self.core.ident[:])
            last.then_inc(self.turned, 1)

        def values(h, kt):
            n = BT * h + kt
            pe.wait_ge(*((self.kept_a, n // 2 + 1) if kt % 2 else (self.kept_v, n // 2 + 1)))
            g, c = divmod(h, self.per_bank)
            if c == 0 and kt == 0 and g >= 2:
                pe.wait_ge(self.out_kept, g - 1)
            r = c * (P // self.per_bank)
            lo = self.low(kt)
            nc.tensor.matmul(bank[6 + g % 2][r:r + self.rows, lo:S], value(h, kt), self.pT[:, h % 2, kt, lo:S],
                             start=kt == 0, stop=kt == BT - 1).then_inc(self.valued, 1)

        for h in range(self.heads + 1):
            for qt in (0, 1):
                if h < self.heads:
                    score(h, qt)
            if h > 0:
                turn(h - 1, 0)
                turn(h - 1, 1)
            if h < self.heads:
                score(h, 2)
            if h > 0:
                values(h - 1, 0)
                turn(h - 1, 2)
                values(h - 1, 1)
            if h < self.heads:
                score(h, 3)
            if h > 0:
                turn(h - 1, 3)
                values(h - 1, 2)
                values(h - 1, 3)

    def vector(self, dve):
        nc, bank = self.core.nc, self.core.bank

        def largest(h, qt):
            dve.wait_ge(self.scored, BT * h + qt + 1)
            nc.vector.tensor_reduce(self.negmax[:, h, qt:qt + 1], bank[qt][:, 0:self.width(qt)], AX.X, ALU.max,
                                    negate=True).then_inc(self.maxed, 1)

        def normalise(h):
            dve.wait_ge(self.exped, BT * (h + 1))
            nc.vector.reciprocal(self.inv[:, h], self.total[:, h]).then_inc(self.inverted, 1)
            dve.wait_ge(self.inverted, h + 1)
            for qt in range(BT):
                p = self.p[:, h % 2, qt, 0:self.width(qt)]
                nc.vector.tensor_scalar(p, p, self.inv[:, h, qt:qt + 1], None, ALU.mult).then_inc(self.normed, 1)

        def keep(h, kt):
            dve.wait_ge(self.turned, BT * h + kt + 1)
            if h >= 2:
                dve.wait_ge(self.valued, BT * (h - 2) + kt + 1)
            lo = self.low(kt)
            nc.vector.tensor_copy(self.pT[:, h % 2, kt, lo:S], bank[4 + kt % 2][:, lo:S]).then_inc(self.kept_v, 1)

        for h in range(self.heads + 1):
            if h < self.heads:
                largest(h, 0)
            if h > 0:
                normalise(h - 1)
            if h < self.heads:
                largest(h, 1)
            if h > 0:
                keep(h - 1, 0)
            if h < self.heads:
                largest(h, 2)
            if h > 0:
                keep(h - 1, 2)
            if h < self.heads:
                largest(h, 3)
            if h > 0 and h % self.per_bank == 0:
                g = h // self.per_bank - 1
                dve.wait_ge(self.valued, BT * h)
                nc.vector.tensor_copy(self.oT[:, g], bank[6 + g % 2][:]).then_inc(self.out_kept, 1)

    def scalar(self, act):
        nc, bank = self.core.nc, self.core.bank

        def exponent(h, qt):
            act.wait_ge(self.maxed, BT * h + qt + 1)
            if h >= 2 and qt == 0:
                act.wait_ge(self.turned, BT * (h - 1))
            w = self.width(qt)
            nc.scalar.activation(self.p[:, h % 2, qt, 0:w], bank[qt][:, 0:w], ACT.Exp,
                                 bias=self.negmax[:, h, qt:qt + 1],
                                 accum_out=self.total[:, h, qt:qt + 1]).then_inc(self.exped, 1)

        def keep(h, kt):
            act.wait_ge(self.turned, BT * h + kt + 1)
            if h >= 2:
                act.wait_ge(self.valued, BT * (h - 2) + kt + 1)
            lo = self.low(kt)
            nc.scalar.activation(self.pT[:, h % 2, kt, lo:S], bank[4 + kt % 2][:, lo:S],
                                 ACT.Copy).then_inc(self.kept_a, 1)

        for h in range(self.heads + 1):
            if h < self.heads:
                exponent(h, 0)
                exponent(h, 1)
            if h > 0:
                keep(h - 1, 1)
            if h < self.heads:
                exponent(h, 2)
            if h > 0:
                keep(h - 1, 3)
            if h < self.heads:
                exponent(h, 3)


def causal_attention(core, d):
    nc = core.nc
    with ExitStack() as ctx:
        w = core.sb(ctx, "aw", [P, 4, AH * ADK])
        mask = core.sb(ctx, "amask", [P, P])
        xb = core.sb(ctx, "axb", [P, S])
        qT = core.sb(ctx, "aqT", [P, 4, S])
        kz = core.sb(ctx, "akz", [P, AH, S])
        v = core.sb(ctx, "av", [P, BT, AH * ADK])
        att = Attention(core, ctx, "at", AH, True, 2, ADK)
        loaded, x_ready, q_mm, k_mm, v_mm, q_kept, k_kept, v_kept, o_mm, o_kept = \
            core.sems("at", "loaded x qmm kmm vmm qkept kkept vkept omm okept")
        with nc.Block() as block:
            @block.sync
            def _(sp):
                sp.dma_start(w[:], d["attn_w"]).then_inc(loaded, 16)
                sp.dma_start(mask[:], d["causal"]).then_inc(loaded, 16)
                sp.wait_ge(loaded, 32)

            @block.vector
            def _(dve):
                nc.vector.memset(kz[:], 0.0)
        with nc.Fori(0, B) as b:
            with nc.Block() as block:
                @block.tensor
                def _(pe):
                    pe.wait_ge(x_ready, 1)
                    for n in range(4):
                        nc.tensor.matmul(core.bank[n][:], w[:, 0, n * P:(n + 1) * P], xb[:], start=True,
                                         stop=True).then_inc(q_mm, 1)
                    for n in range(4):
                        nc.tensor.matmul(core.bank[4 + n][:], w[:, 1, n * P:(n + 1) * P], xb[:], start=True,
                                         stop=True).then_inc(k_mm, 1)
                    for t in range(BT):
                        pe.wait_ge(q_kept, t + 1)
                        nc.tensor.matmul(core.bank[t][:], xb[:, t * P:(t + 1) * P], w[:, 2], start=True,
                                         stop=True).then_inc(v_mm, 1)

                    def key_wait(pe, h):
                        if h == 0:
                            pe.wait_ge(v_kept, BT)
                            pe.wait_ge(k_kept, 8)

                    att.tensor(pe, lambda h, qt: qT[:, h // 2, qt * P:(qt + 1) * P], lambda h: kz[:, h],
                               lambda h, kt: v[:, kt, h * ADK:(h + 1) * ADK], key_wait, mask[:])
                    pe.wait_ge(att.out_kept, 4)
                    for t in range(BT):
                        for n in range(4):
                            last = nc.tensor.matmul(core.bank[0][:, t * D:(t + 1) * D],
                                                    att.oT[:, n, t * P:(t + 1) * P], w[:, 3, n * D:(n + 1) * D],
                                                    start=n == 0, stop=n == 3)
                    last.then_inc(o_mm, 1)

                @block.vector
                def _(dve):
                    nc.vector.tensor_copy(xb[:], core.xT[:, bass.ds(b * S, S)]).then_inc(x_ready, 1)
                    for n in range(4):
                        dve.wait_ge(k_mm, n + 1)
                        for half in (0, 1):
                            r = slice(half * ADK, (half + 1) * ADK)
                            nc.vector.tensor_copy(kz[r, 2 * n + half], core.bank[4 + n][r, :]).then_inc(k_kept, 1)
                    att.vector(dve)
                    dve.wait_ge(o_mm, 1)
                    hb = core.h[:, bass.ds(b * BT, BT)]
                    nc.vector.tensor_tensor(hb, core.bank[0][:].rearrange("p (t d) -> p t d", d=D), hb,
                                            ALU.add).then_inc(o_kept, 1)

                @block.scalar
                def _(act):
                    for n in range(4):
                        act.wait_ge(q_mm, n + 1)
                        nc.scalar.activation(qT[:, n], core.bank[n][:], ACT.Copy,
                                             scale=float(ADK) ** -0.5).then_inc(q_kept, 1)
                    for t in range(BT):
                        act.wait_ge(v_mm, t + 1)
                        nc.scalar.activation(v[:, t], core.bank[t][:], ACT.Copy).then_inc(v_kept, 1)
                    att.scalar(act)
            clear_signals(nc, att.signals + [x_ready, q_mm, k_mm, v_mm, q_kept, k_kept, v_kept, o_mm, o_kept])


def router(core, d):
    nc = core.nc
    with ExitStack() as ctx:
        rw = core.sb(ctx, "rw", [P, E])
        rb = core.sb(ctx, "rb", [P, E])
        logit = core.sb(ctx, "logit", [P, TILES, E])
        shifted = core.sb(ctx, "shifted", [P, TILES, E])
        ex = core.sb(ctx, "rex", [P, TILES, E])
        top = core.sb(ctx, "rtop", [P, TILES])
        total = core.sb(ctx, "rtotal", [P, TILES])
        inv = core.sb(ctx, "rinv", [P, TILES])
        loaded, logits_mm, step, shifted_ready, ex_ready = core.sems("ro", "loaded mm step shifted ex")
        with nc.Block() as block:
            @block.sync
            def _(sp):
                sp.dma_start(rw[:], d["router_w"]).then_inc(loaded, 16)
                sp.dma_start(rb[:], d["router_b"].partition_broadcast(P)).then_inc(loaded, 16)

            @block.tensor
            def _(pe):
                pe.wait_ge(loaded, 32)
                for t in range(TILES):
                    last = nc.tensor.matmul(core.bank[0][:, t * E:(t + 1) * E], core.xT[:, t * P:(t + 1) * P], rw[:],
                                            start=True, stop=True)
                last.then_inc(logits_mm, 1)

            @block.vector
            def _(dve):
                def wide(a):
                    return a.unsqueeze(2).broadcast_to([P, TILES, E])

                dve.wait_ge(logits_mm, 1)
                dve.wait_ge(loaded, 32)
                nc.vector.tensor_tensor(logit[:], core.bank[0][:, 0:TILES * E].rearrange("p (t e) -> p t e", e=E),
                                        rb[:].unsqueeze(1).broadcast_to([P, TILES, E]), ALU.add).then_inc(step, 1)
                dve.wait_ge(step, 1)
                nc.vector.tensor_reduce(top[:], logit[:], AX.X, ALU.max).then_inc(step, 1)
                dve.wait_ge(step, 2)
                nc.vector.tensor_tensor(shifted[:], logit[:], wide(top[:]), ALU.subtract).then_inc(shifted_ready, 1)
                dve.wait_ge(ex_ready, 1)
                nc.vector.tensor_reduce(total[:], ex[:], AX.X, ALU.add).then_inc(step, 1)
                dve.wait_ge(step, 3)
                nc.vector.reciprocal(inv[:], total[:]).then_inc(step, 1)
                dve.wait_ge(step, 4)
                nc.vector.tensor_tensor(core.route[:], ex[:], wide(inv[:]), ALU.mult)

            @block.scalar
            def _(act):
                act.wait_ge(shifted_ready, 1)
                nc.scalar.activation(ex[:], shifted[:], ACT.Exp).then_inc(ex_ready, 1)


def experts_before(core, d):
    nc, bank = core.nc, core.bank
    with ExitStack() as ctx:
        w = core.sb(ctx, "bw", [P, PRE_W])
        cols = core.sb(ctx, "bcols", [P, COLS_W])
        rows = core.sb(ctx, "brows", [P, ROWS_W])
        head_mask = core.sb(ctx, "bmask", [P, 8])
        xb = core.sb(ctx, "bxb", [P, S])
        h1 = core.sb(ctx, "bh1", [P, KH, S])
        h2 = core.sb(ctx, "bh2", [P, BT, DM])
        hn = core.sb(ctx, "bhn", [P, BT, DM])
        hT = core.sb(ctx, "bhT", [P, KH, S])
        qT = core.sb(ctx, "bqT", [P, KH, S])
        kT = core.sb(ctx, "bkT", [P, KH, S])
        km = core.sb(ctx, "bkm", [P, 2, S])
        v = core.sb(ctx, "bv", [P, BT, DM])
        aT = core.sb(ctx, "baT", [P, KH, S])
        zs = core.sb(ctx, "bzs", [P, 4, G4])
        stats = core.sb(ctx, "bstats", [P, BT, 6])
        mv = core.sb(ctx, "bmv", [P, BT, 2])
        var = core.sb(ctx, "bvar", [P, BT])
        std = core.sb(ctx, "bstd", [P, BT])
        rstd = core.sb(ctx, "brstd", [P, BT])
        att = Attention(core, ctx, "bt", NH, False, 4, DH)
        (loaded, x_ready, h1_mm, h1_kept, h2_mm, h2_kept, stats_done, mv_done, var_done, std_done, rstd_done, normed,
         hn_turned, hT_kept, qk_mm, v_mm, q_kept, k_kept, v_kept, masked, a_mm, a_kept, z_mm, z_kept) = \
            core.sems("be", "loaded x h1mm h1kept h2mm h2kept stats mv var std rstd normed hnturned hTkept qkmm vmm "
                            "qkept kkept vkept masked amm akept zmm zkept")
        z_stored = core.sems("be", "zstored0 zstored1 zstored2 zstored3")

        qbs = core.sb(ctx, "bqbs", [P, KH])
        (mask_loaded,) = core.sems("be", "mask")

        def weight(name, part, lo, n):
            width = {"ew1": DM, "ew2": DM, "qkv": 3 * DM, "aow": DM}[name]
            at = PRE[name] + part * width + lo
            return w[:, at:at + n]

        def col(name, part):
            return cols[:, COLS[name] + part:COLS[name] + part + 1]

        with nc.Block() as block:
            @block.sync
            def _(sp):
                sp.dma_start(head_mask[:], d["head_mask"]).then_inc(mask_loaded, 16)
                sp.wait_ge(mask_loaded, 16)
        with nc.Fori(0, E) as e:
            with nc.Block() as block:
                @block.sync
                def _(sp):
                    sp.dma_start(w[:], d["w_before"][e]).then_inc(loaded, 16)
                    sp.dma_start(cols[:], d["cols"][e]).then_inc(loaded, 16)
                    sp.dma_start(rows[:], d["rows"][e].partition_broadcast(P)).then_inc(loaded, 16)
                    sp.wait_ge(loaded, 48)

                @block.vector
                def _(dve):
                    dve.wait_ge(loaded, 48)
                    nc.vector.tensor_scalar(qbs[:], cols[:, COLS["qb"]:COLS["qb"] + KH], float(DH) ** -0.5, None,
                                            ALU.mult)
            with nc.Fori(0, B) as b:
                with nc.Block() as block:
                    @block.tensor
                    def _(pe):
                        pe.wait_ge(x_ready, 1)
                        for m in range(KH):
                            nc.tensor.matmul(bank[m][:], weight("ew1", 0, m * P, P), xb[:], start=True,
                                             stop=True).then_inc(h1_mm, 1)
                        pe.wait_ge(h1_kept, 2)
                        for t in range(BT):
                            for k in range(KH):
                                last = nc.tensor.matmul(bank[2 + t][:, 0:DM], h1[:, k, t * P:(t + 1) * P],
                                                        weight("ew2", k, 0, DM), start=k == 0, stop=k == KH - 1)
                            last.then_inc(h2_mm, 1)
                        for t in range(BT):
                            pe.wait_ge(normed, t + 1)
                            for k in range(KH):
                                last = nc.tensor.transpose(bank[6 + k][:, t * P:(t + 1) * P],
                                                           hn[:, t, k * P:(k + 1) * P], core.ident[:])
                        last.then_inc(hn_turned, 1)
                        pe.wait_ge(hT_kept, 2)
                        for m in range(4):
                            for k in range(KH):
                                last = nc.tensor.matmul(bank[m][:], weight("qkv", k, m * P, P), hT[:, k],
                                                        start=k == 0, stop=k == KH - 1)
                            last.then_inc(qk_mm, 1)
                        for t in range(BT):
                            for k in range(KH):
                                last = nc.tensor.matmul(bank[4 + t][:, 0:DM],
                                                        hT[:, k, t * P:(t + 1) * P], weight("qkv", k, 2 * DM, DM),
                                                        start=k == 0, stop=k == KH - 1)
                            last.then_inc(v_mm, 1)

                        def key_wait(pe, h):
                            if h == 0:
                                pe.wait_ge(q_kept, KH)
                                pe.wait_ge(v_kept, BT)
                            pe.wait_ge(masked, h + 1)

                        att.tensor(pe, lambda h, qt: qT[:, h // 8, qt * P:(qt + 1) * P], lambda h: km[:, h % 2],
                                   lambda h, kt: v[:, kt, h * DH:(h + 1) * DH], key_wait, None)
                        pe.wait_ge(att.out_kept, 4)
                        for m in range(KH):
                            for g in range(4):
                                last = nc.tensor.matmul(bank[4 + m][:], weight("aow", g, m * P, P), att.oT[:, g],
                                                        start=g == 0, stop=g == 3)
                            last.then_inc(a_mm, 1)
                        pe.wait_ge(a_kept, KH)
                        for t in range(BT):
                            for q in range(4):
                                n = 4 * t + q
                                if n >= 4:
                                    pe.wait_ge(z_kept, n - 3)
                                for k in range(KH):
                                    at = PRE["wi"] + (q // 2 * KH + k) * G4 + q % 2 * 512
                                    last = nc.tensor.matmul(bank[n % 4][:], aT[:, k, t * P:(t + 1) * P],
                                                            w[:, at:at + 512], start=k == 0, stop=k == KH - 1)
                                last.then_inc(z_mm, 1)

                    @block.vector
                    def _(dve):
                        nc.vector.tensor_copy(xb[:], core.xT[:, bass.ds(b * S, S)]).then_inc(x_ready, 1)
                        for t in range(BT):
                            dve.wait_ge(h2_mm, t + 1)
                            nc.vector.tensor_tensor(h2[:, t], bank[2 + t][:, 0:DM],
                                                    rows[:, ROWS["eb2"]:ROWS["eb2"] + DM], ALU.add).then_inc(h2_kept, 1)
                            dve.wait_ge(h2_kept, t + 1)
                            nc.vector.bn_stats(stats[:, t], h2[:, t]).then_inc(stats_done, 1)
                            dve.wait_ge(stats_done, t + 1)
                            nc.vector.bn_aggr(mv[:, t], stats[:, t]).then_inc(mv_done, 1)
                        dve.wait_ge(mv_done, BT)
                        nc.vector.tensor_scalar(var[:], mv[:, :, 1], EPS, None, ALU.add).then_inc(var_done, 1)
                        dve.wait_ge(std_done, 1)
                        nc.vector.reciprocal(rstd[:], std[:]).then_inc(rstd_done, 1)
                        dve.wait_ge(rstd_done, 1)
                        for t in range(BT):
                            nc.vector.tensor_scalar(hn[:, t], h2[:, t], mv[:, t, 0:1], rstd[:, t:t + 1],
                                                    ALU.subtract, ALU.mult).then_inc(normed, 1)
                        for m in range(KH):
                            dve.wait_ge(qk_mm, KH + m + 1)
                            nc.vector.tensor_scalar(kT[:, m], bank[KH + m][:], col("kb", m), None,
                                                    ALU.add).then_inc(k_kept, 1)
                        for t in range(BT):
                            dve.wait_ge(v_mm, t + 1)
                            nc.vector.tensor_tensor(v[:, t], bank[4 + t][:, 0:DM],
                                                    rows[:, ROWS["vb"]:ROWS["vb"] + DM], ALU.add).then_inc(v_kept, 1)
                        att.vector(dve)
                        for n in range(4 * BT):
                            t, q = divmod(n, 4)
                            dve.wait_ge(z_mm, n + 1)
                            if n >= 8 and q % 2 == 0:
                                dve.wait_ge(z_stored[n // 2 % 4], 16 * (n // 8))
                            lb = ROWS["lb"] + q * 512
                            nc.vector.tensor_tensor(zs[:, (n // 2) % 4, q % 2 * 512:(q % 2 + 1) * 512], bank[n % 4][:],
                                                    rows[:, lb:lb + 512], ALU.add).then_inc(z_kept, 1)

                    @block.gpsimd
                    def _(pool):
                        pool.wait_ge(k_kept, KH)
                        for h in range(NH):
                            if h >= 2:
                                pool.wait_ge(att.scored, BT * (h - 1))
                            nc.gpsimd.tensor_scalar(km[:, h % 2], kT[:, h // 8], head_mask[:, h % 8:h % 8 + 1], None,
                                                    ALU.mult).then_inc(masked, 1)

                    @block.scalar
                    def _(act):
                        for m in range(KH):
                            act.wait_ge(h1_mm, m + 1)
                            nc.scalar.activation(h1[:, m], bank[m][:], ACT.Relu, bias=col("eb1", m)).then_inc(h1_kept, 1)
                        act.wait_ge(var_done, 1)
                        nc.scalar.activation(std[:], var[:], ACT.Sqrt).then_inc(std_done, 1)
                        act.wait_ge(hn_turned, 1)
                        for k in range(KH):
                            nc.scalar.activation(hT[:, k], bank[6 + k][:], ACT.Identity, scale=col("eg", k),
                                                 bias=col("ebeta", k)).then_inc(hT_kept, 1)
                        for m in range(KH):
                            act.wait_ge(qk_mm, m + 1)
                            nc.scalar.activation(qT[:, m], bank[m][:], ACT.Identity, scale=float(DH) ** -0.5,
                                                 bias=qbs[:, m:m + 1]).then_inc(q_kept, 1)
                        att.scalar(act)
                        for m in range(KH):
                            act.wait_ge(a_mm, m + 1)
                            nc.scalar.activation(aT[:, m], bank[4 + m][:], ACT.Identity,
                                                 bias=col("aob", m)).then_inc(a_kept, 1)

                    @block.sync
                    def _(sp):
                        for n in range(2 * BT):
                            t, way = divmod(n, 2)
                            sp.wait_ge(z_kept, 2 * n + 2)
                            sp.dma_start(d["zx"][way, e, b, t * P:(t + 1) * P], zs[:, n % 4]).then_inc(z_stored[n % 4], 16)
                        for slot in z_stored:
                            sp.wait_ge(slot, 16 * 2)
                clear_signals(nc, att.signals + [
                    x_ready, h1_mm, h1_kept, h2_mm, h2_kept, stats_done, mv_done, var_done, std_done, rstd_done, normed,
                    hn_turned, hT_kept, qk_mm, v_mm, q_kept, k_kept, v_kept, masked, a_mm, a_kept, z_mm,
                    z_kept] + z_stored)
            clear_signals(nc, [loaded])


STEPS = 4
PER_TURN = 2 * STEPS


def recurrence(core, d):
    nc, bank = core.nc, core.bank
    turns = S // PER_TURN
    with ExitStack() as ctx:
        wh = core.sb(ctx, "lwh", [P, 2, E, KH, G4])
        zx = core.sb(ctx, "lzx", [P, 2, 2, STEPS, G4])
        hs = core.sb(ctx, "lhs", [P, 2, 2, STEPS, DM])
        z = core.sb(ctx, "lz", [P, 2, KH, 4, P])
        gate = core.sb(ctx, "lgate", [P, 2, KH, 3, P])
        gc = core.sb(ctx, "lgc", [P, 2, KH, 2, P])
        prod = core.sb(ctx, "lprod", [P, 2, KH, 2, P])
        tc = core.sb(ctx, "ltc", [P, 2, KH, P])
        hT = core.sb(ctx, "lhT", [P, 2, KH, E, B])
        (loaded, cleared) = core.sems("ls", "loaded cleared")

        def pair(name):
            return core.sems("ls", f"{name}0 {name}1")

        made, added, gated, celled, tanhed, ready, turned, kept = (
            pair(n) for n in ("made", "added", "gated", "celled", "tanhed", "ready", "turned", "kept"))
        multiplied = pair("multiplied")
        zx_in = [pair("zxin0"), pair("zxin1")]
        hs_out = [pair("hsout0"), pair("hsout1")]

        def z_bank(way, j):
            return bank[2 * way + j]

        def turn_bank(way, j):
            return bank[4 + 2 * way + j]

        def rows_of(e):
            return slice(32 * e, 32 * e + B)

        def first_time(way, turn, buf):
            n = 2 * turn + buf
            return n * STEPS if way == 0 else n * -STEPS + (S - STEPS)

        def at(way, i):
            return i if way == 0 else STEPS - 1 - i

        def load_zx(sp, way, turn, buf):
            for e in range(E):
                sp.dma_start(zx[rows_of(e), way, buf], d["zx"][way, e, :, bass.ds(first_time(way, turn, buf), STEPS)]
                             ).then_inc(zx_in[way][buf], 16)

        with nc.Block() as block:
            @block.sync
            def _(sp):
                sp.dma_start(wh[:], d["wh"]).then_inc(loaded, 16)
                sp.wait_ge(cleared, 1)
                for buf in range(2):
                    for way in range(2):
                        load_zx(sp, way, 0, buf)
                sp.wait_ge(loaded, 16)

            @block.vector
            def _(dve):
                nc.vector.memset(zx[:], 0.0).then_inc(cleared, 1)
                nc.vector.memset(hT[:], 0.0)
                nc.vector.memset(gc[:], 0.0)
                for n in range(4):
                    nc.vector.memset(bank[n][:], 0.0)
                for way in range(2):
                    dve.sem_inc(added[way], 2)
                    dve.sem_inc(kept[way], 2)
                    for buf in range(2):
                        dve.sem_inc(hs_out[way][buf], 1)

        with nc.Block() as block:
            @block.tensor
            def _(pe):
                with pe.Fori(0, turns) as turn:
                    def products(way, i, k):
                        done = 2 * PER_TURN * turn + 2 * i
                        pe.wait_ge(kept[way], done + k + 1)
                        for j in range(KH):
                            if k == 0:
                                pe.wait_ge(added[way], done + j + 1)
                            for e in range(E):
                                last = nc.tensor.matmul(z_bank(way, j)[rows_of(e), :], hT[:, way, k, e],
                                                        wh[:, way, e, k, j * 512:(j + 1) * 512],
                                                        start=k == 0, stop=k == KH - 1)
                            if k == KH - 1:
                                last.then_inc(made[way], 1)

                    def transposes(way, i, j):
                        pe.wait_ge(ready[way], 2 * PER_TURN * turn + 2 * i + j + 1)
                        nc.tensor.transpose(turn_bank(way, j)[:, 0:P],
                                            hs[:, way, i // STEPS, at(way, i % STEPS), j * P:(j + 1) * P],
                                            core.ident[:]).then_inc(turned[way], 1)

                    for i in range(PER_TURN):
                        products(0, i, 0)
                        products(0, i, 1)
                        if i > 0:
                            transposes(1, i - 1, 0)
                            transposes(1, i - 1, 1)
                        products(1, i, 0)
                        products(1, i, 1)
                        transposes(0, i, 0)
                        transposes(0, i, 1)
                    transposes(1, PER_TURN - 1, 0)
                    transposes(1, PER_TURN - 1, 1)

            @block.vector
            def _(dve):
                with dve.Fori(0, turns) as turn:
                    for i in range(PER_TURN):
                        buf, done = i // STEPS, 2 * PER_TURN * turn + 2 * i
                        for way in range(2):
                            here = at(way, i % STEPS)
                            if i % STEPS == 0:
                                dve.wait_ge(zx_in[way][buf], 64 * turn + 64)
                                dve.wait_ge(hs_out[way][buf], 64 * turn + 1)
                            zw, gw = z[:, way], gate[:, way]

                            def add(j):
                                dve.wait_ge(made[way], done + j + 1)
                                nc.vector.tensor_tensor(z[:, way, j].rearrange("p g n -> p (g n)"), z_bank(way, j)[:],
                                                        zx[:, way, buf, here, j * 512:(j + 1) * 512],
                                                        ALU.add).then_inc(added[way], 1)

                            def cell(j):
                                dve.wait_ge(gated[way], done + j + 1)
                                nc.vector.tensor_tensor(prod[:, way, j], gate[:, way, j, 0:2], gc[:, way, j],
                                                        ALU.mult).then_inc(multiplied[way], 1)
                                dve.wait_ge(multiplied[way], done + j + 1)
                                nc.vector.tensor_tensor(gc[:, way, j, 1], prod[:, way, j, 0], prod[:, way, j, 1],
                                                        ALU.add).then_inc(celled[way], 1)

                            def state(j):
                                dve.wait_ge(tanhed[way], done + j + 1)
                                nc.vector.tensor_tensor(hs[:, way, buf, here, j * P:(j + 1) * P], gate[:, way, j, 2],
                                                        tc[:, way, j], ALU.mult).then_inc(ready[way], 1)

                            def keep(j):
                                dve.wait_ge(turned[way], done + j + 1)
                                nc.vector.tensor_copy(
                                    hT[:, way, j],
                                    turn_bank(way, j)[:, 0:P].rearrange("p (e b) -> p e b", e=E)[:, :, 0:B]
                                ).then_inc(kept[way], 1)

                            add(0)
                            add(1)
                            cell(0)
                            cell(1)
                            state(0)
                            state(1)
                            keep(0)
                            keep(1)

            @block.scalar
            def _(act):
                with act.Fori(0, turns) as turn:
                    for i in range(PER_TURN):
                        done = 2 * PER_TURN * turn + 2 * i
                        for way in range(2):
                            for j in range(KH):
                                act.wait_ge(added[way], 2 + done + j + 1)
                                nc.scalar.activation(gate[:, way, j], z[:, way, j, 0:3], ACT.Sigmoid)
                                nc.scalar.activation(gc[:, way, j, 0], z[:, way, j, 3], ACT.Tanh).then_inc(gated[way], 1)
                            for j in range(KH):
                                act.wait_ge(celled[way], done + j + 1)
                                nc.scalar.activation(tc[:, way, j], gc[:, way, j, 1], ACT.Tanh).then_inc(tanhed[way], 1)

            @block.sync
            def _(sp):
                def store_and_load(turn, more):
                    for buf in range(2):
                        for way in range(2):
                            steps = 2 * PER_TURN * turn + 2 * STEPS * (buf + 1)
                            sp.wait_ge(ready[way], steps)
                            for e in range(E):
                                sp.dma_start(d["hs"][way, e, :, bass.ds(first_time(way, turn, buf), STEPS)],
                                             hs[rows_of(e), way, buf]).then_inc(hs_out[way][buf], 16)
                            if more:
                                load_zx(sp, way, turn + 1, buf)

                with sp.Fori(0, turns - 1) as turn:
                    store_and_load(turn, True)
                store_and_load(turns - 1, False)
                for buf in range(2):
                    for way in range(2):
                        sp.wait_ge(hs_out[way][buf], 64 * turns + 1)


def experts_after(core, d):
    nc, bank = core.nc, core.bank
    with ExitStack() as ctx:
        w = core.sb(ctx, "cw", [P, POST_W])
        cols = core.sb(ctx, "ccols", [P, COLS_W])
        rows = core.sb(ctx, "crows", [P, ROWS_W])
        mem = core.sb(ctx, "cmem", [P, 2, BT, DM])
        memT = core.sb(ctx, "cmemT", [P, 4, S])
        hid = core.sb(ctx, "chid", [P, 4, S])
        gt = core.sb(ctx, "cgt", [P, 4, S])
        g = core.sb(ctx, "cg", [P, KH, S])
        d1 = core.sb(ctx, "cd1", [P, KH, S])
        y = core.sb(ctx, "cy", [P, BT, D])
        yn = core.sb(ctx, "cyn", [P, BT, D])
        yg = core.sb(ctx, "cyg", [P, BT, D])
        yb = core.sb(ctx, "cyb", [P, BT, D])
        wt = core.sb(ctx, "cwt", [P, BT])
        stats = core.sb(ctx, "cstats", [P, BT, 6])
        mv = core.sb(ctx, "cmv", [P, BT, 2])
        var = core.sb(ctx, "cvar", [P, BT])
        std = core.sb(ctx, "cstd", [P, BT])
        rstd = core.sb(ctx, "crstd", [P, BT])
        (loaded, mem_turned, memT_kept, hid_mm, hid_kept, gate_mm, gate_kept, product, d1_mm, d1_kept, y_mm, y_kept,
         stats_done, mv_done, var_done, std_done, rstd_done, normed, gained, shifted) = core.sems(
            "ea", "loaded memturned memTkept hidmm hidkept gatemm gatekept product d1mm d1kept ymm ykept stats mv var "
                  "std rstd normed gained shifted")
        mem_in = core.sems("ea", "memin0 memin1")

        def weight(name, part, m):
            width = D if name == "dw2" else DM
            at = POST[name] + part * width + m * P
            return w[:, at:at + P]

        def col(name, part):
            return cols[:, COLS[name] + part:COLS[name] + part + 1]

        def row(name):
            return rows[:, ROWS[name]:ROWS[name] + D].unsqueeze(1).broadcast_to([P, BT, D])

        with nc.Fori(0, E) as e:
            with nc.Block() as block:
                @block.sync
                def _(sp):
                    sp.dma_start(w[:], d["w_after"][e]).then_inc(loaded, 16)
                    sp.dma_start(cols[:], d["cols"][e]).then_inc(loaded, 16)
                    sp.dma_start(rows[:], d["rows"][e].partition_broadcast(P)).then_inc(loaded, 16)
                    sp.wait_ge(loaded, 48)
            with nc.Fori(0, B) as b:
                with nc.Block() as block:
                    @block.sync
                    def _(sp):
                        for way in range(2):
                            sp.dma_start(mem[:, way], d["hs"][way, e, b].rearrange("(t p) u -> p t u", p=P)
                                         ).then_inc(mem_in[way], 16)

                    @block.tensor
                    def _(pe):
                        for k in range(4):
                            pe.wait_ge(mem_in[k // 2], 16)
                            for t in range(BT):
                                last = nc.tensor.transpose(bank[k][:, t * P:(t + 1) * P],
                                                           mem[:, k // 2, t, k % 2 * P:(k % 2 + 1) * P], core.ident[:])
                            last.then_inc(mem_turned, 1)
                        pe.wait_ge(memT_kept, 4)
                        for m in range(4):
                            for k in range(4):
                                last = nc.tensor.matmul(bank[4 + m][:], weight(("sw1", "tw1")[m // 2], k, m % 2),
                                                        memT[:, k], start=k == 0, stop=k == 3)
                            last.then_inc(hid_mm, 1)
                        for m in range(4):
                            for k in range(KH):
                                pe.wait_ge(hid_kept, m // 2 * 2 + k + 1)
                                last = nc.tensor.matmul(bank[m][:], weight(("sw2", "tw2")[m // 2], k, m % 2),
                                                        hid[:, m // 2 * 2 + k], start=k == 0, stop=k == KH - 1)
                            last.then_inc(gate_mm, 1)
                        pe.wait_ge(product, KH)
                        for m in range(KH):
                            for k in range(KH):
                                last = nc.tensor.matmul(bank[4 + m][:], weight("dw1", k, m), g[:, k], start=k == 0,
                                                        stop=k == KH - 1)
                            last.then_inc(d1_mm, 1)
                        pe.wait_ge(d1_kept, KH)
                        for t in range(BT):
                            for k in range(KH):
                                last = nc.tensor.matmul(bank[t][:, 0:D], d1[:, k, t * P:(t + 1) * P],
                                                        weight("dw2", k, 0), start=k == 0, stop=k == KH - 1)
                            last.then_inc(y_mm, 1)

                    @block.scalar
                    def _(act):
                        for k in (1, 3):
                            act.wait_ge(mem_turned, k + 1)
                            nc.scalar.activation(memT[:, k], bank[k][:], ACT.Copy).then_inc(memT_kept, 1)
                        for m in range(4):
                            act.wait_ge(hid_mm, m + 1)
                            nc.scalar.activation(hid[:, m], bank[4 + m][:], ACT.Relu,
                                                 bias=col(("sb1", "tb1")[m // 2], m % 2)).then_inc(hid_kept, 1)
                        for m in range(4):
                            act.wait_ge(gate_mm, m + 1)
                            nc.scalar.activation(gt[:, m], bank[m][:], (ACT.Sigmoid, ACT.Tanh)[m // 2],
                                                 bias=col(("sb2", "tb2")[m // 2], m % 2)).then_inc(gate_kept, 1)
                        for m in range(KH):
                            act.wait_ge(d1_mm, m + 1)
                            nc.scalar.activation(d1[:, m], bank[4 + m][:], ACT.Relu, bias=col("db1", m)).then_inc(d1_kept, 1)
                        act.wait_ge(var_done, 1)
                        nc.scalar.activation(std[:], var[:], ACT.Sqrt).then_inc(std_done, 1)

                    @block.vector
                    def _(dve):
                        nc.vector.tensor_copy(wt[:], core.route[:, bass.ds(b * BT, BT), e])
                        for k in (0, 2):
                            dve.wait_ge(mem_turned, k + 1)
                            nc.vector.tensor_copy(memT[:, k], bank[k][:]).then_inc(memT_kept, 1)
                        for m in range(KH):
                            dve.wait_ge(gate_kept, KH + m + 1)
                            nc.vector.tensor_tensor(g[:, m], gt[:, m], gt[:, KH + m], ALU.mult).then_inc(product, 1)
                        for t in range(BT):
                            dve.wait_ge(y_mm, t + 1)
                            nc.vector.tensor_tensor(y[:, t], bank[t][:, 0:D], rows[:, ROWS["db2"]:ROWS["db2"] + D],
                                                    ALU.add).then_inc(y_kept, 1)
                            dve.wait_ge(y_kept, t + 1)
                            nc.vector.bn_stats(stats[:, t], y[:, t]).then_inc(stats_done, 1)
                            dve.wait_ge(stats_done, t + 1)
                            nc.vector.bn_aggr(mv[:, t], stats[:, t]).then_inc(mv_done, 1)
                        dve.wait_ge(mv_done, BT)
                        nc.vector.tensor_scalar(var[:], mv[:, :, 1], EPS, None, ALU.add).then_inc(var_done, 1)
                        dve.wait_ge(std_done, 1)
                        nc.vector.reciprocal(rstd[:], std[:]).then_inc(rstd_done, 1)
                        dve.wait_ge(rstd_done, 1)
                        for t in range(BT):
                            nc.vector.tensor_scalar(yn[:, t], y[:, t], mv[:, t, 0:1], rstd[:, t:t + 1],
                                                    ALU.subtract, ALU.mult).then_inc(normed, 1)
                        dve.wait_ge(normed, BT)
                        nc.vector.tensor_tensor(yg[:], yn[:], row("dg"), ALU.mult).then_inc(gained, 1)
                        dve.wait_ge(gained, 1)
                        nc.vector.tensor_tensor(yb[:], yg[:], row("dbeta"), ALU.add).then_inc(shifted, 1)
                        dve.wait_ge(shifted, 1)
                        for t in range(BT):
                            ht = core.h[:, bass.ds(b * BT + t, 1)].rearrange("p t d -> p (t d)")
                            nc.vector.scalar_tensor_tensor(out=ht, in0=yb[:, t], scalar=wt[:, t:t + 1], in1=ht,
                                                           op0=ALU.mult, op1=ALU.add)
                clear_signals(nc, mem_in + [mem_turned, memT_kept, hid_mm, hid_kept, gate_mm, gate_kept, product, d1_mm,
                                            d1_kept, y_mm, y_kept, stats_done, mv_done, var_done, std_done, rstd_done,
                                            normed, gained, shifted])
            clear_signals(nc, [loaded])


def state_space(core, d):
    nc, bank = core.nc, core.bank
    PAIRS = B // 2
    with ExitStack() as ctx:
        bT = core.sb(ctx, "sbT", [P, NST])
        cT = core.sb(ctx, "scT", [P, D])
        alog = core.sb(ctx, "salog", [P, 1])
        a = core.sb(ctx, "sa", [P, 1])
        nega = core.sb(ctx, "snega", [P, 1])
        dtw = core.sb(ctx, "sdtw", [P, 1])
        dtw_wide = core.sb(ctx, "sdtww", [P, NST])
        dtb = core.sb(ctx, "sdtb", [P, 1])
        drow = core.sb(ctx, "sdrow", [P, D])
        gamma = core.sb(ctx, "sgamma", [P, D])
        beta = core.sb(ctx, "sbeta", [P, D])
        sig = core.sb(ctx, "ssig", [P, PAIRS, S])
        dt = core.sb(ctx, "sdt", [P, PAIRS, S])
        da = core.sb(ctx, "sda", [P, PAIRS, S])
        dbu = core.sb(ctx, "sdbu", [P, PAIRS, S])
        st = core.sb(ctx, "sst", [P, PAIRS, S])
        dx = core.sb(ctx, "sdx", [P, TILES, D])
        y = core.sb(ctx, "sy", [P, TILES, D])
        yn = core.sb(ctx, "syn", [P, TILES, D])
        yg = core.sb(ctx, "syg", [P, TILES, D])
        yb = core.sb(ctx, "syb", [P, TILES, D])
        stats = core.sb(ctx, "sstats", [P, TILES, 6])
        mv = core.sb(ctx, "smv", [P, TILES, 2])
        var = core.sb(ctx, "svar", [P, TILES])
        std = core.sb(ctx, "sstd", [P, TILES])
        rstd = core.sb(ctx, "srstd", [P, TILES])
        (loaded, a_exp, a_ready, wide_ready, dt_mm, u_mm, sig_done, dt_done, da_done, dbu_done, scanned, dx_done, y_mm,
         y_kept, stats_done, mv_done, var_done, std_done, rstd_done, normed, gained, shifted) = core.sems(
            "ss", "loaded aexp aready wide dtmm umm sig dt da dbu scanned dx ymm ykept stats mv var std rstd normed "
                  "gained shifted")
        with nc.Block() as block:
            @block.sync
            def _(sp):
                for dst, src in ((bT, d["B_T"]), (dtw, d["dt_w"]), (alog, d["A_log"]), (cT, d["C_T"]),
                                 (dtb, d["dt_b"].partition_broadcast(P)), (drow, d["D_vec"].partition_broadcast(P)),
                                 (gamma, d["gamma"].partition_broadcast(P)), (beta, d["beta"].partition_broadcast(P))):
                    sp.dma_start(dst[:], src).then_inc(loaded, 16)

            @block.tensor
            def _(pe):
                pe.wait_ge(loaded, 8 * 16)
                pe.wait_ge(wide_ready, 1)
                for p in range(PAIRS):
                    for half in range(2):
                        b = 2 * p + half
                        r = slice(half * NST, (half + 1) * NST)
                        x = core.xT[:, b * S:(b + 1) * S]
                        nc.tensor.matmul(bank[p][r, :], dtw_wide[:], x, start=True, stop=True).then_inc(dt_mm, 1)
                        nc.tensor.matmul(bank[2 + p][r, :], bT[:], x, start=True, stop=True).then_inc(u_mm, 1)
                for t in range(TILES):
                    b = t // BT
                    pe.wait_ge(scanned, b // 2 + 1)
                    r = slice(b % 2 * NST, (b % 2 + 1) * NST)
                    last = nc.tensor.matmul(bank[4 + b][:, t % BT * D:(t % BT + 1) * D],
                                            st[r, b // 2, t % BT * P:(t % BT + 1) * P], cT[r, :], start=True, stop=True)
                    if t % BT == BT - 1:
                        last.then_inc(y_mm, 1)

            @block.scalar
            def _(act):
                act.wait_ge(loaded, 8 * 16)
                nc.scalar.activation(a[:], alog[:], ACT.Exp).then_inc(a_exp, 1)
                for p in range(PAIRS):
                    act.wait_ge(dt_mm, 2 * p + 2)
                    nc.scalar.activation(sig[:, p], bank[p][:], ACT.Sigmoid, bias=dtb[:, 0:1]).then_inc(sig_done, 1)
                act.wait_ge(a_ready, 1)
                for p in range(PAIRS):
                    act.wait_ge(dt_done, p + 1)
                    nc.scalar.activation(da[:, p], dt[:, p], ACT.Exp, scale=nega[:, 0:1]).then_inc(da_done, 1)
                act.wait_ge(var_done, 1)
                nc.scalar.activation(std[:], var[:], ACT.Sqrt).then_inc(std_done, 1)

            @block.vector
            def _(dve):
                def wide(v, n=TILES):
                    return v[:].unsqueeze(1).broadcast_to([P, n, D])

                dve.wait_ge(loaded, 8 * 16)
                nc.vector.tensor_copy(dtw_wide[:], dtw[:, 0:1].broadcast_to([P, NST])).then_inc(wide_ready, 1)
                dve.wait_ge(a_exp, 1)
                nc.vector.tensor_scalar(nega[:], a[:], -1.0, None, ALU.mult).then_inc(a_ready, 1)
                nc.vector.tensor_tensor(dx[:], core.xn[:], wide(drow), ALU.mult).then_inc(dx_done, 1)
                for p in range(PAIRS):
                    dve.wait_ge(sig_done, p + 1)
                    nc.vector.tensor_scalar(dt[:, p], sig[:, p], 0.1 - 0.001, 0.001, ALU.mult, ALU.add).then_inc(dt_done, 1)
                for p in range(PAIRS):
                    dve.wait_ge(dt_done, p + 1)
                    dve.wait_ge(u_mm, 2 * p + 2)
                    nc.vector.tensor_tensor(dbu[:, p], bank[2 + p][:], dt[:, p], ALU.mult).then_inc(dbu_done, 1)
                for p in range(PAIRS):
                    dve.wait_ge(da_done, p + 1)
                    dve.wait_ge(dbu_done, p + 1)
                    nc.vector.tensor_tensor_scan(st[:, p], da[:, p], dbu[:, p], 0.0, ALU.mult, ALU.add
                                                 ).then_inc(scanned, 1)
                dve.wait_ge(dx_done, 1)
                for b in range(B):
                    dve.wait_ge(y_mm, b + 1)
                    nc.vector.tensor_tensor(y[:, b * BT:(b + 1) * BT], bank[4 + b][:].rearrange("p (t d) -> p t d", d=D),
                                            dx[:, b * BT:(b + 1) * BT], ALU.add).then_inc(y_kept, 1)
                for t in range(TILES):
                    dve.wait_ge(y_kept, t // BT + 1)
                    nc.vector.bn_stats(stats[:, t], y[:, t]).then_inc(stats_done, 1)
                for t in range(TILES):
                    dve.wait_ge(stats_done, t + 1)
                    nc.vector.bn_aggr(mv[:, t], stats[:, t]).then_inc(mv_done, 1)
                dve.wait_ge(mv_done, TILES)
                nc.vector.tensor_scalar(var[:], mv[:, :, 1], EPS, None, ALU.add).then_inc(var_done, 1)
                dve.wait_ge(std_done, 1)
                nc.vector.reciprocal(rstd[:], std[:]).then_inc(rstd_done, 1)
                dve.wait_ge(rstd_done, 1)
                for t in range(TILES):
                    nc.vector.tensor_scalar(yn[:, t], y[:, t], mv[:, t, 0:1], rstd[:, t:t + 1],
                                            ALU.subtract, ALU.mult).then_inc(normed, 1)
                dve.wait_ge(normed, TILES)
                nc.vector.tensor_tensor(yg[:], yn[:], wide(gamma), ALU.mult).then_inc(gained, 1)
                dve.wait_ge(gained, 1)
                nc.vector.tensor_tensor(yb[:], yg[:], wide(beta), ALU.add).then_inc(shifted, 1)
                dve.wait_ge(shifted, 1)
                nc.vector.tensor_tensor(core.h[:], core.h[:], yb[:], ALU.add)


def feature_mixer(core, d):
    nc, bank = core.nc, core.bank
    with ExitStack() as ctx:
        w = core.sb(ctx, "fw", [P, 2, P])
        wm = core.sb(ctx, "fwm", [P, 2, P])
        keep = core.sb(ctx, "fkeep", [P, P])
        b1 = core.sb(ctx, "fb1", [P, 1])
        b2 = core.sb(ctx, "fb2", [P, D])
        act_out = core.sb(ctx, "fact", [P, B, S])
        hb = core.sb(ctx, "fhb", [P, TILES, D])
        loaded, masked, mm1, acted, mm2, biased = core.sems("fm", "loaded masked mm1 acted mm2 biased")
        with nc.Block() as block:
            @block.sync
            def _(sp):
                for dst, src in ((w, d["mix_w"]), (keep, d["tril_T"]), (b1, d["mix_b1"]),
                                 (b2, d["mix_b2"].partition_broadcast(P))):
                    sp.dma_start(dst[:], src).then_inc(loaded, 16)

            @block.vector
            def _(dve):
                dve.wait_ge(loaded, 64)
                nc.vector.tensor_tensor(wm[:], w[:], keep[:].unsqueeze(1).broadcast_to([P, 2, P]), ALU.mult
                                        ).then_inc(masked, 1)
                nc.vector.tensor_tensor(hb[:], core.h[:], b2[:].unsqueeze(1).broadcast_to([P, TILES, D]), ALU.add
                                        ).then_inc(biased, 1)
                dve.wait_ge(biased, 1)
                for b in range(B):
                    dve.wait_ge(mm2, b + 1)
                    nc.vector.tensor_tensor(core.h[:, b * BT:(b + 1) * BT],
                                            bank[4 + b][:].rearrange("p (t d) -> p t d", d=D),
                                            hb[:, b * BT:(b + 1) * BT], ALU.add)

            @block.tensor
            def _(pe):
                pe.wait_ge(masked, 1)
                for b in range(B):
                    nc.tensor.matmul(bank[b][:], wm[:, 0], core.xT[:, b * S:(b + 1) * S], start=True,
                                     stop=True).then_inc(mm1, 1)
                for b in range(B):
                    pe.wait_ge(acted, b + 1)
                    for t in range(BT):
                        last = nc.tensor.matmul(bank[4 + b][:, t * D:(t + 1) * D], act_out[:, b, t * P:(t + 1) * P],
                                                wm[:, 1], start=True, stop=True)
                    last.then_inc(mm2, 1)

            @block.scalar
            def _(act):
                act.wait_ge(loaded, 64)
                for b in range(B):
                    act.wait_ge(mm1, b + 1)
                    nc.scalar.activation(act_out[:, b], bank[b][:], ACT.Gelu, bias=b1[:, 0:1]).then_inc(acted, 1)


def store(core, d):
    nc = core.nc
    (stored,) = core.sems("out", "stored")
    with nc.Block() as block:
        @block.sync
        def _(sp):
            sp.dma_start(d["out"].rearrange("(t p) d -> p t d", p=P), core.h[:]).then_inc(stored, 16)
            sp.wait_ge(stored, 16)


def pack(x, **w):
    n = np
    f = n.float32

    def permute_gates(a):
        a = a.reshape(a.shape[:-1] + (4, 2, P))
        return n.ascontiguousarray(n.moveaxis(a[..., [0, 1, 3, 2], :, :], -2, -3)).reshape(a.shape[:-3] + (G4,))

    def rows(a):
        e, k, m = a.shape
        return n.moveaxis(a.reshape(e, k // P, P, m), 1, 2).reshape(e, P, k // P * m)

    def cols(a):
        return n.moveaxis(a.reshape(E, KH, P), 1, 2)

    out = {}
    pos = n.arange(N_FRAMES)[:, None] * N_FFT + n.arange(N_FFT)[None] - N_FFT // 2
    pos = n.abs(pos)
    pos = n.where(pos >= S, 2 * (S - 1) - pos, pos)
    out["ids_frames"] = n.ascontiguousarray(x[:, pos].reshape(BF, N_FFT).T)
    out["ids"] = n.ascontiguousarray(x.reshape(TOK))
    out["vocab_row"] = n.broadcast_to(n.arange(VOCAB, dtype=f), (N_FFT, VOCAB)).copy()
    out["vocab_col"] = n.arange(VOCAB, dtype=f)[:, None].copy()
    j = n.arange(N_FFT, dtype=n.float64)[:, None]
    fr = n.arange(N_FREQ, dtype=n.float64)[None]
    win = 0.5 - 0.5 * n.cos(2 * n.pi * j / N_FFT)
    ang = 2 * n.pi * (j * fr % N_FFT) / N_FFT
    out["dft"] = n.stack([win * n.cos(ang), win * n.sin(ang)], 1).astype(f)
    up = n.zeros((BF, TOK), f)
    for b in range(B):
        up[b * N_FRAMES + n.arange(S) * N_FRAMES // S, b * S + n.arange(S)] = 1
    out["upsample"] = up
    out["ident"] = n.eye(P, dtype=f)
    out["causal"] = n.where(n.arange(P)[None] > n.arange(P)[:, None], f(-1e30), f(0)).astype(f)
    out["emb_table"] = w["L0_tok_emb_table"]
    out["proj_w"] = w["L0_tok_proj_w"].reshape(N_FREQ, VOCAB, D_STFT)
    out["proj_b"] = w["L0_tok_proj_b"]
    qkv = [n.moveaxis(w[f"L0_attn_W_{c}"], 0, 1).reshape(D, AH * ADK) for c in "qkv"]
    wo = n.moveaxis(w["L0_attn_W_o"].reshape(4, P, D), 0, 1).reshape(P, 4 * D)
    out["attn_w"] = n.stack(qkv + [wo], 1)
    for name in ("router_w", "router_b"):
        out[name] = w["L0_ffn_" + name]
    out["head_mask"] = (n.arange(P)[:, None] // DH == n.arange(8)[None]).astype(f)
    ff = {k[len("L0_ffn_"):]: v for k, v in w.items() if k.startswith("L0_ffn_")}
    aow = n.zeros((E, 4, 4, 32, DM), f)
    aow[:, :, :, 0:DH] = ff["attn_out_w"].reshape(E, 4, 4, DH, DM)
    out["w_before"] = n.concatenate(
        [rows(ff["enc_w1"]), rows(ff["enc_w2"]), rows(ff["attn_in_w"]), rows(aow.reshape(E, 4 * P, DM)),
         rows(permute_gates(ff["lstm_wi_f"])), rows(permute_gates(ff["lstm_wi_b"]))], 2)
    out["w_after"] = n.concatenate([rows(ff[c]) for c in ("sig_w1", "sig_w2", "tan_w1", "tan_w2", "dec_w1", "dec_w2")], 2)
    inb = ff["attn_in_b"]
    out["cols"] = n.concatenate(
        [cols(a) for a in (ff["enc_b1"], ff["enc_g"], ff["enc_beta"], inb[:, 0:DM], inb[:, DM:2 * DM],
                           ff["attn_out_b"], ff["sig_b1"], ff["tan_b1"], ff["sig_b2"], ff["tan_b2"], ff["dec_b1"])], 2)
    out["rows"] = n.concatenate(
        [ff["enc_b2"], inb[:, 2 * DM:], permute_gates(ff["lstm_b_f"]), permute_gates(ff["lstm_b_b"]), ff["dec_b2"],
         ff["dec_g"], ff["dec_beta"]], 1)
    out["wh"] = n.ascontiguousarray(n.stack([rows(permute_gates(ff["lstm_wh_" + c])) for c in "fb"])
                                    .reshape(2, E, P, KH, G4).transpose(2, 0, 1, 3, 4))
    ss = {k[len("L1_attn_"):]: v for k, v in w.items() if k.startswith("L1_attn_")}
    out["B_T"] = ss["B_mat"].T
    out["C_T"] = n.concatenate([ss["C_mat"].T, ss["C_mat"].T], 0)
    out["A_log"] = n.concatenate([ss["A_log"], ss["A_log"]])[:, None]
    out["dt_w"] = ss["dt_w"].reshape(D, 1)
    for name in ("dt_b", "D_vec", "gamma", "beta"):
        out[name] = ss[name]
    out["mix_w"] = n.stack([w["L1_ffn_W1"].T, w["L1_ffn_W2"].T], 1)
    out["tril_T"] = n.triu(n.ones((P, P), f))
    out["mix_b1"] = w["L1_ffn_b1"][:, None]
    out["mix_b2"] = w["L1_ffn_b2"]
    return out


def build(nc, d, phases=None):
    with ExitStack() as ctx:
        core = Core(nc, ctx)
        d["zx"] = nc.dram_tensor("zx", (2, E, B, S, G4), F32, kind="Internal").ap()
        d["hs"] = nc.dram_tensor("hs", (2, E, B, S, DM), F32, kind="Internal").ap()
        for phase in PHASES[:phases]:
            core.run(phase, d)
        core.run(store, d)


PHASES = [
    embed,
    lambda core, d: layer_norm(core, "ln0"),
    causal_attention,
    lambda core, d: layer_norm(core, "ln1"),
    router,
    experts_before,
    recurrence,
    experts_after,
    lambda core, d: layer_norm(core, "ln2"),
    state_space,
    lambda core, d: layer_norm(core, "ln3"),
    feature_mixer,
]

NAMES = []


def kernel(**inputs):
    import concourse.bacc as bacc
    from concourse.bass_utils import run_bass_kernel_spmd

    nc = bacc.Bacc("TRN2", target_bir_lowering=False, num_devices=1)
    arrays = pack(**{k: np.asarray(v) for k, v in inputs.items()})
    arrays = {f"in_{k}": np.ascontiguousarray(v) for k, v in arrays.items()}
    d = {k[3:]: nc.dram_tensor(k, a.shape, mybir.dt.from_np(a.dtype), kind="ExternalInput").ap()
         for k, a in arrays.items()}
    d["out"] = nc.dram_tensor("out", (TOK, D), F32, kind="ExternalOutput").ap()
    build(nc, d)
    r = run_bass_kernel_spmd(nc, [arrays], core_ids=[0])
    return r.results[0]["out"].reshape(B, S, D)
```

```python
import concourse.bass as bass
from concourse import mybir
from contextlib import ExitStack
import numpy as np

F32 = mybir.dt.float32
BF16 = mybir.dt.bfloat16
I32 = mybir.dt.int32
ALU = mybir.AluOpType
ACT = mybir.ActivationFunctionType
AX = mybir.AxisListType

P = 128
B, S, D = 4, 512, 128
TOK = B * S
TILES = TOK // P
BT = S // P
EPS = 1e-5

VOCAB, D_EMB = 16, 89
D_STFT = D - D_EMB
N_FFT = 64
N_FREQ = N_FFT // 2 + 1
N_FRAMES = S // N_FFT + 1
BF = B * N_FRAMES

AH, ADK = 8, 64
E, DM, NH, DH = 4, 256, 16, 16
KH = DM // P
G4 = 4 * DM
NST = 64



def columns(*widths):
    at, out = 0, {}
    for name, width in widths:
        out[name] = at
        at += width
    return out, at


ENC, ENC_W = columns(("ew1", DM), ("ew2", KH * DM), ("qkv", KH * 3 * DM))
ATT, ATT_W = columns(("aow", KH * DM), ("wi", 2 * KH * G4))
POST, POST_W = columns(("sw1", 2 * KH * DM), ("sw2", KH * DM), ("tw1", 2 * KH * DM), ("tw2", KH * DM),
                       ("dw1", KH * DM), ("dw2", KH * D))
COLS = {n: KH * i for i, n in enumerate(("eb1", "eg", "ebeta", "qb", "kb", "aob", "sb1", "tb1", "sb2", "tb2", "db1"))}
COLS_W = KH * len(COLS)
ROWS, ROWS_W = columns(("eb2", DM), ("vb", DM), ("lb", 2 * G4), ("db2", D), ("dg", D), ("dbeta", D))


def clear_signals(nc, signals):
    with nc.Block() as block:
        @block.vector
        def _(dve):
            for s in signals:
                dve.sem_clear(s)


class Core:

    def __init__(self, nc, ctx):
        self.nc, self.ctx = nc, ctx
        self.bank = [ctx.enter_context(nc.psum_tensor(f"bank{i}", [P, 512], F32)) for i in range(8)]
        self.h = self.sb(ctx, "h", [P, TILES, D])
        self.xn = self.sb(ctx, "xn", [P, TILES, D])
        self.xT = self.sb(ctx, "xT", [P, TOK])
        self.ident = self.sb(ctx, "ident", [P, P])
        self.route = self.sb(ctx, "route", [P, TILES, E])

    def sb(self, ctx, name, shape, dt=F32):
        return ctx.enter_context(self.nc.sbuf_tensor(name, shape, dt))

    def sems(self, tag, names):
        made = [self.stage.enter_context(self.nc.semaphore(f"{tag}_{n}")) for n in names.split()]
        self.made += made
        return made

    def run(self, stage, d):
        self.made = []
        with ExitStack() as self.stage:
            stage(self, d)
            clear_signals(self.nc, self.made)


def embed(core, d):
    nc = core.nc
    half = BF // 2 * VOCAB
    with ExitStack() as ctx:
        ids_fr = core.sb(ctx, "ids_fr", [N_FFT, BF], I32)
        ids_tok = core.sb(ctx, "ids_tok", [VOCAB, TOK], I32)
        idf_fr = core.sb(ctx, "idf_fr", [N_FFT, BF])
        idf_tok = core.sb(ctx, "idf_tok", [VOCAB, TOK])
        vocab_row = core.sb(ctx, "vocab_row", [N_FFT, VOCAB])
        vocab_col = core.sb(ctx, "vocab_col", [VOCAB, 1])
        dft = core.sb(ctx, "dft", [N_FFT, 2, N_FREQ])
        hot_fr = core.sb(ctx, "hot_fr", [N_FFT, BF, VOCAB])
        hot_tok = core.sb(ctx, "hot_tok", [VOCAB, TOK])
        sq = core.sb(ctx, "sq", [N_FREQ, 2, BF * VOCAB])
        power = core.sb(ctx, "power", [N_FREQ, BF * VOCAB])
        mag = core.sb(ctx, "mag", [N_FREQ, BF, VOCAB])
        proj = core.sb(ctx, "proj", [N_FREQ, VOCAB, D_STFT])
        table = core.sb(ctx, "table", [VOCAB, D])
        enc = core.sb(ctx, "enc", [BF, D])
        bias = core.sb(ctx, "bias", [1, D])
        up = core.sb(ctx, "up", [BF, TOK])
        ones = core.sb(ctx, "ones", [1, P])
        loaded, zeroed, placed, cast, hot, dft_done, squared, summed, mag_ready, enc_done, enc_ready, h_done, h_kept = \
            core.sems("em", "loaded zeroed placed cast hot dft squared summed mag enc encr h kept")
        with nc.Block() as block:
            @block.sync
            def _(sp):
                for dst, src in ((ids_fr, d["ids_frames"]), (vocab_row, d["vocab_row"]), (dft, d["dft"]),
                                 (vocab_col, d["vocab_col"]), (proj, d["proj_w"]), (up, d["upsample"]),
                                 (core.ident, d["ident"])):
                    sp.dma_start(dst[:], src).then_inc(loaded, 16)
                sp.dma_start(ids_tok[:], d["ids"].partition_broadcast(VOCAB)).then_inc(loaded, 16)
                sp.wait_ge(zeroed, 3)
                sp.dma_start(table[:, 0:D_EMB], d["emb_table"]).then_inc(placed, 16)
                sp.dma_start(bias[:, D_EMB:D], d["proj_b"].unsqueeze(0)).then_inc(placed, 16)

            @block.vector
            def _(dve):
                nc.vector.memset(table[:], 0.0).then_inc(zeroed, 1)
                nc.vector.memset(bias[:], 0.0).then_inc(zeroed, 1)
                nc.vector.memset(enc[:], 0.0).then_inc(zeroed, 1)
                nc.vector.memset(ones[:], 1.0).then_inc(zeroed, 1)
                dve.wait_ge(loaded, 8 * 16)
                nc.vector.tensor_copy(idf_fr[:], ids_fr[:]).then_inc(cast, 1)
                nc.vector.tensor_copy(idf_tok[:], ids_tok[:]).then_inc(cast, 1)
                dve.wait_ge(cast, 2)
                nc.vector.tensor_tensor(hot_fr[:], idf_fr[:].unsqueeze(2).broadcast_to([N_FFT, BF, VOCAB]),
                                        vocab_row[:].unsqueeze(1).broadcast_to([N_FFT, BF, VOCAB]),
                                        ALU.is_equal).then_inc(hot, 1)
                nc.vector.tensor_scalar(hot_tok[:], idf_tok[:], vocab_col[:, 0:1], None,
                                        ALU.is_equal).then_inc(hot, 1)
                dve.wait_ge(squared, 4)
                nc.vector.tensor_tensor(power[:], sq[:, 0], sq[:, 1], ALU.add).then_inc(summed, 1)
                dve.wait_ge(enc_done, 1)
                nc.vector.tensor_copy(enc[:, D_EMB:D], core.bank[4][0:BF, 0:D_STFT]).then_inc(enc_ready, 1)
                for g in range(4):
                    dve.wait_ge(h_done, g + 1)
                    nc.vector.tensor_copy(core.h[:, 4 * g:4 * g + 4],
                                          core.bank[g][:].rearrange("p (t d) -> p t d", d=D)).then_inc(h_kept, 1)

            @block.tensor
            def _(pe):
                pe.wait_ge(hot, 2)
                frames = hot_fr[:].rearrange("p f v -> p (f v)")
                for part in range(2):
                    for n in range(2):
                        nc.tensor.matmul(core.bank[2 * part + n][0:N_FREQ, 0:half], dft[:, part],
                                         frames[:, n * half:(n + 1) * half], start=True,
                                         stop=True).then_inc(dft_done, 1)
                pe.wait_ge(mag_ready, 1)
                for v in range(VOCAB):
                    last = nc.tensor.matmul(core.bank[4][0:BF, 0:D_STFT], mag[:, :, v], proj[:, v],
                                            start=v == 0, stop=v == VOCAB - 1)
                last.then_inc(enc_done, 1)
                pe.wait_ge(enc_ready, 1)
                pe.wait_ge(placed, 32)
                pe.wait_ge(zeroed, 4)
                for t in range(TILES):
                    out = core.bank[t // 4][:, (t % 4) * D:(t % 4 + 1) * D]
                    tok = slice(t * P, (t + 1) * P)
                    nc.tensor.matmul(out, hot_tok[:, tok], table[:], start=True, stop=False)
                    nc.tensor.matmul(out, up[:, tok], enc[:], start=False, stop=False)
                    last = nc.tensor.matmul(out, ones[:], bias[:], start=False, stop=True)
                    if t % 4 == 3:
                        last.then_inc(h_done, 1)

            @block.scalar
            def _(act):
                for part in range(2):
                    for n in range(2):
                        act.wait_ge(dft_done, 2 * part + n + 1)
                        nc.scalar.activation(sq[:, part, n * half:(n + 1) * half],
                                             core.bank[2 * part + n][0:N_FREQ, 0:half],
                                             ACT.Square).then_inc(squared, 1)
                act.wait_ge(summed, 1)
                nc.scalar.activation(mag[:].rearrange("p f v -> p (f v)"), power[:], ACT.Sqrt).then_inc(mag_ready, 1)


def layer_norm(core, tag):
    nc = core.nc
    with ExitStack() as ctx:
        stats = core.sb(ctx, f"{tag}_stats", [P, TILES, 6])
        mv = core.sb(ctx, f"{tag}_mv", [P, TILES, 2])
        var = core.sb(ctx, f"{tag}_var", [P, TILES])
        std = core.sb(ctx, f"{tag}_std", [P, TILES])
        rstd = core.sb(ctx, f"{tag}_rstd", [P, TILES])
        stats_done, mv_done, var_done, std_done, rstd_done, normed, turned, kept = \
            core.sems(tag, "stats mv var std rstd normed turned kept")
        with nc.Block() as block:
            @block.vector
            def _(dve):
                for t in range(TILES):
                    nc.vector.bn_stats(stats[:, t], core.h[:, t]).then_inc(stats_done, 1)
                for t in range(TILES):
                    dve.wait_ge(stats_done, t + 1)
                    nc.vector.bn_aggr(mv[:, t], stats[:, t]).then_inc(mv_done, 1)
                dve.wait_ge(mv_done, TILES)
                nc.vector.tensor_scalar(var[:], mv[:, :, 1], EPS, None, ALU.add).then_inc(var_done, 1)
                dve.wait_ge(std_done, 1)
                nc.vector.reciprocal(rstd[:], std[:]).then_inc(rstd_done, 1)
                dve.wait_ge(rstd_done, 1)
                for t in range(TILES):
                    nc.vector.tensor_scalar(core.xn[:, t], core.h[:, t], mv[:, t, 0:1], rstd[:, t:t + 1],
                                            ALU.subtract, ALU.mult).then_inc(normed, 1)

            @block.scalar
            def _(act):
                act.wait_ge(var_done, 1)
                nc.scalar.activation(std[:], var[:], ACT.Sqrt).then_inc(std_done, 1)
                for g in range(4):
                    act.wait_ge(turned, g + 1)
                    nc.scalar.activation(core.xT[:, g * 512:(g + 1) * 512], core.bank[g][:], ACT.Copy).then_inc(kept, 1)

            @block.tensor
            def _(pe):
                for t in range(TILES):
                    pe.wait_ge(normed, t + 1)
                    last = nc.tensor.transpose(core.bank[t // 4][:, (t % 4) * P:(t % 4 + 1) * P], core.xn[:, t],
                                               core.ident[:])
                    if t % 4 == 3:
                        last.then_inc(turned, 1)


class Attention:

    def __init__(self, core, ctx, tag, heads, causal, per_bank, rows):
        self.core, self.heads, self.causal, self.per_bank, self.rows = core, heads, causal, per_bank, rows
        self.p = core.sb(ctx, f"{tag}_p", [P, 2, BT, S])
        self.pT = core.sb(ctx, f"{tag}_pT", [P, 2, BT, S])
        self.negmax = core.sb(ctx, f"{tag}_negmax", [P, heads, BT])
        self.total = core.sb(ctx, f"{tag}_total", [P, heads, BT])
        self.inv = core.sb(ctx, f"{tag}_inv", [P, heads, BT])
        self.oT = core.sb(ctx, f"{tag}_oT", [P, heads // per_bank, S])
        (self.scored, self.maxed, self.exped, self.inverted, self.normed, self.turned, self.kept_v, self.kept_a,
         self.valued, self.out_kept) = core.sems(
            tag, "scored maxed exped inverted normed turned keptv kepta valued outkept")
        self.signals = [self.scored, self.maxed, self.exped, self.inverted, self.normed, self.turned, self.kept_v,
                        self.kept_a, self.valued, self.out_kept]

    def width(self, qt):
        return (qt + 1) * P if self.causal else S

    def low(self, kt):
        return kt * P if self.causal else 0

    def tensor(self, pe, query, key, value, key_wait, mask):
        nc, bank = self.core.nc, self.core.bank

        def score(h, qt):
            if qt == 0:
                key_wait(pe, h)
            if h > 0:
                pe.wait_ge(self.exped, BT * (h - 1) + qt + 1)
            w = self.width(qt)
            last = nc.tensor.matmul(bank[qt][:, 0:w], query(h, qt), key(h)[:, 0:w], start=True, stop=not self.causal)
            if self.causal:
                last = nc.tensor.matmul(bank[qt][:, qt * P:w], self.core.ident[:], mask, start=False, stop=True)
            last.then_inc(self.scored, 1)

        def turn(h, kt):
            n = BT * h + kt
            if kt == 0:
                pe.wait_ge(self.normed, BT * (h + 1))
            if n >= 2:
                pe.wait_ge(*((self.kept_a, (n - 2) // 2 + 1) if kt % 2 else (self.kept_v, (n - 2) // 2 + 1)))
            for qt in range(kt if self.causal else 0, BT):
                last = nc.tensor.transpose(bank[4 + kt % 2][:, qt * P:(qt + 1) * P],
                                           self.p[:, h % 2, qt, kt * P:(kt + 1) * P], self.core.ident[:])
            last.then_inc(self.turned, 1)

        def values(h, kt):
            n = BT * h + kt
            pe.wait_ge(*((self.kept_a, n // 2 + 1) if kt % 2 else (self.kept_v, n // 2 + 1)))
            g, c = divmod(h, self.per_bank)
            if c == 0 and kt == 0 and g >= 2:
                pe.wait_ge(self.out_kept, g - 1)
            r = c * (P // self.per_bank)
            lo = self.low(kt)
            nc.tensor.matmul(bank[6 + g % 2][r:r + self.rows, lo:S], value(h, kt), self.pT[:, h % 2, kt, lo:S],
                             start=kt == 0, stop=kt == BT - 1).then_inc(self.valued, 1)

        for h in range(self.heads + 1):
            for qt in (0, 1):
                if h < self.heads:
                    score(h, qt)
            if h > 0:
                turn(h - 1, 0)
                turn(h - 1, 1)
            if h < self.heads:
                score(h, 2)
            if h > 0:
                values(h - 1, 0)
                turn(h - 1, 2)
                values(h - 1, 1)
            if h < self.heads:
                score(h, 3)
            if h > 0:
                turn(h - 1, 3)
                values(h - 1, 2)
                values(h - 1, 3)

    def vector(self, dve):
        nc, bank = self.core.nc, self.core.bank

        def largest(h, qt):
            dve.wait_ge(self.scored, BT * h + qt + 1)
            nc.vector.tensor_reduce(self.negmax[:, h, qt:qt + 1], bank[qt][:, 0:self.width(qt)], AX.X, ALU.max,
                                    negate=True).then_inc(self.maxed, 1)

        def normalise(h):
            dve.wait_ge(self.exped, BT * (h + 1))
            nc.vector.reciprocal(self.inv[:, h], self.total[:, h]).then_inc(self.inverted, 1)
            dve.wait_ge(self.inverted, h + 1)
            for qt in range(BT):
                p = self.p[:, h % 2, qt, 0:self.width(qt)]
                nc.vector.tensor_scalar(p, p, self.inv[:, h, qt:qt + 1], None, ALU.mult).then_inc(self.normed, 1)

        def keep(h, kt):
            dve.wait_ge(self.turned, BT * h + kt + 1)
            if h >= 2:
                dve.wait_ge(self.valued, BT * (h - 2) + kt + 1)
            lo = self.low(kt)
            nc.vector.tensor_copy(self.pT[:, h % 2, kt, lo:S], bank[4 + kt % 2][:, lo:S]).then_inc(self.kept_v, 1)

        for h in range(self.heads + 1):
            if h < self.heads:
                largest(h, 0)
            if h > 0:
                normalise(h - 1)
            if h < self.heads:
                largest(h, 1)
            if h > 0:
                keep(h - 1, 0)
            if h < self.heads:
                largest(h, 2)
            if h > 0:
                keep(h - 1, 2)
            if h < self.heads:
                largest(h, 3)
            if h > 0 and h % self.per_bank == 0:
                g = h // self.per_bank - 1
                dve.wait_ge(self.valued, BT * h)
                nc.vector.tensor_copy(self.oT[:, g], bank[6 + g % 2][:]).then_inc(self.out_kept, 1)

    def scalar(self, act):
        nc, bank = self.core.nc, self.core.bank

        def exponent(h, qt):
            act.wait_ge(self.maxed, BT * h + qt + 1)
            if h >= 2 and qt == 0:
                act.wait_ge(self.turned, BT * (h - 1))
            w = self.width(qt)
            nc.scalar.activation(self.p[:, h % 2, qt, 0:w], bank[qt][:, 0:w], ACT.Exp,
                                 bias=self.negmax[:, h, qt:qt + 1],
                                 accum_out=self.total[:, h, qt:qt + 1]).then_inc(self.exped, 1)

        def keep(h, kt):
            act.wait_ge(self.turned, BT * h + kt + 1)
            if h >= 2:
                act.wait_ge(self.valued, BT * (h - 2) + kt + 1)
            lo = self.low(kt)
            nc.scalar.activation(self.pT[:, h % 2, kt, lo:S], bank[4 + kt % 2][:, lo:S],
                                 ACT.Copy).then_inc(self.kept_a, 1)

        for h in range(self.heads + 1):
            if h < self.heads:
                exponent(h, 0)
                exponent(h, 1)
            if h > 0:
                keep(h - 1, 1)
            if h < self.heads:
                exponent(h, 2)
            if h > 0:
                keep(h - 1, 3)
            if h < self.heads:
                exponent(h, 3)


def causal_attention(core, d):
    nc = core.nc
    with ExitStack() as ctx:
        w = core.sb(ctx, "aw", [P, 4, AH * ADK])
        mask = core.sb(ctx, "amask", [P, P])
        xb = core.sb(ctx, "axb", [P, S])
        qT = core.sb(ctx, "aqT", [P, 4, S])
        kz = core.sb(ctx, "akz", [P, AH, S])
        v = core.sb(ctx, "av", [P, BT, AH * ADK])
        att = Attention(core, ctx, "at", AH, True, 2, ADK)
        loaded, x_ready, q_mm, k_mm, v_mm, q_kept, k_kept, v_kept, o_mm, o_kept = \
            core.sems("at", "loaded x qmm kmm vmm qkept kkept vkept omm okept")
        with nc.Block() as block:
            @block.sync
            def _(sp):
                sp.dma_start(w[:], d["attn_w"]).then_inc(loaded, 16)
                sp.dma_start(mask[:], d["causal"]).then_inc(loaded, 16)
                sp.wait_ge(loaded, 32)

            @block.vector
            def _(dve):
                nc.vector.memset(kz[:], 0.0)
        with nc.Fori(0, B) as b:
            with nc.Block() as block:
                @block.tensor
                def _(pe):
                    pe.wait_ge(x_ready, 1)
                    for n in range(4):
                        nc.tensor.matmul(core.bank[n][:], w[:, 0, n * P:(n + 1) * P], xb[:], start=True,
                                         stop=True).then_inc(q_mm, 1)
                    for n in range(4):
                        nc.tensor.matmul(core.bank[4 + n][:], w[:, 1, n * P:(n + 1) * P], xb[:], start=True,
                                         stop=True).then_inc(k_mm, 1)
                    for t in range(BT):
                        pe.wait_ge(q_kept, t + 1)
                        nc.tensor.matmul(core.bank[t][:], xb[:, t * P:(t + 1) * P], w[:, 2], start=True,
                                         stop=True).then_inc(v_mm, 1)

                    def key_wait(pe, h):
                        if h == 0:
                            pe.wait_ge(v_kept, BT)
                            pe.wait_ge(k_kept, 8)

                    att.tensor(pe, lambda h, qt: qT[:, h // 2, qt * P:(qt + 1) * P], lambda h: kz[:, h],
                               lambda h, kt: v[:, kt, h * ADK:(h + 1) * ADK], key_wait, mask[:])
                    pe.wait_ge(att.out_kept, 4)
                    for t in range(BT):
                        for n in range(4):
                            last = nc.tensor.matmul(core.bank[0][:, t * D:(t + 1) * D],
                                                    att.oT[:, n, t * P:(t + 1) * P], w[:, 3, n * D:(n + 1) * D],
                                                    start=n == 0, stop=n == 3)
                    last.then_inc(o_mm, 1)

                @block.vector
                def _(dve):
                    nc.vector.tensor_copy(xb[:], core.xT[:, bass.ds(b * S, S)]).then_inc(x_ready, 1)
                    for n in range(4):
                        dve.wait_ge(k_mm, n + 1)
                        for half in (0, 1):
                            r = slice(half * ADK, (half + 1) * ADK)
                            nc.vector.tensor_copy(kz[r, 2 * n + half], core.bank[4 + n][r, :]).then_inc(k_kept, 1)
                    att.vector(dve)
                    dve.wait_ge(o_mm, 1)
                    hb = core.h[:, bass.ds(b * BT, BT)]
                    nc.vector.tensor_tensor(hb, core.bank[0][:].rearrange("p (t d) -> p t d", d=D), hb,
                                            ALU.add).then_inc(o_kept, 1)

                @block.scalar
                def _(act):
                    for n in range(4):
                        act.wait_ge(q_mm, n + 1)
                        nc.scalar.activation(qT[:, n], core.bank[n][:], ACT.Copy,
                                             scale=float(ADK) ** -0.5).then_inc(q_kept, 1)
                    for t in range(BT):
                        act.wait_ge(v_mm, t + 1)
                        nc.scalar.activation(v[:, t], core.bank[t][:], ACT.Copy).then_inc(v_kept, 1)
                    att.scalar(act)
            clear_signals(nc, att.signals + [x_ready, q_mm, k_mm, v_mm, q_kept, k_kept, v_kept, o_mm, o_kept])


def router(core, d):
    nc = core.nc
    with ExitStack() as ctx:
        rw = core.sb(ctx, "rw", [P, E])
        rb = core.sb(ctx, "rb", [P, E])
        logit = core.sb(ctx, "logit", [P, TILES, E])
        shifted = core.sb(ctx, "shifted", [P, TILES, E])
        ex = core.sb(ctx, "rex", [P, TILES, E])
        top = core.sb(ctx, "rtop", [P, TILES])
        total = core.sb(ctx, "rtotal", [P, TILES])
        inv = core.sb(ctx, "rinv", [P, TILES])
        loaded, logits_mm, step, shifted_ready, ex_ready = core.sems("ro", "loaded mm step shifted ex")
        with nc.Block() as block:
            @block.sync
            def _(sp):
                sp.dma_start(rw[:], d["router_w"]).then_inc(loaded, 16)
                sp.dma_start(rb[:], d["router_b"].partition_broadcast(P)).then_inc(loaded, 16)

            @block.tensor
            def _(pe):
                pe.wait_ge(loaded, 32)
                for t in range(TILES):
                    last = nc.tensor.matmul(core.bank[0][:, t * E:(t + 1) * E], core.xT[:, t * P:(t + 1) * P], rw[:],
                                            start=True, stop=True)
                last.then_inc(logits_mm, 1)

            @block.vector
            def _(dve):
                def wide(a):
                    return a.unsqueeze(2).broadcast_to([P, TILES, E])

                dve.wait_ge(logits_mm, 1)
                dve.wait_ge(loaded, 32)
                nc.vector.tensor_tensor(logit[:], core.bank[0][:, 0:TILES * E].rearrange("p (t e) -> p t e", e=E),
                                        rb[:].unsqueeze(1).broadcast_to([P, TILES, E]), ALU.add).then_inc(step, 1)
                dve.wait_ge(step, 1)
                nc.vector.tensor_reduce(top[:], logit[:], AX.X, ALU.max).then_inc(step, 1)
                dve.wait_ge(step, 2)
                nc.vector.tensor_tensor(shifted[:], logit[:], wide(top[:]), ALU.subtract).then_inc(shifted_ready, 1)
                dve.wait_ge(ex_ready, 1)
                nc.vector.tensor_reduce(total[:], ex[:], AX.X, ALU.add).then_inc(step, 1)
                dve.wait_ge(step, 3)
                nc.vector.reciprocal(inv[:], total[:]).then_inc(step, 1)
                dve.wait_ge(step, 4)
                nc.vector.tensor_tensor(core.route[:], ex[:], wide(inv[:]), ALU.mult)

            @block.scalar
            def _(act):
                act.wait_ge(shifted_ready, 1)
                nc.scalar.activation(ex[:], shifted[:], ACT.Exp).then_inc(ex_ready, 1)


def experts_encode(core, d):
    nc, bank = core.nc, core.bank
    with ExitStack() as ctx:
        w = core.sb(ctx, "ew", [P, ENC_W])
        cols = core.sb(ctx, "ecols", [P, COLS_W])
        rows = core.sb(ctx, "erows", [P, 2, 2, DM])
        qbs = core.sb(ctx, "eqbs", [P, KH])
        h1 = core.sb(ctx, "eh1", [P, 2, KH, S])
        h2 = core.sb(ctx, "eh2", [P, 2, BT, DM])
        hn = core.sb(ctx, "ehn", [P, 2, BT, DM])
        hT = core.sb(ctx, "ehT", [P, 2, KH, S])
        qk = core.sb(ctx, "eqk", [P, 2, KH, S])
        rest = core.sb(ctx, "erest", [P, 2, KH, S])
        parts = core.sb(ctx, "eparts", [P, 2, 2, 3, KH, S], BF16)
        vx = core.sb(ctx, "evx", [P, 2, BT, NH, DH + 1])
        stats = core.sb(ctx, "estats", [P, BT, 6])
        mv = core.sb(ctx, "emv", [P, BT, 2])
        var = core.sb(ctx, "evar", [P, BT])
        std = core.sb(ctx, "estd", [P, BT])
        rstd = core.sb(ctx, "erstd", [P, BT])
        (loaded, qbs_done, h1_mm, h1_kept, h2_mm, h2_kept, stats_done, mv_done, var_done, std_done, rstd_done, normed,
         hn_turned, hT_kept, qk_mm, q_kept, k_kept, v_mm, v_kept) = core.sems(
            "ee", "loaded qbs h1mm h1kept h2mm h2kept stats mv var std rstd normed hnturned hTkept qkmm qkept kkept "
                  "vmm vkept")
        part1, part2, part3, rested = (core.sems("ee", f"{n}q {n}k") for n in ("p1", "p2", "p3", "rest"))
        qk_out = [core.sems("ee", "qout0 qout1"), core.sems("ee", "kout0 kout1")]
        vx_out = core.sems("ee", "vout0 vout1")

        def weight(name, part, lo, n):
            width = {"ew1": DM, "ew2": DM, "qkv": 3 * DM}[name]
            at = ENC[name] + part * width + lo
            return w[:, at:at + n]

        def col(name, part):
            return cols[:, COLS[name] + part:COLS[name] + part + 1]

        with nc.Block() as block:
            @block.vector
            def _(dve):
                nc.vector.memset(vx[:], 1.0)
        with nc.Fori(0, E) as e:
            with nc.Block() as block:
                @block.sync
                def _(sp):
                    sp.dma_start(w[:], d["w_encode"][e]).then_inc(loaded, 16)
                    sp.dma_start(cols[:], d["cols"][e]).then_inc(loaded, 16)
                    for n, name in enumerate(("eb2", "vb")):
                        for twice in range(2):
                            sp.dma_start(rows[:, n, twice], d["rows"][e, ROWS[name]:ROWS[name] + DM]
                                         .partition_broadcast(P)).then_inc(loaded, 16)
                    for b in range(B):
                        for side in (1, 0):
                            sp.wait_ge(part3[side], b + 1)
                            for part in range(3):
                                sp.dma_start(d["qk"][e * B + b, side, part].rearrange("(c p) n -> p c n", p=P),
                                             parts[:, b % 2, side, part]).then_inc(qk_out[side][b % 2], 16)
                        sp.wait_ge(v_kept, 2 * b + 2)
                        sp.dma_start(d["vx"][e * B + b], vx[:, b % 2].rearrange("p t h r -> p (t h r)")
                                     ).then_inc(vx_out[b % 2], 16)
                    for parity in range(2):
                        for side in range(2):
                            sp.wait_ge(qk_out[side][parity], 2 * 48)
                        sp.wait_ge(vx_out[parity], 2 * 16)

                @block.tensor
                def _(pe):
                    def encode(b):
                        if b > 0:
                            pe.wait_ge(h1_kept, 2 * b)
                        for m in range(KH):
                            nc.tensor.matmul(bank[m][:], weight("ew1", 0, m * P, P), core.xT[:, b * S:(b + 1) * S],
                                             start=True, stop=True).then_inc(h1_mm, 1)
                        pe.wait_ge(h1_kept, 2 * b + 2)
                        for pair in range(2):
                            if b > 0:
                                pe.wait_ge(h2_kept, 2 * (b - 1) + pair + 1)
                            for t in (2 * pair, 2 * pair + 1):
                                for k in range(KH):
                                    last = nc.tensor.matmul(bank[2 + pair][:, t % 2 * DM:(t % 2 + 1) * DM],
                                                            h1[:, b % 2, k, t * P:(t + 1) * P],
                                                            weight("ew2", k, 0, DM), start=k == 0, stop=k == KH - 1)
                            last.then_inc(h2_mm, 1)

                    pe.wait_ge(loaded, 6 * 16)
                    encode(0)
                    for b in range(B):
                        if b < B - 1:
                            encode(b + 1)
                        if b > 0:
                            pe.wait_ge(v_kept, 2 * b)
                        for t in range(BT):
                            pe.wait_ge(normed, BT * b + t + 1)
                            for k in range(KH):
                                last = nc.tensor.transpose(bank[4 + k][:, t * P:(t + 1) * P],
                                                           hn[:, b % 2, t, k * P:(k + 1) * P], core.ident[:])
                        last.then_inc(hn_turned, 1)
                        pe.wait_ge(hT_kept, 2 * b + 2)
                        for m in range(4):
                            side, c = 1 - m // 2, m % 2
                            if side == 0:
                                pe.wait_ge(k_kept, 2 * b + c + 1)
                            elif b > 0:
                                pe.wait_ge(q_kept, 2 * b - 1 + c)
                            for k in range(KH):
                                last = nc.tensor.matmul(bank[6 + c][:], weight("qkv", k, side * DM + c * P, P),
                                                        hT[:, b % 2, k], start=k == 0, stop=k == KH - 1)
                            last.then_inc(qk_mm, 1)
                        for pair in range(2):
                            for t in (2 * pair, 2 * pair + 1):
                                for k in range(KH):
                                    last = nc.tensor.matmul(bank[4 + pair][:, t % 2 * DM:(t % 2 + 1) * DM],
                                                            hT[:, b % 2, k, t * P:(t + 1) * P],
                                                            weight("qkv", k, 2 * DM, DM), start=k == 0, stop=k == KH - 1)
                            last.then_inc(v_mm, 1)

                @block.vector
                def _(dve):
                    def norm(b):
                        for pair in range(2):
                            dve.wait_ge(h2_mm, 2 * b + pair + 1)
                            nc.vector.tensor_tensor(h2[:, b % 2, 2 * pair:2 * pair + 2],
                                                    bank[2 + pair][:].rearrange("p (t n) -> p t n", t=2), rows[:, 0],
                                                    ALU.add).then_inc(h2_kept, 1)
                        for t in range(BT):
                            dve.wait_ge(h2_kept, 2 * b + t // 2 + 1)
                            nc.vector.bn_stats(stats[:, t], h2[:, b % 2, t]).then_inc(stats_done, 1)
                        for t in range(BT):
                            dve.wait_ge(stats_done, BT * b + t + 1)
                            nc.vector.bn_aggr(mv[:, t], stats[:, t]).then_inc(mv_done, 1)
                        dve.wait_ge(mv_done, BT * (b + 1))
                        nc.vector.tensor_scalar(var[:], mv[:, :, 1], EPS, None, ALU.add).then_inc(var_done, 1)
                        dve.wait_ge(std_done, b + 1)
                        nc.vector.reciprocal(rstd[:], std[:]).then_inc(rstd_done, 1)
                        dve.wait_ge(rstd_done, b + 1)
                        for t in range(BT):
                            nc.vector.tensor_scalar(hn[:, b % 2, t], h2[:, b % 2, t], mv[:, t, 0:1], rstd[:, t:t + 1],
                                                    ALU.subtract, ALU.mult).then_inc(normed, 1)

                    dve.wait_ge(loaded, 6 * 16)
                    nc.vector.tensor_scalar(qbs[:], cols[:, COLS["qb"]:COLS["qb"] + KH], float(DH) ** -0.5, None,
                                            ALU.mult).then_inc(qbs_done, 1)
                    norm(0)
                    for b in range(B):
                        if b < B - 1:
                            norm(b + 1)
                        for c in range(KH):
                            dve.wait_ge(qk_mm, 4 * b + c + 1)
                            nc.vector.tensor_scalar(qk[:, 1, c], bank[6 + c][:], col("kb", c), None,
                                                    ALU.add).then_inc(k_kept, 1)
                        if b >= 2:
                            dve.wait_ge(vx_out[b % 2], 16)
                        for pair in range(2):
                            dve.wait_ge(v_mm, 2 * b + pair + 1)
                            nc.vector.tensor_tensor(
                                vx[:, b % 2, 2 * pair:2 * pair + 2, :, 0:DH].rearrange("p t h r -> p (t h) r"),
                                bank[4 + pair][:].rearrange("p (t r) -> p t r", r=DH),
                                rows[:, 1].rearrange("p t (h r) -> p (t h) r", r=DH), ALU.add).then_inc(v_kept, 1)
                        for side in (1, 0):
                            dve.wait_ge(part1[side], b + 1)
                            nc.vector.tensor_tensor(rest[:, side], qk[:, side], parts[:, b % 2, side, 0], ALU.subtract
                                                    ).then_inc(rested[side], 1)
                        for side in (1, 0):
                            dve.wait_ge(part2[side], b + 1)
                            nc.vector.tensor_tensor(parts[:, b % 2, side, 2], rest[:, side], parts[:, b % 2, side, 1],
                                                    ALU.subtract).then_inc(part3[side], 1)

                @block.scalar
                def _(act):
                    def relu(b):
                        for m in range(KH):
                            act.wait_ge(h1_mm, 2 * b + m + 1)
                            nc.scalar.activation(h1[:, b % 2, m], bank[m][:], ACT.Relu, bias=col("eb1", m)
                                                 ).then_inc(h1_kept, 1)

                    def root(b):
                        act.wait_ge(var_done, b + 1)
                        nc.scalar.activation(std[:], var[:], ACT.Sqrt).then_inc(std_done, 1)

                    act.wait_ge(loaded, 6 * 16)
                    act.wait_ge(qbs_done, 1)
                    relu(0)
                    root(0)
                    for b in range(B):
                        if b < B - 1:
                            relu(b + 1)
                        act.wait_ge(hn_turned, b + 1)
                        for k in range(KH):
                            nc.scalar.activation(hT[:, b % 2, k], bank[4 + k][:], ACT.Identity, scale=col("eg", k),
                                                 bias=col("ebeta", k)).then_inc(hT_kept, 1)
                        if b < B - 1:
                            root(b + 1)
                        for c in range(KH):
                            act.wait_ge(qk_mm, 4 * b + KH + c + 1)
                            if b > 0:
                                act.wait_ge(rested[0], b)
                            nc.scalar.activation(qk[:, 0, c], bank[6 + c][:], ACT.Identity, scale=float(DH) ** -0.5,
                                                 bias=qbs[:, c:c + 1]).then_inc(q_kept, 1)
                        for side in (1, 0):
                            act.wait_ge(*((q_kept, k_kept)[side], 2 * b + 2))
                            if b >= 2:
                                act.wait_ge(qk_out[side][b % 2], 48)
                            nc.scalar.activation(parts[:, b % 2, side, 0], qk[:, side], ACT.Copy).then_inc(part1[side], 1)
                        for side in (1, 0):
                            act.wait_ge(rested[side], b + 1)
                            nc.scalar.activation(parts[:, b % 2, side, 1], rest[:, side], ACT.Copy
                                                 ).then_inc(part2[side], 1)
            clear_signals(nc, [
                loaded, qbs_done, h1_mm, h1_kept, h2_mm, h2_kept, stats_done, mv_done, var_done, std_done, rstd_done,
                normed, hn_turned, hT_kept, qk_mm, q_kept, k_kept, v_mm, v_kept] + part1 + part2 + part3 + rested
                + qk_out[0] + qk_out[1] + vx_out)


PAIRS = ((0, 0), (0, 1), (0, 2), (1, 0), (1, 1), (2, 0))
KROWS = len(PAIRS) * DH
RING = 6


def experts_attend(core, d):
    nc, bank = core.nc, core.bank
    with ExitStack() as ctx:
        w = core.sb(ctx, "bw", [P, ATT_W])
        cols = core.sb(ctx, "bcols", [P, COLS_W])
        lb = core.sb(ctx, "blb", [P, 2 * G4])
        qp = core.sb(ctx, "bqp", [KROWS, NH, S], BF16)
        kp = core.sb(ctx, "bkp", [KROWS, NH, S], BF16)
        vx = core.sb(ctx, "bvx", [P, BT, NH, DH + 1])
        p = core.sb(ctx, "bp", [P, 2, BT, S])
        pT = core.sb(ctx, "bpT", [P, RING, BT, S])
        negmax = core.sb(ctx, "bnegmax", [P, NH, BT])
        o = core.sb(ctx, "bo", [P, 4, S])
        inv = core.sb(ctx, "binv", [P, BT, NH])
        on = core.sb(ctx, "bon", [P, BT, NH, DH])
        oT = core.sb(ctx, "boT", [P, KH, S])
        aT = core.sb(ctx, "baT", [P, KH, S])
        zs = core.sb(ctx, "bzs", [P, 4, G4])
        (loaded, filled, scored, maxed, exped, turned, kept_v, kept_a, valued, o_kept, o_turned, inverted, on_done,
         on_turned, oT_kept, a_mm, a_kept, z_mm, z_kept) = core.sems(
            "ba", "loaded filled scored maxed exped turned keptv kepta valued okept oturned inverted on onturned "
                  "oTkept amm akept zmm zkept")
        qk_in = core.sems("ba", "qkin0 qkin1")
        (vx_in,) = core.sems("ba", "vxin")
        z_stored = core.sems("ba", "zstored0 zstored1 zstored2 zstored3")

        def load_heads(sp, slab, half):
            heads = slice(half * NH // 2, (half + 1) * NH // 2)
            for side, dst in ((0, qp), (1, kp)):
                for n, pair in enumerate(PAIRS):
                    src = d["qk"][slab, side, pair[side]].rearrange("(h r) n -> r h n", r=DH)
                    sp.dma_start(dst[n * DH:(n + 1) * DH, heads], src[:, heads]).then_inc(qk_in[half], 16)

        HEADS_IN = 2 * len(PAIRS) * 16

        def product(pe, n):
            t, q = divmod(n, 4)
            if n > 0:
                pe.wait_ge(z_kept, n)
            for k in range(KH):
                at = ATT["wi"] + (q // 2 * KH + k) * G4 + q % 2 * 512
                last = nc.tensor.matmul(bank[7][:], aT[:, k, t * P:(t + 1) * P], w[:, at:at + 512],
                                        start=k == 0, stop=k == KH - 1)
            last.then_inc(z_mm, 1)

        def keep_product(dve, n):
            dve.wait_ge(z_mm, n + 1)
            if n >= 8 and n % 2 == 0:
                dve.wait_ge(z_stored[n // 2 % 4], 16 * (n // 8))
            nc.vector.tensor_tensor(zs[:, (n // 2) % 4, n % 2 * 512:(n % 2 + 1) * 512], bank[7][:],
                                    lb[:, n % 4 * 512:(n % 4 + 1) * 512], ALU.add).then_inc(z_kept, 1)

        def store_product(sp, n, e, b):
            t, way = divmod(n, 2)
            sp.wait_ge(z_kept, 2 * n + 2)
            sp.dma_start(d["zx"][way, e, b, t * P:(t + 1) * P], zs[:, n % 4]).then_inc(z_stored[n % 4], 16)

        def attend(e, b, products):
            with nc.Block() as block:
                @block.sync
                def _(sp):
                    load_heads(sp, e * B + b, 1)
                    sp.dma_start(vx[:].rearrange("p t h r -> p (t h r)"), d["vx"][e * B + b]).then_inc(vx_in, 16)
                    if products:
                        for n in range(4):
                            store_product(sp, n, e, b - 1)
                    sp.wait_ge(scored, BT * NH // 2)
                    load_heads(sp, e * B + b + 1, 0)
                    if products:
                        for n in range(4, 8):
                            store_product(sp, n, e, b - 1)
                        for slot in z_stored:
                            sp.wait_ge(slot, 2 * 16)
                    sp.wait_ge(qk_in[0], HEADS_IN)

                @block.tensor
                def _(pe):
                    def score(h, qt):
                        if h == NH // 2 and qt == 0:
                            pe.wait_ge(qk_in[1], HEADS_IN)
                        if h > 0:
                            pe.wait_ge(exped, BT * (h - 1) + qt + 1)
                        nc.tensor.matmul(bank[qt][:], qp[:, h, qt * P:(qt + 1) * P], kp[:, h], start=True,
                                         stop=True).then_inc(scored, 1)

                    def turn(h, kt):
                        if kt == 0:
                            pe.wait_ge(exped, BT * (h + 1))
                        if 2 * h + kt // 2 > 0:
                            pe.wait_ge((kept_v, kept_a)[kt % 2], 2 * h + kt // 2)
                        for qt in range(BT):
                            last = nc.tensor.transpose(bank[4 + kt % 2][:, qt * P:(qt + 1) * P],
                                                       p[:, h % 2, qt, kt * P:(kt + 1) * P], core.ident[:])
                        last.then_inc(turned, 1)

                    def values(g):
                        if g == 0:
                            pe.wait_ge(vx_in, 16)
                        else:
                            pe.wait_ge(o_kept, g)
                        pe.wait_ge(kept_v, 8 * (g + 1))
                        pe.wait_ge(kept_a, 8 * (g + 1))
                        for kt in range(BT):
                            for c in range(4):
                                h = 4 * g + c
                                last = nc.tensor.matmul(bank[6][32 * c:32 * c + DH + 1, :], vx[:, kt, h],
                                                        pT[:, h % RING, kt], start=kt == 0, stop=kt == BT - 1)
                        last.then_inc(valued, 1)

                    for h in range(NH + 2):
                        if h < NH:
                            score(h, 0)
                            score(h, 1)
                        if 0 < h <= NH:
                            turn(h - 1, 0)
                            turn(h - 1, 1)
                        if h < NH:
                            score(h, 2)
                        if h > 1 and h % 4 == 1:
                            values(h // 4 - 1)
                        if 0 < h <= NH:
                            turn(h - 1, 2)
                        if h < NH:
                            score(h, 3)
                        if 0 < h <= NH:
                            turn(h - 1, 3)
                        if products and h < NH:
                            product(pe, h)
                    for qt in range(BT):
                        pe.wait_ge(o_kept, 4)
                        for g in range(4):
                            last = nc.tensor.transpose(bank[qt][:, g * P:(g + 1) * P], o[:, g, qt * P:(qt + 1) * P],
                                                       core.ident[:])
                        last.then_inc(o_turned, 1)
                    for qt in range(BT):
                        pe.wait_ge(on_done, qt + 1)
                        for k in range(KH):
                            last = nc.tensor.transpose(
                                bank[4 + k][:, qt * P:(qt + 1) * P],
                                on[:, qt, k * NH // KH:(k + 1) * NH // KH].rearrange("p h r -> p (h r)"),
                                core.ident[:])
                    last.then_inc(on_turned, 1)
                    pe.wait_ge(oT_kept, KH)
                    if products:
                        pe.wait_ge(z_kept, NH)
                    for m in range(KH):
                        for k in range(KH):
                            at = ATT["aow"] + k * DM + m * P
                            last = nc.tensor.matmul(bank[6 + m][:], w[:, at:at + P], oT[:, k], start=k == 0,
                                                    stop=k == KH - 1)
                        last.then_inc(a_mm, 1)

                @block.vector
                def _(dve):
                    def largest(h, qt):
                        dve.wait_ge(scored, BT * h + qt + 1)
                        nc.vector.tensor_reduce(negmax[:, h, qt:qt + 1], bank[qt][:], AX.X, ALU.max,
                                                negate=True).then_inc(maxed, 1)

                    def keep(h, kt):
                        dve.wait_ge(turned, BT * h + kt + 1)
                        if h >= RING:
                            dve.wait_ge(valued, (h - RING) // 4 + 1)
                        nc.vector.tensor_copy(pT[:, h % RING, kt], bank[4 + kt % 2][:]).then_inc(kept_v, 1)

                    for h in range(NH + 1):
                        if h < NH:
                            largest(h, 0)
                            largest(h, 1)
                        if products and h > 0:
                            keep_product(dve, h - 1)
                        if h > 0:
                            keep(h - 1, 0)
                        if h < NH:
                            largest(h, 2)
                        if h > 0:
                            keep(h - 1, 2)
                        if h < NH:
                            largest(h, 3)
                    for qt in range(BT):
                        heads = bank[qt][:].rearrange("p (h r) -> p h r", r=32)
                        dve.wait_ge(o_turned, qt + 1)
                        nc.vector.reciprocal(inv[:, qt], heads[:, :, DH]).then_inc(inverted, 1)
                        dve.wait_ge(inverted, qt + 1)
                        nc.vector.tensor_tensor(on[:, qt], heads[:, :, 0:DH],
                                                inv[:, qt].unsqueeze(2).broadcast_to([P, NH, DH]), ALU.mult
                                                ).then_inc(on_done, 1)

                @block.scalar
                def _(act):
                    def exponent(h, qt):
                        act.wait_ge(maxed, BT * h + qt + 1)
                        if h >= 2 and qt == 0:
                            act.wait_ge(turned, BT * (h - 1))
                        nc.scalar.activation(p[:, h % 2, qt], bank[qt][:], ACT.Exp, bias=negmax[:, h, qt:qt + 1]
                                             ).then_inc(exped, 1)

                    def keep(h, kt):
                        act.wait_ge(turned, BT * h + kt + 1)
                        if h >= RING:
                            act.wait_ge(valued, (h - RING) // 4 + 1)
                        nc.scalar.activation(pT[:, h % RING, kt], bank[4 + kt % 2][:], ACT.Copy).then_inc(kept_a, 1)

                    for h in range(NH + 2):
                        if h < NH:
                            exponent(h, 0)
                            exponent(h, 1)
                        if 0 < h <= NH:
                            keep(h - 1, 1)
                        if h < NH:
                            exponent(h, 2)
                        if 0 < h <= NH:
                            keep(h - 1, 3)
                        if h > 1 and h % 4 == 1:
                            g = h // 4 - 1
                            act.wait_ge(valued, g + 1)
                            nc.scalar.activation(o[:, g], bank[6][:], ACT.Copy).then_inc(o_kept, 1)
                        if h < NH:
                            exponent(h, 3)
                    act.wait_ge(on_turned, 1)
                    for k in range(KH):
                        nc.scalar.activation(oT[:, k], bank[4 + k][:], ACT.Copy).then_inc(oT_kept, 1)
                    for m in range(KH):
                        act.wait_ge(a_mm, m + 1)
                        nc.scalar.activation(aT[:, m], bank[6 + m][:], ACT.Identity,
                                             bias=cols[:, COLS["aob"] + m:COLS["aob"] + m + 1]).then_inc(a_kept, 1)
            clear_signals(nc, [scored, maxed, exped, turned, kept_v, kept_a, valued, o_kept, o_turned, inverted, on_done,
                               on_turned, oT_kept, a_mm, a_kept, z_mm, z_kept, vx_in] + qk_in + z_stored)

        with nc.Block() as block:
            @block.sync
            def _(sp):
                sp.dma_start(d["qk"][E * B], d["qk"][0]).then_inc(filled, 16)
                load_heads(sp, 0, 0)
                sp.wait_ge(qk_in[0], HEADS_IN)
                sp.wait_ge(filled, 16)

            @block.vector
            def _(dve):
                nc.vector.memset(bank[6][:], 0.0)
        clear_signals(nc, qk_in)
        with nc.Fori(0, E) as e:
            with nc.Block() as block:
                @block.sync
                def _(sp):
                    sp.dma_start(w[:], d["w_attend"][e]).then_inc(loaded, 16)
                    sp.dma_start(cols[:], d["cols"][e]).then_inc(loaded, 16)
                    sp.dma_start(lb[:], d["rows"][e, ROWS["lb"]:ROWS["lb"] + 2 * G4].partition_broadcast(P)
                                 ).then_inc(loaded, 16)
                    sp.wait_ge(loaded, 48)
            attend(e, 0, False)
            with nc.Fori(1, B) as b:
                attend(e, b, True)
            with nc.Block() as block:
                @block.tensor
                def _(pe):
                    for n in range(NH):
                        product(pe, n)

                @block.vector
                def _(dve):
                    for n in range(NH):
                        keep_product(dve, n)

                @block.sync
                def _(sp):
                    for n in range(8):
                        store_product(sp, n, e, B - 1)
                    for slot in z_stored:
                        sp.wait_ge(slot, 2 * 16)
            clear_signals(nc, [loaded, z_mm, z_kept] + z_stored)


STEPS = 4
PER_TURN = 2 * STEPS


def recurrence(core, d):
    nc, bank = core.nc, core.bank
    turns = S // PER_TURN
    with ExitStack() as ctx:
        wh = core.sb(ctx, "lwh", [P, 2, E, KH, G4])
        zx = core.sb(ctx, "lzx", [P, 2, 2, STEPS, G4])
        hs = core.sb(ctx, "lhs", [P, 2, 2, STEPS, DM])
        z = core.sb(ctx, "lz", [P, 2, KH, 4, P])
        gate = core.sb(ctx, "lgate", [P, 2, KH, 3, P])
        gc = core.sb(ctx, "lgc", [P, 2, KH, 2, P])
        prod = core.sb(ctx, "lprod", [P, 2, KH, 2, P])
        tc = core.sb(ctx, "ltc", [P, 2, KH, P])
        hT = core.sb(ctx, "lhT", [P, 2, KH, E, B])
        (loaded, cleared) = core.sems("ls", "loaded cleared")

        def pair(name):
            return core.sems("ls", f"{name}0 {name}1")

        made, added, gated, celled, tanhed, ready, turned, kept = (
            pair(n) for n in ("made", "added", "gated", "celled", "tanhed", "ready", "turned", "kept"))
        multiplied = pair("multiplied")
        zx_in = [pair("zxin0"), pair("zxin1")]
        hs_out = [pair("hsout0"), pair("hsout1")]

        AHEAD = KH

        def z_bank(way, j):
            return bank[2 * way + j]

        def turn_bank(way, j):
            return bank[4 + 2 * way + j]

        def rows_of(e):
            return slice(32 * e, 32 * e + B)

        def first_time(way, turn, buf):
            n = 2 * turn + buf
            return n * STEPS if way == 0 else n * -STEPS + (S - STEPS)

        def at(way, i):
            return i if way == 0 else STEPS - 1 - i

        def load_zx(sp, way, turn, buf):
            for e in range(E):
                sp.dma_start(zx[rows_of(e), way, buf], d["zx"][way, e, :, bass.ds(first_time(way, turn, buf), STEPS)]
                             ).then_inc(zx_in[way][buf], 16)

        with nc.Block() as block:
            @block.sync
            def _(sp):
                sp.dma_start(wh[:], d["wh"]).then_inc(loaded, 16)
                sp.wait_ge(cleared, 1)
                for buf in range(2):
                    for way in range(2):
                        load_zx(sp, way, 0, buf)
                sp.wait_ge(loaded, 16)

            @block.vector
            def _(dve):
                nc.vector.memset(zx[:], 0.0).then_inc(cleared, 1)
                nc.vector.memset(hT[:], 0.0)
                nc.vector.memset(gc[:], 0.0)
                nc.vector.memset(hs[:], 0.0)
                for n in range(4):
                    nc.vector.memset(bank[n][:], 0.0)
                for way in range(2):
                    dve.sem_inc(added[way], AHEAD)
                    dve.sem_inc(ready[way], AHEAD)
                    for buf in range(2):
                        dve.sem_inc(hs_out[way][buf], 1)

        with nc.Block() as block:
            @block.tensor
            def _(pe):
                def products(way, done, k, j):
                    if j == 0:
                        pe.wait_ge(kept[way], done + k + 1)
                    if k == 0:
                        pe.wait_ge(added[way], done + j + 1)
                    for e in range(E):
                        last = nc.tensor.matmul(z_bank(way, j)[rows_of(e), :], hT[:, way, k, e],
                                                wh[:, way, e, k, j * 512:(j + 1) * 512],
                                                start=k == 0, stop=k == KH - 1)
                    if k == KH - 1:
                        last.then_inc(made[way], 1)

                def transpose(way, i, done, j):
                    pe.wait_ge(ready[way], done + AHEAD + j + 1)
                    nc.tensor.transpose(turn_bank(way, j)[:, 0:P],
                                        hs[:, way, i // STEPS, at(way, i % STEPS), j * P:(j + 1) * P],
                                        core.ident[:]).then_inc(turned[way], 1)

                transpose(0, PER_TURN - 1, -AHEAD, 0)
                with pe.Fori(0, turns) as turn:
                    for i in range(PER_TURN):
                        for way in range(2):
                            done = 2 * PER_TURN * turn + 2 * i
                            products(way, done, 0, 0)
                            transpose(way, (i - 1) % PER_TURN, done - AHEAD, 1)
                            products(way, done, 0, 1)
                            products(way, done, 1, 0)
                            if way == 0:
                                transpose(1, (i - 1) % PER_TURN, done - AHEAD, 0)
                            else:
                                transpose(0, i, done, 0)
                            products(way, done, 1, 1)
                transpose(0, PER_TURN - 1, 2 * S - 2, 1)

            @block.vector
            def _(dve):
                def keep(way, done, j):
                    dve.wait_ge(turned[way], done + AHEAD + j + 1)
                    nc.vector.tensor_copy(hT[:, way, j], turn_bank(way, j)[:, 0:P].rearrange(
                        "p (e b) -> p e b", e=E)[:, :, 0:B]).then_inc(kept[way], 1)

                for j in range(KH):
                    keep(0, -AHEAD, j)
                with dve.Fori(0, turns) as turn:
                    for i in range(PER_TURN):
                        buf, done = i // STEPS, 2 * PER_TURN * turn + 2 * i
                        for way in range(2):
                            here = at(way, i % STEPS)
                            if i % STEPS == 0:
                                dve.wait_ge(zx_in[way][buf], 64 * turn + 64)
                                dve.wait_ge(hs_out[way][buf], 64 * turn + 1)

                            def add(j):
                                dve.wait_ge(made[way], done + j + 1)
                                nc.vector.tensor_tensor(z[:, way, j].rearrange("p g n -> p (g n)"), z_bank(way, j)[:],
                                                        zx[:, way, buf, here, j * 512:(j + 1) * 512],
                                                        ALU.add).then_inc(added[way], 1)

                            def cell(j):
                                dve.wait_ge(gated[way], done + j + 1)
                                nc.vector.tensor_tensor(prod[:, way, j], gate[:, way, j, 0:2], gc[:, way, j],
                                                        ALU.mult).then_inc(multiplied[way], 1)
                                dve.wait_ge(multiplied[way], done + j + 1)
                                nc.vector.tensor_tensor(gc[:, way, j, 1], prod[:, way, j, 0], prod[:, way, j, 1],
                                                        ALU.add).then_inc(celled[way], 1)

                            def state(j):
                                dve.wait_ge(tanhed[way], done + j + 1)
                                nc.vector.tensor_tensor(hs[:, way, buf, here, j * P:(j + 1) * P], gate[:, way, j, 2],
                                                        tc[:, way, j], ALU.mult).then_inc(ready[way], 1)

                            other = done - AHEAD if way == 0 else done
                            keep(1 - way, other, 0)
                            add(0)
                            add(1)
                            cell(0)
                            keep(1 - way, other, 1)
                            cell(1)
                            state(0)
                            state(1)

            @block.scalar
            def _(act):
                with act.Fori(0, turns) as turn:
                    for i in range(PER_TURN):
                        done = 2 * PER_TURN * turn + 2 * i
                        for way in range(2):
                            for j in range(KH):
                                act.wait_ge(added[way], AHEAD + done + j + 1)
                                nc.scalar.activation(gate[:, way, j], z[:, way, j, 0:3], ACT.Sigmoid)
                                nc.scalar.activation(gc[:, way, j, 0], z[:, way, j, 3], ACT.Tanh).then_inc(gated[way], 1)
                            for j in range(KH):
                                act.wait_ge(celled[way], done + j + 1)
                                nc.scalar.activation(tc[:, way, j], gc[:, way, j, 1], ACT.Tanh).then_inc(tanhed[way], 1)

            @block.sync
            def _(sp):
                def store_and_load(turn, more):
                    for buf in range(2):
                        for way in range(2):
                            steps = 2 * PER_TURN * turn + 2 * STEPS * (buf + 1)
                            sp.wait_ge(ready[way], steps + AHEAD)
                            for e in range(E):
                                sp.dma_start(d["hs"][way, e, :, bass.ds(first_time(way, turn, buf), STEPS)],
                                             hs[rows_of(e), way, buf]).then_inc(hs_out[way][buf], 16)
                            if more:
                                load_zx(sp, way, turn + 1, buf)

                with sp.Fori(0, turns - 1) as turn:
                    store_and_load(turn, True)
                store_and_load(turns - 1, False)
                for buf in range(2):
                    for way in range(2):
                        sp.wait_ge(hs_out[way][buf], 64 * turns + 1)


def experts_after(core, d):
    nc, bank = core.nc, core.bank
    with ExitStack() as ctx:
        w = core.sb(ctx, "cw", [P, POST_W])
        cols = core.sb(ctx, "ccols", [P, COLS_W])
        rows = core.sb(ctx, "crows", [P, ROWS_W])
        mem = core.sb(ctx, "cmem", [P, 2, BT, DM])
        memT = core.sb(ctx, "cmemT", [P, 4, S])
        hid = core.sb(ctx, "chid", [P, 4, S])
        gt = core.sb(ctx, "cgt", [P, 4, S])
        g = core.sb(ctx, "cg", [P, KH, S])
        d1 = core.sb(ctx, "cd1", [P, KH, S])
        y = core.sb(ctx, "cy", [P, BT, D])
        yn = core.sb(ctx, "cyn", [P, BT, D])
        yg = core.sb(ctx, "cyg", [P, BT, D])
        yb = core.sb(ctx, "cyb", [P, BT, D])
        wt = core.sb(ctx, "cwt", [P, BT])
        stats = core.sb(ctx, "cstats", [P, BT, 6])
        mv = core.sb(ctx, "cmv", [P, BT, 2])
        var = core.sb(ctx, "cvar", [P, BT])
        std = core.sb(ctx, "cstd", [P, BT])
        rstd = core.sb(ctx, "crstd", [P, BT])
        (loaded, mem_turned, memT_kept, hid_mm, hid_kept, gate_mm, gate_kept, product, d1_mm, d1_kept, y_mm, y_kept,
         stats_done, mv_done, var_done, std_done, rstd_done, normed, gained, shifted) = core.sems(
            "ea", "loaded memturned memTkept hidmm hidkept gatemm gatekept product d1mm d1kept ymm ykept stats mv var "
                  "std rstd normed gained shifted")
        mem_in = core.sems("ea", "memin0 memin1")

        def weight(name, part, m):
            width = D if name == "dw2" else DM
            at = POST[name] + part * width + m * P
            return w[:, at:at + P]

        def col(name, part):
            return cols[:, COLS[name] + part:COLS[name] + part + 1]

        def row(name):
            return rows[:, ROWS[name]:ROWS[name] + D].unsqueeze(1).broadcast_to([P, BT, D])

        with nc.Fori(0, E) as e:
            with nc.Block() as block:
                @block.sync
                def _(sp):
                    sp.dma_start(w[:], d["w_after"][e]).then_inc(loaded, 16)
                    sp.dma_start(cols[:], d["cols"][e]).then_inc(loaded, 16)
                    sp.dma_start(rows[:], d["rows"][e].partition_broadcast(P)).then_inc(loaded, 16)
                    sp.wait_ge(loaded, 48)
            with nc.Fori(0, B) as b:
                with nc.Block() as block:
                    @block.sync
                    def _(sp):
                        for way in range(2):
                            sp.dma_start(mem[:, way], d["hs"][way, e, b].rearrange("(t p) u -> p t u", p=P)
                                         ).then_inc(mem_in[way], 16)

                    @block.tensor
                    def _(pe):
                        for k in range(4):
                            pe.wait_ge(mem_in[k // 2], 16)
                            for t in range(BT):
                                last = nc.tensor.transpose(bank[k][:, t * P:(t + 1) * P],
                                                           mem[:, k // 2, t, k % 2 * P:(k % 2 + 1) * P], core.ident[:])
                            last.then_inc(mem_turned, 1)
                        pe.wait_ge(memT_kept, 4)
                        for m in range(4):
                            for k in range(4):
                                last = nc.tensor.matmul(bank[4 + m][:], weight(("sw1", "tw1")[m // 2], k, m % 2),
                                                        memT[:, k], start=k == 0, stop=k == 3)
                            last.then_inc(hid_mm, 1)
                        for m in range(4):
                            for k in range(KH):
                                pe.wait_ge(hid_kept, m // 2 * 2 + k + 1)
                                last = nc.tensor.matmul(bank[m][:], weight(("sw2", "tw2")[m // 2], k, m % 2),
                                                        hid[:, m // 2 * 2 + k], start=k == 0, stop=k == KH - 1)
                            last.then_inc(gate_mm, 1)
                        pe.wait_ge(product, KH)
                        for m in range(KH):
                            for k in range(KH):
                                last = nc.tensor.matmul(bank[4 + m][:], weight("dw1", k, m), g[:, k], start=k == 0,
                                                        stop=k == KH - 1)
                            last.then_inc(d1_mm, 1)
                        pe.wait_ge(d1_kept, KH)
                        for t in range(BT):
                            for k in range(KH):
                                last = nc.tensor.matmul(bank[t][:, 0:D], d1[:, k, t * P:(t + 1) * P],
                                                        weight("dw2", k, 0), start=k == 0, stop=k == KH - 1)
                            last.then_inc(y_mm, 1)

                    @block.scalar
                    def _(act):
                        for k in (1, 3):
                            act.wait_ge(mem_turned, k + 1)
                            nc.scalar.activation(memT[:, k], bank[k][:], ACT.Copy).then_inc(memT_kept, 1)
                        for m in range(4):
                            act.wait_ge(hid_mm, m + 1)
                            nc.scalar.activation(hid[:, m], bank[4 + m][:], ACT.Relu,
                                                 bias=col(("sb1", "tb1")[m // 2], m % 2)).then_inc(hid_kept, 1)
                        for m in range(4):
                            act.wait_ge(gate_mm, m + 1)
                            nc.scalar.activation(gt[:, m], bank[m][:], (ACT.Sigmoid, ACT.Tanh)[m // 2],
                                                 bias=col(("sb2", "tb2")[m // 2], m % 2)).then_inc(gate_kept, 1)
                        for m in range(KH):
                            act.wait_ge(d1_mm, m + 1)
                            nc.scalar.activation(d1[:, m], bank[4 + m][:], ACT.Relu, bias=col("db1", m)).then_inc(d1_kept, 1)
                        act.wait_ge(var_done, 1)
                        nc.scalar.activation(std[:], var[:], ACT.Sqrt).then_inc(std_done, 1)

                    @block.vector
                    def _(dve):
                        nc.vector.tensor_copy(wt[:], core.route[:, bass.ds(b * BT, BT), e])
                        for k in (0, 2):
                            dve.wait_ge(mem_turned, k + 1)
                            nc.vector.tensor_copy(memT[:, k], bank[k][:]).then_inc(memT_kept, 1)
                        for m in range(KH):
                            dve.wait_ge(gate_kept, KH + m + 1)
                            nc.vector.tensor_tensor(g[:, m], gt[:, m], gt[:, KH + m], ALU.mult).then_inc(product, 1)
                        for t in range(BT):
                            dve.wait_ge(y_mm, t + 1)
                            nc.vector.tensor_tensor(y[:, t], bank[t][:, 0:D], rows[:, ROWS["db2"]:ROWS["db2"] + D],
                                                    ALU.add).then_inc(y_kept, 1)
                            dve.wait_ge(y_kept, t + 1)
                            nc.vector.bn_stats(stats[:, t], y[:, t]).then_inc(stats_done, 1)
                            dve.wait_ge(stats_done, t + 1)
                            nc.vector.bn_aggr(mv[:, t], stats[:, t]).then_inc(mv_done, 1)
                        dve.wait_ge(mv_done, BT)
                        nc.vector.tensor_scalar(var[:], mv[:, :, 1], EPS, None, ALU.add).then_inc(var_done, 1)
                        dve.wait_ge(std_done, 1)
                        nc.vector.reciprocal(rstd[:], std[:]).then_inc(rstd_done, 1)
                        dve.wait_ge(rstd_done, 1)
                        for t in range(BT):
                            nc.vector.tensor_scalar(yn[:, t], y[:, t], mv[:, t, 0:1], rstd[:, t:t + 1],
                                                    ALU.subtract, ALU.mult).then_inc(normed, 1)
                        dve.wait_ge(normed, BT)
                        nc.vector.tensor_tensor(yg[:], yn[:], row("dg"), ALU.mult).then_inc(gained, 1)
                        dve.wait_ge(gained, 1)
                        nc.vector.tensor_tensor(yb[:], yg[:], row("dbeta"), ALU.add).then_inc(shifted, 1)
                        dve.wait_ge(shifted, 1)
                        for t in range(BT):
                            ht = core.h[:, bass.ds(b * BT + t, 1)].rearrange("p t d -> p (t d)")
                            nc.vector.scalar_tensor_tensor(out=ht, in0=yb[:, t], scalar=wt[:, t:t + 1], in1=ht,
                                                           op0=ALU.mult, op1=ALU.add)
                clear_signals(nc, mem_in + [mem_turned, memT_kept, hid_mm, hid_kept, gate_mm, gate_kept, product, d1_mm,
                                            d1_kept, y_mm, y_kept, stats_done, mv_done, var_done, std_done, rstd_done,
                                            normed, gained, shifted])
            clear_signals(nc, [loaded])


def state_space(core, d):
    nc, bank = core.nc, core.bank
    PAIRS = B // 2
    with ExitStack() as ctx:
        bT = core.sb(ctx, "sbT", [P, NST])
        cT = core.sb(ctx, "scT", [P, D])
        alog = core.sb(ctx, "salog", [P, 1])
        a = core.sb(ctx, "sa", [P, 1])
        nega = core.sb(ctx, "snega", [P, 1])
        dtw = core.sb(ctx, "sdtw", [P, 1])
        dtw_wide = core.sb(ctx, "sdtww", [P, NST])
        dtb = core.sb(ctx, "sdtb", [P, 1])
        drow = core.sb(ctx, "sdrow", [P, D])
        gamma = core.sb(ctx, "sgamma", [P, D])
        beta = core.sb(ctx, "sbeta", [P, D])
        sig = core.sb(ctx, "ssig", [P, PAIRS, S])
        dt = core.sb(ctx, "sdt", [P, PAIRS, S])
        da = core.sb(ctx, "sda", [P, PAIRS, S])
        dbu = core.sb(ctx, "sdbu", [P, PAIRS, S])
        st = core.sb(ctx, "sst", [P, PAIRS, S])
        dx = core.sb(ctx, "sdx", [P, TILES, D])
        y = core.sb(ctx, "sy", [P, TILES, D])
        yn = core.sb(ctx, "syn", [P, TILES, D])
        yg = core.sb(ctx, "syg", [P, TILES, D])
        yb = core.sb(ctx, "syb", [P, TILES, D])
        stats = core.sb(ctx, "sstats", [P, TILES, 6])
        mv = core.sb(ctx, "smv", [P, TILES, 2])
        var = core.sb(ctx, "svar", [P, TILES])
        std = core.sb(ctx, "sstd", [P, TILES])
        rstd = core.sb(ctx, "srstd", [P, TILES])
        (loaded, a_exp, a_ready, wide_ready, dt_mm, u_mm, sig_done, dt_done, da_done, dbu_done, scanned, dx_done, y_mm,
         y_kept, stats_done, mv_done, var_done, std_done, rstd_done, normed, gained, shifted) = core.sems(
            "ss", "loaded aexp aready wide dtmm umm sig dt da dbu scanned dx ymm ykept stats mv var std rstd normed "
                  "gained shifted")
        with nc.Block() as block:
            @block.sync
            def _(sp):
                for dst, src in ((bT, d["B_T"]), (dtw, d["dt_w"]), (alog, d["A_log"]), (cT, d["C_T"]),
                                 (dtb, d["dt_b"].partition_broadcast(P)), (drow, d["D_vec"].partition_broadcast(P)),
                                 (gamma, d["gamma"].partition_broadcast(P)), (beta, d["beta"].partition_broadcast(P))):
                    sp.dma_start(dst[:], src).then_inc(loaded, 16)

            @block.tensor
            def _(pe):
                pe.wait_ge(loaded, 8 * 16)
                pe.wait_ge(wide_ready, 1)
                for p in range(PAIRS):
                    for half in range(2):
                        b = 2 * p + half
                        r = slice(half * NST, (half + 1) * NST)
                        x = core.xT[:, b * S:(b + 1) * S]
                        nc.tensor.matmul(bank[p][r, :], dtw_wide[:], x, start=True, stop=True).then_inc(dt_mm, 1)
                        nc.tensor.matmul(bank[2 + p][r, :], bT[:], x, start=True, stop=True).then_inc(u_mm, 1)
                for t in range(TILES):
                    b = t // BT
                    pe.wait_ge(scanned, b // 2 + 1)
                    r = slice(b % 2 * NST, (b % 2 + 1) * NST)
                    last = nc.tensor.matmul(bank[4 + b][:, t % BT * D:(t % BT + 1) * D],
                                            st[r, b // 2, t % BT * P:(t % BT + 1) * P], cT[r, :], start=True, stop=True)
                    if t % BT == BT - 1:
                        last.then_inc(y_mm, 1)

            @block.scalar
            def _(act):
                act.wait_ge(loaded, 8 * 16)
                nc.scalar.activation(a[:], alog[:], ACT.Exp).then_inc(a_exp, 1)
                for p in range(PAIRS):
                    act.wait_ge(dt_mm, 2 * p + 2)
                    nc.scalar.activation(sig[:, p], bank[p][:], ACT.Sigmoid, bias=dtb[:, 0:1]).then_inc(sig_done, 1)
                act.wait_ge(a_ready, 1)
                for p in range(PAIRS):
                    act.wait_ge(dt_done, p + 1)
                    nc.scalar.activation(da[:, p], dt[:, p], ACT.Exp, scale=nega[:, 0:1]).then_inc(da_done, 1)
                act.wait_ge(var_done, 1)
                nc.scalar.activation(std[:], var[:], ACT.Sqrt).then_inc(std_done, 1)

            @block.vector
            def _(dve):
                def wide(v, n=TILES):
                    return v[:].unsqueeze(1).broadcast_to([P, n, D])

                dve.wait_ge(loaded, 8 * 16)
                nc.vector.tensor_copy(dtw_wide[:], dtw[:, 0:1].broadcast_to([P, NST])).then_inc(wide_ready, 1)
                dve.wait_ge(a_exp, 1)
                nc.vector.tensor_scalar(nega[:], a[:], -1.0, None, ALU.mult).then_inc(a_ready, 1)
                nc.vector.tensor_tensor(dx[:], core.xn[:], wide(drow), ALU.mult).then_inc(dx_done, 1)
                for p in range(PAIRS):
                    dve.wait_ge(sig_done, p + 1)
                    nc.vector.tensor_scalar(dt[:, p], sig[:, p], 0.1 - 0.001, 0.001, ALU.mult, ALU.add).then_inc(dt_done, 1)
                for p in range(PAIRS):
                    dve.wait_ge(dt_done, p + 1)
                    dve.wait_ge(u_mm, 2 * p + 2)
                    nc.vector.tensor_tensor(dbu[:, p], bank[2 + p][:], dt[:, p], ALU.mult).then_inc(dbu_done, 1)
                for p in range(PAIRS):
                    dve.wait_ge(da_done, p + 1)
                    dve.wait_ge(dbu_done, p + 1)
                    nc.vector.tensor_tensor_scan(st[:, p], da[:, p], dbu[:, p], 0.0, ALU.mult, ALU.add
                                                 ).then_inc(scanned, 1)
                dve.wait_ge(dx_done, 1)
                for b in range(B):
                    dve.wait_ge(y_mm, b + 1)
                    nc.vector.tensor_tensor(y[:, b * BT:(b + 1) * BT], bank[4 + b][:].rearrange("p (t d) -> p t d", d=D),
                                            dx[:, b * BT:(b + 1) * BT], ALU.add).then_inc(y_kept, 1)
                for t in range(TILES):
                    dve.wait_ge(y_kept, t // BT + 1)
                    nc.vector.bn_stats(stats[:, t], y[:, t]).then_inc(stats_done, 1)
                for t in range(TILES):
                    dve.wait_ge(stats_done, t + 1)
                    nc.vector.bn_aggr(mv[:, t], stats[:, t]).then_inc(mv_done, 1)
                dve.wait_ge(mv_done, TILES)
                nc.vector.tensor_scalar(var[:], mv[:, :, 1], EPS, None, ALU.add).then_inc(var_done, 1)
                dve.wait_ge(std_done, 1)
                nc.vector.reciprocal(rstd[:], std[:]).then_inc(rstd_done, 1)
                dve.wait_ge(rstd_done, 1)
                for t in range(TILES):
                    nc.vector.tensor_scalar(yn[:, t], y[:, t], mv[:, t, 0:1], rstd[:, t:t + 1],
                                            ALU.subtract, ALU.mult).then_inc(normed, 1)
                dve.wait_ge(normed, TILES)
                nc.vector.tensor_tensor(yg[:], yn[:], wide(gamma), ALU.mult).then_inc(gained, 1)
                dve.wait_ge(gained, 1)
                nc.vector.tensor_tensor(yb[:], yg[:], wide(beta), ALU.add).then_inc(shifted, 1)
                dve.wait_ge(shifted, 1)
                nc.vector.tensor_tensor(core.h[:], core.h[:], yb[:], ALU.add)


def feature_mixer(core, d):
    nc, bank = core.nc, core.bank
    with ExitStack() as ctx:
        w = core.sb(ctx, "fw", [P, 2, P])
        wm = core.sb(ctx, "fwm", [P, 2, P])
        keep = core.sb(ctx, "fkeep", [P, P])
        b1 = core.sb(ctx, "fb1", [P, 1])
        b2 = core.sb(ctx, "fb2", [P, D])
        act_out = core.sb(ctx, "fact", [P, B, S])
        hb = core.sb(ctx, "fhb", [P, TILES, D])
        loaded, masked, mm1, acted, mm2, biased = core.sems("fm", "loaded masked mm1 acted mm2 biased")
        with nc.Block() as block:
            @block.sync
            def _(sp):
                for dst, src in ((w, d["mix_w"]), (keep, d["tril_T"]), (b1, d["mix_b1"]),
                                 (b2, d["mix_b2"].partition_broadcast(P))):
                    sp.dma_start(dst[:], src).then_inc(loaded, 16)

            @block.vector
            def _(dve):
                dve.wait_ge(loaded, 64)
                nc.vector.tensor_tensor(wm[:], w[:], keep[:].unsqueeze(1).broadcast_to([P, 2, P]), ALU.mult
                                        ).then_inc(masked, 1)
                nc.vector.tensor_tensor(hb[:], core.h[:], b2[:].unsqueeze(1).broadcast_to([P, TILES, D]), ALU.add
                                        ).then_inc(biased, 1)
                dve.wait_ge(biased, 1)
                for b in range(B):
                    dve.wait_ge(mm2, b + 1)
                    nc.vector.tensor_tensor(core.h[:, b * BT:(b + 1) * BT],
                                            bank[4 + b][:].rearrange("p (t d) -> p t d", d=D),
                                            hb[:, b * BT:(b + 1) * BT], ALU.add)

            @block.tensor
            def _(pe):
                pe.wait_ge(masked, 1)
                for b in range(B):
                    nc.tensor.matmul(bank[b][:], wm[:, 0], core.xT[:, b * S:(b + 1) * S], start=True,
                                     stop=True).then_inc(mm1, 1)
                for b in range(B):
                    pe.wait_ge(acted, b + 1)
                    for t in range(BT):
                        last = nc.tensor.matmul(bank[4 + b][:, t * D:(t + 1) * D], act_out[:, b, t * P:(t + 1) * P],
                                                wm[:, 1], start=True, stop=True)
                    last.then_inc(mm2, 1)

            @block.scalar
            def _(act):
                act.wait_ge(loaded, 64)
                for b in range(B):
                    act.wait_ge(mm1, b + 1)
                    nc.scalar.activation(act_out[:, b], bank[b][:], ACT.Gelu, bias=b1[:, 0:1]).then_inc(acted, 1)


def store(core, d):
    nc = core.nc
    (stored,) = core.sems("out", "stored")
    with nc.Block() as block:
        @block.sync
        def _(sp):
            sp.dma_start(d["out"].rearrange("(t p) d -> p t d", p=P), core.h[:]).then_inc(stored, 16)
            sp.wait_ge(stored, 16)


def pack(x, **w):
    n = np
    f = n.float32

    def permute_gates(a):
        a = a.reshape(a.shape[:-1] + (4, 2, P))
        return n.ascontiguousarray(n.moveaxis(a[..., [0, 1, 3, 2], :, :], -2, -3)).reshape(a.shape[:-3] + (G4,))

    def rows(a):
        e, k, m = a.shape
        return n.moveaxis(a.reshape(e, k // P, P, m), 1, 2).reshape(e, P, k // P * m)

    def cols(a):
        return n.moveaxis(a.reshape(E, KH, P), 1, 2)

    out = {}
    pos = n.arange(N_FRAMES)[:, None] * N_FFT + n.arange(N_FFT)[None] - N_FFT // 2
    pos = n.abs(pos)
    pos = n.where(pos >= S, 2 * (S - 1) - pos, pos)
    out["ids_frames"] = n.ascontiguousarray(x[:, pos].reshape(BF, N_FFT).T)
    out["ids"] = n.ascontiguousarray(x.reshape(TOK))
    out["vocab_row"] = n.broadcast_to(n.arange(VOCAB, dtype=f), (N_FFT, VOCAB)).copy()
    out["vocab_col"] = n.arange(VOCAB, dtype=f)[:, None].copy()
    j = n.arange(N_FFT, dtype=n.float64)[:, None]
    fr = n.arange(N_FREQ, dtype=n.float64)[None]
    win = 0.5 - 0.5 * n.cos(2 * n.pi * j / N_FFT)
    ang = 2 * n.pi * (j * fr % N_FFT) / N_FFT
    out["dft"] = n.stack([win * n.cos(ang), win * n.sin(ang)], 1).astype(f)
    up = n.zeros((BF, TOK), f)
    for b in range(B):
        up[b * N_FRAMES + n.arange(S) * N_FRAMES // S, b * S + n.arange(S)] = 1
    out["upsample"] = up
    out["ident"] = n.eye(P, dtype=f)
    out["causal"] = n.where(n.arange(P)[None] > n.arange(P)[:, None], f(-1e30), f(0)).astype(f)
    out["emb_table"] = w["L0_tok_emb_table"]
    out["proj_w"] = w["L0_tok_proj_w"].reshape(N_FREQ, VOCAB, D_STFT)
    out["proj_b"] = w["L0_tok_proj_b"]
    qkv = [n.moveaxis(w[f"L0_attn_W_{c}"], 0, 1).reshape(D, AH * ADK) for c in "qkv"]
    wo = n.moveaxis(w["L0_attn_W_o"].reshape(4, P, D), 0, 1).reshape(P, 4 * D)
    out["attn_w"] = n.stack(qkv + [wo], 1)
    for name in ("router_w", "router_b"):
        out[name] = w["L0_ffn_" + name]
    ff = {k[len("L0_ffn_"):]: v for k, v in w.items() if k.startswith("L0_ffn_")}
    out["w_encode"] = n.concatenate([rows(ff[c]) for c in ("enc_w1", "enc_w2", "attn_in_w")], 2)
    out["w_attend"] = n.concatenate(
        [rows(ff["attn_out_w"]), rows(permute_gates(ff["lstm_wi_f"])), rows(permute_gates(ff["lstm_wi_b"]))], 2)
    out["w_after"] = n.concatenate([rows(ff[c]) for c in ("sig_w1", "sig_w2", "tan_w1", "tan_w2", "dec_w1", "dec_w2")], 2)
    inb = ff["attn_in_b"]
    out["cols"] = n.concatenate(
        [cols(a) for a in (ff["enc_b1"], ff["enc_g"], ff["enc_beta"], inb[:, 0:DM], inb[:, DM:2 * DM],
                           ff["attn_out_b"], ff["sig_b1"], ff["tan_b1"], ff["sig_b2"], ff["tan_b2"], ff["dec_b1"])], 2)
    out["rows"] = n.concatenate(
        [ff["enc_b2"], inb[:, 2 * DM:], permute_gates(ff["lstm_b_f"]), permute_gates(ff["lstm_b_b"]), ff["dec_b2"],
         ff["dec_g"], ff["dec_beta"]], 1)
    out["wh"] = n.ascontiguousarray(n.stack([rows(permute_gates(ff["lstm_wh_" + c])) for c in "fb"])
                                    .reshape(2, E, P, KH, G4).transpose(2, 0, 1, 3, 4))
    ss = {k[len("L1_attn_"):]: v for k, v in w.items() if k.startswith("L1_attn_")}
    out["B_T"] = ss["B_mat"].T
    out["C_T"] = n.concatenate([ss["C_mat"].T, ss["C_mat"].T], 0)
    out["A_log"] = n.concatenate([ss["A_log"], ss["A_log"]])[:, None]
    out["dt_w"] = ss["dt_w"].reshape(D, 1)
    for name in ("dt_b", "D_vec", "gamma", "beta"):
        out[name] = ss[name]
    out["mix_w"] = n.stack([w["L1_ffn_W1"].T, w["L1_ffn_W2"].T], 1)
    out["tril_T"] = n.triu(n.ones((P, P), f))
    out["mix_b1"] = w["L1_ffn_b1"][:, None]
    out["mix_b2"] = w["L1_ffn_b2"]
    return out


def build(nc, d, phases=None):
    with ExitStack() as ctx:
        core = Core(nc, ctx)
        d["zx"] = nc.dram_tensor("zx", (2, E, B, S, G4), F32, kind="Internal").ap()
        d["qk"] = nc.dram_tensor("qk", (E * B + 1, 2, 3, DM, S), BF16, kind="Internal").ap()
        d["vx"] = nc.dram_tensor("vx", (E * B, P, BT * NH * (DH + 1)), F32, kind="Internal").ap()
        d["hs"] = nc.dram_tensor("hs", (2, E, B, S, DM), F32, kind="Internal").ap()
        for phase in PHASES[:phases]:
            core.run(phase, d)
        core.run(store, d)


PHASES = [
    embed,
    lambda core, d: layer_norm(core, "ln0"),
    causal_attention,
    lambda core, d: layer_norm(core, "ln1"),
    router,
    experts_encode,
    experts_attend,
    recurrence,
    experts_after,
    lambda core, d: layer_norm(core, "ln2"),
    state_space,
    lambda core, d: layer_norm(core, "ln3"),
    feature_mixer,
]

NAMES = []


def kernel(**inputs):
    import concourse.bacc as bacc
    from concourse.bass_utils import run_bass_kernel_spmd

    nc = bacc.Bacc("TRN2", target_bir_lowering=False, num_devices=1)
    arrays = pack(**{k: np.asarray(v) for k, v in inputs.items()})
    arrays = {f"in_{k}": np.ascontiguousarray(v) for k, v in arrays.items()}
    d = {k[3:]: nc.dram_tensor(k, a.shape, mybir.dt.from_np(a.dtype), kind="ExternalInput").ap()
         for k, a in arrays.items()}
    d["out"] = nc.dram_tensor("out", (TOK, D), F32, kind="ExternalOutput").ap()
    build(nc, d)
    r = run_bass_kernel_spmd(nc, [arrays], core_ids=[0])
    return r.results[0]["out"].reshape(B, S, D)
```

```python
import concourse.bass as bass
from concourse import mybir
from contextlib import ExitStack
import numpy as np

F32 = mybir.dt.float32
BF16 = mybir.dt.bfloat16
I32 = mybir.dt.int32
ALU = mybir.AluOpType
ACT = mybir.ActivationFunctionType
AX = mybir.AxisListType

P = 128
B, S, D = 4, 512, 128
TOK = B * S
TILES = TOK // P
BT = S // P
EPS = 1e-5

VOCAB, D_EMB = 16, 89
D_STFT = D - D_EMB
N_FFT = 64
N_FREQ = N_FFT // 2 + 1
N_FRAMES = S // N_FFT + 1
BF = B * N_FRAMES

AH, ADK = 8, 64
E, DM, NH, DH = 4, 256, 16, 16
KH = DM // P
G4 = 4 * DM
NST = 64


def columns(*widths):
    at, out = 0, {}
    for name, width in widths:
        out[name] = at
        at += width
    return out, at


ENC, ENC_W = columns(("ew1", DM), ("ew2", KH * DM), ("qkv", KH * 3 * DM))
ATT, ATT_W = columns(("aow", KH * DM), ("wi", 2 * KH * G4))
POST, POST_W = columns(("sw1", 2 * KH * DM), ("tw1", 2 * KH * DM), ("sw2", KH * DM), ("tw2", KH * DM),
                       ("dw1", KH * DM), ("dw2", KH * D))
COLS = {n: KH * i for i, n in enumerate(("eb1", "eg", "ebeta", "qb", "kb", "aob", "sb1", "tb1", "sb2", "tb2", "db1"))}
COLS_W = KH * len(COLS)
ROWS, ROWS_W = columns(("eb2", DM), ("vb", DM), ("lb", 2 * G4), ("db2", D), ("dg", D), ("dbeta", D))


def clear_signals(nc, signals):
    with nc.Block() as block:
        @block.vector
        def _(dve):
            for s in signals[0::4]:
                dve.sem_clear(s)

        @block.scalar
        def _(act):
            for s in signals[1::4]:
                act.sem_clear(s)

        @block.tensor
        def _(pe):
            for s in signals[2::4]:
                pe.sem_clear(s)

        @block.sync
        def _(sp):
            for s in signals[3::4]:
                sp.sem_clear(s)


class Core:

    def __init__(self, nc, ctx):
        self.nc, self.ctx = nc, ctx
        self.bank = [ctx.enter_context(nc.psum_tensor(f"bank{i}", [P, 512], F32)) for i in range(8)]
        self.h = self.sb(ctx, "h", [P, TILES, D])
        self.xn = self.sb(ctx, "xn", [P, TILES, D])
        self.xT = self.sb(ctx, "xT", [P, TOK])
        self.ident = self.sb(ctx, "ident", [P, P])
        self.route = self.sb(ctx, "route", [P, TILES, E])

    def sb(self, ctx, name, shape, dt=F32):
        return ctx.enter_context(self.nc.sbuf_tensor(name, shape, dt))

    def sems(self, tag, names):
        made = [self.stage.enter_context(self.nc.semaphore(f"{tag}_{n}")) for n in names.split()]
        self.made += made
        return made

    def run(self, stage, d):
        self.made = []
        with ExitStack() as self.stage:
            stage(self, d)
            clear_signals(self.nc, self.made)


def embed(core, d):
    nc = core.nc
    half = BF // 2 * VOCAB
    with ExitStack() as ctx:
        ids_fr = core.sb(ctx, "ids_fr", [N_FFT, BF], I32)
        ids_tok = core.sb(ctx, "ids_tok", [VOCAB, TOK], I32)
        idf_fr = core.sb(ctx, "idf_fr", [N_FFT, BF])
        idf_tok = core.sb(ctx, "idf_tok", [VOCAB, TOK])
        vocab_row = core.sb(ctx, "vocab_row", [N_FFT, VOCAB])
        vocab_col = core.sb(ctx, "vocab_col", [VOCAB, 1])
        dft = core.sb(ctx, "dft", [N_FFT, 2, N_FREQ])
        hot_fr = core.sb(ctx, "hot_fr", [N_FFT, BF, VOCAB])
        hot_tok = core.sb(ctx, "hot_tok", [VOCAB, TOK])
        sq = core.sb(ctx, "sq", [N_FREQ, 2, BF * VOCAB])
        power = core.sb(ctx, "power", [N_FREQ, BF * VOCAB])
        mag = core.sb(ctx, "mag", [N_FREQ, BF, VOCAB])
        proj = core.sb(ctx, "proj", [N_FREQ, VOCAB, D_STFT])
        table = core.sb(ctx, "table", [VOCAB, D])
        enc = core.sb(ctx, "enc", [BF, D])
        bias = core.sb(ctx, "bias", [1, D])
        up = core.sb(ctx, "up", [BF, TOK])
        ones = core.sb(ctx, "ones", [1, P])
        loaded, zeroed, placed, cast, hot, dft_done, squared, summed, mag_ready, enc_done, enc_ready, h_done, h_kept = \
            core.sems("em", "loaded zeroed placed cast hot dft squared summed mag enc encr h kept")
        with nc.Block() as block:
            @block.sync
            def _(sp):
                for dst, src in ((ids_fr, d["ids_frames"]), (vocab_row, d["vocab_row"]), (dft, d["dft"]),
                                 (vocab_col, d["vocab_col"]), (proj, d["proj_w"]), (up, d["upsample"]),
                                 (core.ident, d["ident"])):
                    sp.dma_start(dst[:], src).then_inc(loaded, 16)
                sp.dma_start(ids_tok[:], d["ids"].partition_broadcast(VOCAB)).then_inc(loaded, 16)
                sp.wait_ge(zeroed, 3)
                sp.dma_start(table[:, 0:D_EMB], d["emb_table"]).then_inc(placed, 16)
                sp.dma_start(bias[:, D_EMB:D], d["proj_b"].unsqueeze(0)).then_inc(placed, 16)

            @block.vector
            def _(dve):
                nc.vector.memset(table[:], 0.0).then_inc(zeroed, 1)
                nc.vector.memset(bias[:], 0.0).then_inc(zeroed, 1)
                nc.vector.memset(enc[:], 0.0).then_inc(zeroed, 1)
                nc.vector.memset(ones[:], 1.0).then_inc(zeroed, 1)
                dve.wait_ge(loaded, 8 * 16)
                nc.vector.tensor_copy(idf_fr[:], ids_fr[:]).then_inc(cast, 1)
                nc.vector.tensor_copy(idf_tok[:], ids_tok[:]).then_inc(cast, 1)
                dve.wait_ge(cast, 2)
                nc.vector.tensor_tensor(hot_fr[:], idf_fr[:].unsqueeze(2).broadcast_to([N_FFT, BF, VOCAB]),
                                        vocab_row[:].unsqueeze(1).broadcast_to([N_FFT, BF, VOCAB]),
                                        ALU.is_equal).then_inc(hot, 1)
                nc.vector.tensor_scalar(hot_tok[:], idf_tok[:], vocab_col[:, 0:1], None,
                                        ALU.is_equal).then_inc(hot, 1)
                dve.wait_ge(squared, 4)
                nc.vector.tensor_tensor(power[:], sq[:, 0], sq[:, 1], ALU.add).then_inc(summed, 1)
                dve.wait_ge(enc_done, 1)
                nc.vector.tensor_copy(enc[:, D_EMB:D], core.bank[4][0:BF, 0:D_STFT]).then_inc(enc_ready, 1)
                for g in range(4):
                    dve.wait_ge(h_done, g + 1)
                    nc.vector.tensor_copy(core.h[:, 4 * g:4 * g + 4],
                                          core.bank[g][:].rearrange("p (t d) -> p t d", d=D)).then_inc(h_kept, 1)

            @block.tensor
            def _(pe):
                pe.wait_ge(hot, 2)
                frames = hot_fr[:].rearrange("p f v -> p (f v)")
                for part in range(2):
                    for n in range(2):
                        nc.tensor.matmul(core.bank[2 * part + n][0:N_FREQ, 0:half], dft[:, part],
                                         frames[:, n * half:(n + 1) * half], start=True,
                                         stop=True).then_inc(dft_done, 1)
                pe.wait_ge(mag_ready, 1)
                for v in range(VOCAB):
                    last = nc.tensor.matmul(core.bank[4][0:BF, 0:D_STFT], mag[:, :, v], proj[:, v],
                                            start=v == 0, stop=v == VOCAB - 1)
                last.then_inc(enc_done, 1)
                pe.wait_ge(enc_ready, 1)
                pe.wait_ge(placed, 32)
                pe.wait_ge(zeroed, 4)
                for t in range(TILES):
                    out = core.bank[t // 4][:, (t % 4) * D:(t % 4 + 1) * D]
                    tok = slice(t * P, (t + 1) * P)
                    nc.tensor.matmul(out, hot_tok[:, tok], table[:], start=True, stop=False)
                    nc.tensor.matmul(out, up[:, tok], enc[:], start=False, stop=False)
                    last = nc.tensor.matmul(out, ones[:], bias[:], start=False, stop=True)
                    if t % 4 == 3:
                        last.then_inc(h_done, 1)

            @block.scalar
            def _(act):
                for part in range(2):
                    for n in range(2):
                        act.wait_ge(dft_done, 2 * part + n + 1)
                        nc.scalar.activation(sq[:, part, n * half:(n + 1) * half],
                                             core.bank[2 * part + n][0:N_FREQ, 0:half],
                                             ACT.Square).then_inc(squared, 1)
                act.wait_ge(summed, 1)
                nc.scalar.activation(mag[:].rearrange("p f v -> p (f v)"), power[:], ACT.Sqrt).then_inc(mag_ready, 1)


def layer_norm(core, tag):
    nc = core.nc
    with ExitStack() as ctx:
        stats = core.sb(ctx, f"{tag}_stats", [P, TILES, 6])
        mv = core.sb(ctx, f"{tag}_mv", [P, TILES, 2])
        var = core.sb(ctx, f"{tag}_var", [P, TILES])
        std = core.sb(ctx, f"{tag}_std", [P, TILES])
        rstd = core.sb(ctx, f"{tag}_rstd", [P, TILES])
        stats_done, mv_done, var_done, std_done, rstd_done, normed, turned, kept = \
            core.sems(tag, "stats mv var std rstd normed turned kept")
        with nc.Block() as block:
            @block.vector
            def _(dve):
                for t in range(TILES):
                    nc.vector.bn_stats(stats[:, t], core.h[:, t]).then_inc(stats_done, 1)
                for t in range(TILES):
                    dve.wait_ge(stats_done, t + 1)
                    nc.vector.bn_aggr(mv[:, t], stats[:, t]).then_inc(mv_done, 1)
                dve.wait_ge(mv_done, TILES)
                nc.vector.tensor_scalar(var[:], mv[:, :, 1], EPS, None, ALU.add).then_inc(var_done, 1)
                dve.wait_ge(std_done, 1)
                nc.vector.reciprocal(rstd[:], std[:]).then_inc(rstd_done, 1)
                dve.wait_ge(rstd_done, 1)
                for t in range(TILES):
                    nc.vector.tensor_scalar(core.xn[:, t], core.h[:, t], mv[:, t, 0:1], rstd[:, t:t + 1],
                                            ALU.subtract, ALU.mult).then_inc(normed, 1)

            @block.scalar
            def _(act):
                act.wait_ge(var_done, 1)
                nc.scalar.activation(std[:], var[:], ACT.Sqrt).then_inc(std_done, 1)
                for g in range(4):
                    act.wait_ge(turned, g + 1)
                    nc.scalar.activation(core.xT[:, g * 512:(g + 1) * 512], core.bank[g][:], ACT.Copy).then_inc(kept, 1)

            @block.tensor
            def _(pe):
                for t in range(TILES):
                    pe.wait_ge(normed, t + 1)
                    last = nc.tensor.transpose(core.bank[t // 4][:, (t % 4) * P:(t % 4 + 1) * P], core.xn[:, t],
                                               core.ident[:])
                    if t % 4 == 3:
                        last.then_inc(turned, 1)


class Attention:

    def __init__(self, core, ctx, tag, heads, causal, per_bank, rows):
        self.core, self.heads, self.causal, self.per_bank, self.rows = core, heads, causal, per_bank, rows
        self.p = core.sb(ctx, f"{tag}_p", [P, 2, BT, S])
        self.pT = core.sb(ctx, f"{tag}_pT", [P, 2, BT, S])
        self.negmax = core.sb(ctx, f"{tag}_negmax", [P, heads, BT])
        self.total = core.sb(ctx, f"{tag}_total", [P, heads, BT])
        self.inv = core.sb(ctx, f"{tag}_inv", [P, heads, BT])
        self.oT = core.sb(ctx, f"{tag}_oT", [P, heads // per_bank, S])
        (self.scored, self.maxed, self.exped, self.inverted, self.normed, self.turned, self.kept_v, self.kept_a,
         self.valued, self.out_kept) = core.sems(
            tag, "scored maxed exped inverted normed turned keptv kepta valued outkept")
        self.signals = [self.scored, self.maxed, self.exped, self.inverted, self.normed, self.turned, self.kept_v,
                        self.kept_a, self.valued, self.out_kept]

    def width(self, qt):
        return (qt + 1) * P if self.causal else S

    def low(self, kt):
        return kt * P if self.causal else 0

    def tensor(self, pe, query, key, value, key_wait, mask):
        nc, bank = self.core.nc, self.core.bank

        def score(h, qt):
            if qt == 0:
                key_wait(pe, h)
            if h > 0:
                pe.wait_ge(self.exped, BT * (h - 1) + qt + 1)
            w = self.width(qt)
            last = nc.tensor.matmul(bank[qt][:, 0:w], query(h, qt), key(h)[:, 0:w], start=True, stop=not self.causal)
            if self.causal:
                last = nc.tensor.matmul(bank[qt][:, qt * P:w], self.core.ident[:], mask, start=False, stop=True)
            last.then_inc(self.scored, 1)

        def turn(h, kt):
            n = BT * h + kt
            if kt == 0:
                pe.wait_ge(self.normed, BT * (h + 1))
            if n >= 2:
                pe.wait_ge(*((self.kept_a, (n - 2) // 2 + 1) if kt % 2 else (self.kept_v, (n - 2) // 2 + 1)))
            for qt in range(kt if self.causal else 0, BT):
                last = nc.tensor.transpose(bank[4 + kt % 2][:, qt * P:(qt + 1) * P],
                                           self.p[:, h % 2, qt, kt * P:(kt + 1) * P], self.core.ident[:])
            last.then_inc(self.turned, 1)

        def values(h, kt):
            n = BT * h + kt
            pe.wait_ge(*((self.kept_a, n // 2 + 1) if kt % 2 else (self.kept_v, n // 2 + 1)))
            g, c = divmod(h, self.per_bank)
            if c == 0 and kt == 0 and g >= 2:
                pe.wait_ge(self.out_kept, g - 1)
            r = c * (P // self.per_bank)
            lo = self.low(kt)
            nc.tensor.matmul(bank[6 + g % 2][r:r + self.rows, lo:S], value(h, kt), self.pT[:, h % 2, kt, lo:S],
                             start=kt == 0, stop=kt == BT - 1).then_inc(self.valued, 1)

        for h in range(self.heads + 1):
            if h < self.heads:
                for qt in range(BT):
                    score(h, qt)
            if h > 0:
                turn(h - 1, 0)
                turn(h - 1, 1)
                values(h - 1, 0)
                turn(h - 1, 2)
                values(h - 1, 1)
                turn(h - 1, 3)
                values(h - 1, 2)
                values(h - 1, 3)

    def vector(self, dve):
        nc, bank = self.core.nc, self.core.bank

        def largest(h, qt):
            dve.wait_ge(self.scored, BT * h + qt + 1)
            nc.vector.tensor_reduce(self.negmax[:, h, qt:qt + 1], bank[qt][:, 0:self.width(qt)], AX.X, ALU.max,
                                    negate=True).then_inc(self.maxed, 1)

        def normalise(h):
            dve.wait_ge(self.exped, BT * (h + 1))
            nc.vector.reciprocal(self.inv[:, h], self.total[:, h]).then_inc(self.inverted, 1)
            dve.wait_ge(self.inverted, h + 1)
            for qt in range(BT):
                p = self.p[:, h % 2, qt, 0:self.width(qt)]
                nc.vector.tensor_scalar(p, p, self.inv[:, h, qt:qt + 1], None, ALU.mult).then_inc(self.normed, 1)

        def keep(h, kt):
            dve.wait_ge(self.turned, BT * h + kt + 1)
            if h >= 2:
                dve.wait_ge(self.valued, BT * (h - 2) + kt + 1)
            lo = self.low(kt)
            nc.vector.tensor_copy(self.pT[:, h % 2, kt, lo:S], bank[4 + kt % 2][:, lo:S]).then_inc(self.kept_v, 1)

        for h in range(self.heads + 1):
            if h > 0:
                normalise(h - 1)
            if h < self.heads:
                largest(h, 0)
                largest(h, 1)
                largest(h, 2)
            if h > 0:
                keep(h - 1, 0)
            if h < self.heads:
                largest(h, 3)
            if h > 0:
                keep(h - 1, 2)
            if h > 0 and h % self.per_bank == 0:
                g = h // self.per_bank - 1
                dve.wait_ge(self.valued, BT * h)
                nc.vector.tensor_copy(self.oT[:, g], bank[6 + g % 2][:]).then_inc(self.out_kept, 1)

    def scalar(self, act):
        nc, bank = self.core.nc, self.core.bank

        def exponent(h, qt):
            act.wait_ge(self.maxed, BT * h + qt + 1)
            if h >= 2 and qt == 0:
                act.wait_ge(self.turned, BT * (h - 1))
            w = self.width(qt)
            nc.scalar.activation(self.p[:, h % 2, qt, 0:w], bank[qt][:, 0:w], ACT.Exp,
                                 bias=self.negmax[:, h, qt:qt + 1],
                                 accum_out=self.total[:, h, qt:qt + 1]).then_inc(self.exped, 1)

        def keep(h, kt):
            act.wait_ge(self.turned, BT * h + kt + 1)
            if h >= 2:
                act.wait_ge(self.valued, BT * (h - 2) + kt + 1)
            lo = self.low(kt)
            nc.scalar.activation(self.pT[:, h % 2, kt, lo:S], bank[4 + kt % 2][:, lo:S],
                                 ACT.Copy).then_inc(self.kept_a, 1)

        for h in range(self.heads + 1):
            if h < self.heads:
                exponent(h, 0)
                exponent(h, 1)
                exponent(h, 2)
            if h > 0:
                keep(h - 1, 1)
            if h < self.heads:
                exponent(h, 3)
            if h > 0:
                keep(h - 1, 3)


def causal_attention(core, d):
    nc = core.nc
    with ExitStack() as ctx:
        w = core.sb(ctx, "aw", [P, 4, AH * ADK])
        mask = core.sb(ctx, "amask", [P, P])
        xb = core.sb(ctx, "axb", [P, S])
        qT = core.sb(ctx, "aqT", [P, 4, S])
        kz = core.sb(ctx, "akz", [P, AH, S])
        v = core.sb(ctx, "av", [P, BT, AH * ADK])
        att = Attention(core, ctx, "at", AH, True, 2, ADK)
        loaded, x_ready, q_mm, k_mm, v_mm, q_kept, k_kept, v_kept, o_mm, o_kept = \
            core.sems("at", "loaded x qmm kmm vmm qkept kkept vkept omm okept")
        with nc.Block() as block:
            @block.sync
            def _(sp):
                sp.dma_start(w[:], d["attn_w"]).then_inc(loaded, 16)
                sp.dma_start(mask[:], d["causal"]).then_inc(loaded, 16)
                sp.wait_ge(loaded, 32)

            @block.vector
            def _(dve):
                nc.vector.memset(kz[:], 0.0)
        with nc.Fori(0, B) as b:
            with nc.Block() as block:
                @block.tensor
                def _(pe):
                    pe.wait_ge(x_ready, 1)
                    for n in range(4):
                        nc.tensor.matmul(core.bank[n][:], w[:, 0, n * P:(n + 1) * P], xb[:], start=True,
                                         stop=True).then_inc(q_mm, 1)
                    for n in range(4):
                        nc.tensor.matmul(core.bank[4 + n][:], w[:, 1, n * P:(n + 1) * P], xb[:], start=True,
                                         stop=True).then_inc(k_mm, 1)
                    for t in range(BT):
                        pe.wait_ge(q_kept, t + 1)
                        nc.tensor.matmul(core.bank[t][:], xb[:, t * P:(t + 1) * P], w[:, 2], start=True,
                                         stop=True).then_inc(v_mm, 1)

                    def key_wait(pe, h):
                        if h == 0:
                            pe.wait_ge(v_kept, BT)
                            pe.wait_ge(k_kept, 8)

                    att.tensor(pe, lambda h, qt: qT[:, h // 2, qt * P:(qt + 1) * P], lambda h: kz[:, h],
                               lambda h, kt: v[:, kt, h * ADK:(h + 1) * ADK], key_wait, mask[:])
                    pe.wait_ge(att.out_kept, 4)
                    for t in range(BT):
                        for n in range(4):
                            last = nc.tensor.matmul(core.bank[0][:, t * D:(t + 1) * D],
                                                    att.oT[:, n, t * P:(t + 1) * P], w[:, 3, n * D:(n + 1) * D],
                                                    start=n == 0, stop=n == 3)
                    last.then_inc(o_mm, 1)

                @block.vector
                def _(dve):
                    nc.vector.tensor_copy(xb[:], core.xT[:, bass.ds(b * S, S)]).then_inc(x_ready, 1)
                    for n in range(4):
                        dve.wait_ge(k_mm, n + 1)
                        for half in (0, 1):
                            r = slice(half * ADK, (half + 1) * ADK)
                            nc.vector.tensor_copy(kz[r, 2 * n + half], core.bank[4 + n][r, :]).then_inc(k_kept, 1)
                    att.vector(dve)
                    dve.wait_ge(o_mm, 1)
                    hb = core.h[:, bass.ds(b * BT, BT)]
                    nc.vector.tensor_tensor(hb, core.bank[0][:].rearrange("p (t d) -> p t d", d=D), hb,
                                            ALU.add).then_inc(o_kept, 1)

                @block.scalar
                def _(act):
                    for n in range(4):
                        act.wait_ge(q_mm, n + 1)
                        nc.scalar.activation(qT[:, n], core.bank[n][:], ACT.Copy,
                                             scale=float(ADK) ** -0.5).then_inc(q_kept, 1)
                    for t in range(BT):
                        act.wait_ge(v_mm, t + 1)
                        nc.scalar.activation(v[:, t], core.bank[t][:], ACT.Copy).then_inc(v_kept, 1)
                    att.scalar(act)
            clear_signals(nc, att.signals + [x_ready, q_mm, k_mm, v_mm, q_kept, k_kept, v_kept, o_mm, o_kept])


def router(core, d):
    nc = core.nc
    with ExitStack() as ctx:
        rw = core.sb(ctx, "rw", [P, E])
        rb = core.sb(ctx, "rb", [P, E])
        logit = core.sb(ctx, "logit", [P, TILES, E])
        shifted = core.sb(ctx, "shifted", [P, TILES, E])
        ex = core.sb(ctx, "rex", [P, TILES, E])
        top = core.sb(ctx, "rtop", [P, TILES])
        total = core.sb(ctx, "rtotal", [P, TILES])
        inv = core.sb(ctx, "rinv", [P, TILES])
        loaded, logits_mm, step, shifted_ready, ex_ready = core.sems("ro", "loaded mm step shifted ex")
        with nc.Block() as block:
            @block.sync
            def _(sp):
                sp.dma_start(rw[:], d["router_w"]).then_inc(loaded, 16)
                sp.dma_start(rb[:], d["router_b"].partition_broadcast(P)).then_inc(loaded, 16)

            @block.tensor
            def _(pe):
                pe.wait_ge(loaded, 32)
                for t in range(TILES):
                    last = nc.tensor.matmul(core.bank[0][:, t * E:(t + 1) * E], core.xT[:, t * P:(t + 1) * P], rw[:],
                                            start=True, stop=True)
                last.then_inc(logits_mm, 1)

            @block.vector
            def _(dve):
                def wide(a):
                    return a.unsqueeze(2).broadcast_to([P, TILES, E])

                dve.wait_ge(logits_mm, 1)
                dve.wait_ge(loaded, 32)
                nc.vector.tensor_tensor(logit[:], core.bank[0][:, 0:TILES * E].rearrange("p (t e) -> p t e", e=E),
                                        rb[:].unsqueeze(1).broadcast_to([P, TILES, E]), ALU.add).then_inc(step, 1)
                dve.wait_ge(step, 1)
                nc.vector.tensor_reduce(top[:], logit[:], AX.X, ALU.max).then_inc(step, 1)
                dve.wait_ge(step, 2)
                nc.vector.tensor_tensor(shifted[:], logit[:], wide(top[:]), ALU.subtract).then_inc(shifted_ready, 1)
                dve.wait_ge(ex_ready, 1)
                nc.vector.tensor_reduce(total[:], ex[:], AX.X, ALU.add).then_inc(step, 1)
                dve.wait_ge(step, 3)
                nc.vector.reciprocal(inv[:], total[:]).then_inc(step, 1)
                dve.wait_ge(step, 4)
                nc.vector.tensor_tensor(core.route[:], ex[:], wide(inv[:]), ALU.mult)

            @block.scalar
            def _(act):
                act.wait_ge(shifted_ready, 1)
                nc.scalar.activation(ex[:], shifted[:], ACT.Exp).then_inc(ex_ready, 1)


def experts_encode(core, d):
    nc, bank = core.nc, core.bank
    with ExitStack() as ctx:
        steps = 2 * B
        w = core.sb(ctx, "ew", [P, 2, ENC_W])
        cols = core.sb(ctx, "ecols", [P, 2, COLS_W])
        rows = core.sb(ctx, "erows", [P, 2, 2, 2, DM])
        qbs = core.sb(ctx, "eqbs", [P, 2, KH])
        h1 = core.sb(ctx, "eh1", [P, 2, KH, S])
        h2 = core.sb(ctx, "eh2", [P, 2, BT, DM])
        hn = core.sb(ctx, "ehn", [P, 2, BT, DM])
        hT = core.sb(ctx, "ehT", [P, 2, KH, S])
        qk = core.sb(ctx, "eqk", [P, 2, KH, S])
        rest = core.sb(ctx, "erest", [P, 2, KH, S])
        parts = core.sb(ctx, "eparts", [P, 2, 2, 3, KH, S], BF16)
        vx = core.sb(ctx, "evx", [P, 2, BT, NH, DH + 1])
        stats = core.sb(ctx, "estats", [P, BT, 6])
        mv = core.sb(ctx, "emv", [P, BT, 2])
        var = core.sb(ctx, "evar", [P, BT])
        std = core.sb(ctx, "estd", [P, BT])
        rstd = core.sb(ctx, "erstd", [P, BT])
        (qbs_done, h1_mm, h1_kept, h2_mm, h2_kept, stats_done, mv_done, var_done, std_done, rstd_done, normed,
         hn_turned, hT_kept, qk_mm, q_kept, k_kept, v_mm, v_kept) = core.sems(
            "ee", "qbs h1mm h1kept h2mm h2kept stats mv var std rstd normed hnturned hTkept qkmm qkept kkept "
                  "vmm vkept")
        ew1_in, ew2_in, qkv_in, vectors_in = (core.sems("ee", f"{n}0 {n}1") for n in ("ew1", "ew2", "qkv", "vec"))
        part1, part2, part3, rested = (core.sems("ee", f"{n}q {n}k") for n in ("p1", "p2", "p3", "rest"))
        qk_out = [core.sems("ee", "qout0 qout1"), core.sems("ee", "kout0 kout1")]
        vx_out = core.sems("ee", "vout0 vout1")

        def weight(s, name, part, lo, n):
            width = {"ew1": DM, "ew2": DM, "qkv": 3 * DM}[name]
            at = ENC[name] + part * width + lo
            return w[:, s // B, at:at + n]

        def col(s, name, part):
            return cols[:, s // B, COLS[name] + part:COLS[name] + part + 1]

        with nc.Block() as block:
            @block.vector
            def _(dve):
                nc.vector.memset(vx[:], 1.0)
        with nc.Fori(0, E // 2) as turn:
            with nc.Block() as block:
                @block.sync
                def _(sp):
                    for half in range(2):
                        e = 2 * turn + half
                        for lo, hi, signal in ((0, ENC["ew2"], ew1_in), (ENC["ew2"], ENC["qkv"], ew2_in),
                                               (ENC["qkv"], ENC_W, qkv_in)):
                            sp.dma_start(w[:, half, lo:hi], d["w_encode"][e, :, lo:hi]).then_inc(signal[half], 16)
                            if lo == 0:
                                sp.dma_start(cols[:, half], d["cols"][e]).then_inc(vectors_in[half], 16)
                                for n, name in enumerate(("eb2", "vb")):
                                    for twice in range(2):
                                        sp.dma_start(rows[:, half, n, twice], d["rows"][e, ROWS[name]:ROWS[name] + DM]
                                                     .partition_broadcast(P)).then_inc(vectors_in[half], 16)
                    def store_part(b, side, part):
                        sp.wait_ge((part1, part2, part3)[part][side], b + 1)
                        sp.dma_start(d["qk"][2 * B * turn + b, side, part].rearrange("(c p) n -> p c n", p=P),
                                     parts[:, b % 2, side, part]).then_inc(qk_out[side][b % 2], 16)

                    def store_later_parts(b):
                        for side in (1, 0):
                            for part in (1, 2):
                                store_part(b, side, part)

                    for b in range(steps):
                        for side in (1, 0):
                            store_part(b, side, 0)
                        if b > 0:
                            store_later_parts(b - 1)
                        sp.wait_ge(v_kept, 2 * b + 2)
                        sp.dma_start(d["vx"][2 * B * turn + b], vx[:, b % 2].rearrange("p t h r -> p (t h r)")
                                     ).then_inc(vx_out[b % 2], 16)
                    store_later_parts(steps - 1)
                    for parity in range(2):
                        for side in range(2):
                            sp.wait_ge(qk_out[side][parity], steps // 2 * 48)
                        sp.wait_ge(vx_out[parity], steps // 2 * 16)
                    for half in range(2):
                        for signal, amount in ((ew1_in, 16), (ew2_in, 16), (qkv_in, 16), (vectors_in, 5 * 16)):
                            sp.wait_ge(signal[half], amount)

                @block.tensor
                def _(pe):
                    def encode1(b):
                        if b > 0:
                            pe.wait_ge(h1_kept, 2 * b)
                        if b % B == 0:
                            pe.wait_ge(ew1_in[b // B], 16)
                        for m in range(KH):
                            nc.tensor.matmul(bank[m][:], weight(b, "ew1", 0, m * P, P), core.xT[:, b % B * S:(b % B + 1) * S],
                                             start=True, stop=True).then_inc(h1_mm, 1)

                    def encode2(b):
                        pe.wait_ge(h1_kept, 2 * b + 2)
                        if b % B == 0:
                            pe.wait_ge(ew2_in[b // B], 16)
                        for pair in range(2):
                            if b > 0:
                                pe.wait_ge(h2_kept, 2 * (b - 1) + pair + 1)
                            for t in (2 * pair, 2 * pair + 1):
                                for k in range(KH):
                                    last = nc.tensor.matmul(bank[2 + pair][:, t % 2 * DM:(t % 2 + 1) * DM],
                                                            h1[:, b % 2, k, t * P:(t + 1) * P],
                                                            weight(b, "ew2", k, 0, DM), start=k == 0, stop=k == KH - 1)
                            last.then_inc(h2_mm, 1)

                    def project(b, side):
                        for c in range(KH):
                            if side == 0:
                                pe.wait_ge(k_kept, 2 * b + c + 1)
                            elif b > 0:
                                pe.wait_ge(q_kept, 2 * b - 1 + c)
                            for k in range(KH):
                                last = nc.tensor.matmul(bank[6 + c][:], weight(b, "qkv", k, side * DM + c * P, P),
                                                        hT[:, b % 2, k], start=k == 0, stop=k == KH - 1)
                            last.then_inc(qk_mm, 1)

                    encode1(0)
                    encode2(0)
                    for b in range(steps):
                        if b > 0:
                            pe.wait_ge(v_kept, 2 * b)
                        for t in range(BT):
                            pe.wait_ge(normed, BT * b + t + 1)
                            for k in range(KH):
                                last = nc.tensor.transpose(bank[4 + k][:, t * P:(t + 1) * P],
                                                           hn[:, b % 2, t, k * P:(k + 1) * P], core.ident[:])
                        last.then_inc(hn_turned, 1)
                        if b < steps - 1:
                            encode1(b + 1)
                        pe.wait_ge(hT_kept, 2 * b + 2)
                        if b % B == 0:
                            pe.wait_ge(qkv_in[b // B], 16)
                        project(b, 1)
                        if b < steps - 1:
                            encode2(b + 1)
                        project(b, 0)
                        for pair in range(2):
                            for t in (2 * pair, 2 * pair + 1):
                                for k in range(KH):
                                    last = nc.tensor.matmul(bank[4 + pair][:, t % 2 * DM:(t % 2 + 1) * DM],
                                                            hT[:, b % 2, k, t * P:(t + 1) * P],
                                                            weight(b, "qkv", k, 2 * DM, DM), start=k == 0, stop=k == KH - 1)
                            last.then_inc(v_mm, 1)

                @block.vector
                def _(dve):
                    def norm(b):
                        if b % B == 0:
                            half = b // B
                            dve.wait_ge(vectors_in[half], 5 * 16)
                            nc.vector.tensor_scalar(qbs[:, half], cols[:, half, COLS["qb"]:COLS["qb"] + KH],
                                                    float(DH) ** -0.5, None, ALU.mult).then_inc(qbs_done, 1)
                        for pair in range(2):
                            dve.wait_ge(h2_mm, 2 * b + pair + 1)
                            nc.vector.tensor_tensor(h2[:, b % 2, 2 * pair:2 * pair + 2],
                                                    bank[2 + pair][:].rearrange("p (t n) -> p t n", t=2), rows[:, b // B, 0],
                                                    ALU.add).then_inc(h2_kept, 1)
                        for t in range(BT):
                            dve.wait_ge(h2_kept, 2 * b + t // 2 + 1)
                            nc.vector.bn_stats(stats[:, t], h2[:, b % 2, t]).then_inc(stats_done, 1)
                        for t in range(BT):
                            dve.wait_ge(stats_done, BT * b + t + 1)
                            nc.vector.bn_aggr(mv[:, t], stats[:, t]).then_inc(mv_done, 1)
                        dve.wait_ge(mv_done, BT * (b + 1))
                        nc.vector.tensor_scalar(var[:], mv[:, :, 1], EPS, None, ALU.add).then_inc(var_done, 1)
                        dve.wait_ge(std_done, b + 1)
                        nc.vector.reciprocal(rstd[:], std[:]).then_inc(rstd_done, 1)
                        dve.wait_ge(rstd_done, b + 1)
                        for t in range(BT):
                            nc.vector.tensor_scalar(hn[:, b % 2, t], h2[:, b % 2, t], mv[:, t, 0:1], rstd[:, t:t + 1],
                                                    ALU.subtract, ALU.mult).then_inc(normed, 1)

                    def leave_rest(b, side):
                        dve.wait_ge(part1[side], b + 1)
                        if b > 0:
                            dve.wait_ge(part3[side], b)
                        nc.vector.tensor_tensor(rest[:, side], qk[:, side], parts[:, b % 2, side, 0], ALU.subtract
                                                ).then_inc(rested[side], 1)

                    def last_parts(b):
                        for side in (1, 0):
                            dve.wait_ge(part2[side], b + 1)
                            nc.vector.tensor_tensor(parts[:, b % 2, side, 2], rest[:, side], parts[:, b % 2, side, 1],
                                                    ALU.subtract).then_inc(part3[side], 1)

                    norm(0)
                    for b in range(steps):
                        for c in range(KH):
                            dve.wait_ge(qk_mm, 4 * b + c + 1)
                            if b > 0:
                                dve.wait_ge(rested[1], b)
                            nc.vector.tensor_scalar(qk[:, 1, c], bank[6 + c][:], col(b, "kb", c), None,
                                                    ALU.add).then_inc(k_kept, 1)
                        if b > 0:
                            last_parts(b - 1)
                        if b < steps - 1:
                            norm(b + 1)
                        else:
                            leave_rest(b, 1)
                        if b >= 2:
                            dve.wait_ge(vx_out[b % 2], b // 2 * 16)
                        for pair in range(2):
                            dve.wait_ge(v_mm, 2 * b + pair + 1)
                            nc.vector.tensor_tensor(
                                vx[:, b % 2, 2 * pair:2 * pair + 2, :, 0:DH].rearrange("p t h r -> p (t h) r"),
                                bank[4 + pair][:].rearrange("p (t r) -> p t r", r=DH),
                                rows[:, b // B, 1].rearrange("p t (h r) -> p (t h) r", r=DH), ALU.add).then_inc(v_kept, 1)
                        if b < steps - 1:
                            leave_rest(b, 1)
                        leave_rest(b, 0)
                    last_parts(steps - 1)

                @block.scalar
                def _(act):
                    def relu(b):
                        if b % B == 0:
                            act.wait_ge(vectors_in[b // B], 5 * 16)
                        for m in range(KH):
                            act.wait_ge(h1_mm, 2 * b + m + 1)
                            nc.scalar.activation(h1[:, b % 2, m], bank[m][:], ACT.Relu, bias=col(b, "eb1", m)
                                                 ).then_inc(h1_kept, 1)

                    def root(b):
                        act.wait_ge(var_done, b + 1)
                        nc.scalar.activation(std[:], var[:], ACT.Sqrt).then_inc(std_done, 1)

                    def first_part(b, side):
                        act.wait_ge((q_kept, k_kept)[side], 2 * b + 2)
                        if b >= 2:
                            act.wait_ge(qk_out[side][b % 2], b // 2 * 48)
                        nc.scalar.activation(parts[:, b % 2, side, 0], qk[:, side], ACT.Copy).then_inc(part1[side], 1)

                    def second_parts(b):
                        for side in (1, 0):
                            act.wait_ge(rested[side], b + 1)
                            nc.scalar.activation(parts[:, b % 2, side, 1], rest[:, side], ACT.Copy
                                                 ).then_inc(part2[side], 1)

                    relu(0)
                    root(0)
                    for b in range(steps):
                        act.wait_ge(hn_turned, b + 1)
                        for k in range(KH):
                            nc.scalar.activation(hT[:, b % 2, k], bank[4 + k][:], ACT.Identity, scale=col(b, "eg", k),
                                                 bias=col(b, "ebeta", k)).then_inc(hT_kept, 1)
                        if b < steps - 1:
                            relu(b + 1)
                        if b > 0:
                            second_parts(b - 1)
                        first_part(b, 1)
                        if b < steps - 1:
                            root(b + 1)
                        if b % B == 0:
                            act.wait_ge(qbs_done, b // B + 1)
                        for c in range(KH):
                            act.wait_ge(qk_mm, 4 * b + KH + c + 1)
                            if b > 0:
                                act.wait_ge(rested[0], b)
                            nc.scalar.activation(qk[:, 0, c], bank[6 + c][:], ACT.Identity, scale=float(DH) ** -0.5,
                                                 bias=qbs[:, b // B, c:c + 1]).then_inc(q_kept, 1)
                        first_part(b, 0)
                    second_parts(steps - 1)
            clear_signals(nc, [
                qbs_done, h1_mm, h1_kept, h2_mm, h2_kept, stats_done, mv_done, var_done, std_done, rstd_done,
                normed, hn_turned, hT_kept, qk_mm, q_kept, k_kept, v_mm, v_kept] + part1 + part2 + part3 + rested
                + qk_out[0] + qk_out[1] + vx_out + ew1_in + ew2_in + qkv_in + vectors_in)


PAIRS = ((0, 0), (0, 1), (0, 2), (1, 0), (1, 1), (2, 0))
KROWS = len(PAIRS) * DH
RING = 8


def experts_attend(core, d):
    nc, bank = core.nc, core.bank
    core.lstm = core.ctx.enter_context(ExitStack())
    core.wh = core.sb(core.lstm, "wh", [P, 2, E, KH, G4])
    (wh_in,) = core.sems("ba", "whin")
    with ExitStack() as ctx:
        w = core.sb(ctx, "bw", [P, ATT_W])
        cols = core.sb(ctx, "bcols", [P, COLS_W])
        lb = core.sb(ctx, "blb", [P, 2 * G4])
        qp = core.sb(ctx, "bqp", [KROWS + 3, NH, S], BF16)
        kp = core.sb(ctx, "bkp", [KROWS + 3, NH, S], BF16)
        vx = core.sb(ctx, "bvx", [P, BT, NH, DH + 1])
        pT = core.wh[:].rearrange("p w e k n -> p (w e k n)").rearrange(
            "p (r t s) -> p r t s", r=RING, t=BT)
        negmax = core.sb(ctx, "bnegmax", [P, NH, BT])
        maxparts = core.sb(ctx, "bmaxparts", [P, 2, BT, 3], BF16)
        rest = core.sb(ctx, "brest", [P, BT])
        ident16 = core.sb(ctx, "bident", [P, P], BF16)
        o = core.sb(ctx, "bo", [P, 4, S])
        inv = core.sb(ctx, "binv", [P, BT, NH])
        on = core.sb(ctx, "bon", [P, BT, NH, DH])
        oT = core.sb(ctx, "boT", [P, KH, S])
        aT = core.sb(ctx, "baT", [P, KH, S])
        zs = core.sb(ctx, "bzs", [P, 4, G4])
        (loaded, filled, scored, maxed, part1, part2, part3, rested, rows_mm, rows_kept, scored_t, exped, valued, o_kept,
         o_turned, inverted, on_done, on_turned, oT_kept, a_mm, a_kept, z_mm, z_kept) = core.sems(
            "ba", "loaded filled scored maxed part1 part2 part3 rested rowsmm rowskept scoredt exped valued okept "
                  "oturned inverted on onturned oTkept amm akept zmm zkept")
        qk_in = core.sems("ba", "qkin0 qkin1")
        (vx_in,) = core.sems("ba", "vxin")
        z_stored = core.sems("ba", "zstored0 zstored1 zstored2 zstored3")

        def load_heads(sp, slab, half):
            heads = slice(half * NH // 2, (half + 1) * NH // 2)
            for side, dst in ((0, qp), (1, kp)):
                for n, pair in enumerate(PAIRS):
                    src = d["qk"][slab, side, pair[side]].rearrange("(h r) n -> r h n", r=DH)
                    sp.dma_start(dst[n * DH:(n + 1) * DH, heads], src[:, heads]).then_inc(qk_in[half], 16)

        BESIDE, ALONE = (7,), (7, 5)
        HEADS_IN = 2 * len(PAIRS) * 16

        def product(pe, n, k, banks):
            t, q = divmod(n, 4)
            if k == 0:
                if n == 0:
                    pe.wait_ge(a_kept, KH)
                elif n >= len(banks):
                    pe.wait_ge(z_kept, n - len(banks) + 1)
            at = ATT["wi"] + (q // 2 * KH + k) * G4 + q % 2 * 512
            last = nc.tensor.matmul(bank[banks[n % len(banks)]][:], aT[:, k, t * P:(t + 1) * P], w[:, at:at + 512],
                                    start=k == 0, stop=k == KH - 1)
            if k == KH - 1:
                last.then_inc(z_mm, 1)

        def keep_product(dve, n, banks):
            dve.wait_ge(z_mm, n + 1)
            if n >= 8 and n % 2 == 0:
                dve.wait_ge(z_stored[n // 2 % 4], 16 * (n // 8))
            nc.vector.tensor_tensor(zs[:, (n // 2) % 4, n % 2 * 512:(n % 2 + 1) * 512],
                                    bank[banks[n % len(banks)]][:],
                                    lb[:, n % 4 * 512:(n % 4 + 1) * 512], ALU.add).then_inc(z_kept, 1)

        def store_product(sp, n, e, b):
            t, way = divmod(n, 2)
            sp.wait_ge(z_kept, 2 * n + 2)
            sp.dma_start(d["zx"][way, e, b, t * P:(t + 1) * P], zs[:, n % 4]).then_inc(z_stored[n % 4], 16)

        turn_banks = [bank[2], bank[3], bank[4], bank[7]]
        project_banks = [bank[7], bank[4]]

        def turn_values(pe):
            for qt in range(BT):
                for g in range(4):
                    last = nc.tensor.transpose(turn_banks[qt][:, g * P:(g + 1) * P], o[:, g, qt * P:(qt + 1) * P],
                                               core.ident[:])
                last.then_inc(o_turned, 1)

        def divide(dve):
            for qt in range(BT):
                heads = turn_banks[qt][:].rearrange("p (h r) -> p h r", r=32)
                dve.wait_ge(o_turned, qt + 1)
                nc.vector.reciprocal(inv[:, qt], heads[:, :, DH]).then_inc(inverted, 1)
                dve.wait_ge(inverted, qt + 1)
                nc.vector.tensor_tensor(on[:, qt], heads[:, :, 0:DH],
                                        inv[:, qt].unsqueeze(2).broadcast_to([P, NH, DH]), ALU.mult).then_inc(on_done, 1)

        def turn_divided(pe):
            for qt in range(BT):
                pe.wait_ge(on_done, max(qt + 1, 2))
                for k in range(KH):
                    last = nc.tensor.transpose(turn_banks[k][:, qt * P:(qt + 1) * P],
                                               on[:, qt, k * NH // KH:(k + 1) * NH // KH].rearrange("p h r -> p (h r)"),
                                               core.ident[:])
            last.then_inc(on_turned, 1)

        def keep_divided(act):
            act.wait_ge(on_turned, 1)
            for k in range(KH):
                nc.scalar.activation(oT[:, k], turn_banks[k][:], ACT.Copy).then_inc(oT_kept, 1)

        def project(pe):
            pe.wait_ge(oT_kept, KH)
            for m in range(KH):
                for k in range(KH):
                    at = ATT["aow"] + k * DM + m * P
                    last = nc.tensor.matmul(project_banks[m][:], w[:, at:at + P], oT[:, k], start=k == 0,
                                            stop=k == KH - 1)
                last.then_inc(a_mm, 1)

        def keep_projected(act):
            for m in range(KH):
                act.wait_ge(a_mm, m + 1)
                nc.scalar.activation(aT[:, m], project_banks[m][:], ACT.Identity,
                                     bias=cols[:, COLS["aob"] + m:COLS["aob"] + m + 1]).then_inc(a_kept, 1)

        def attend(e, b, products):
            with nc.Block() as block:
                @block.sync
                def _(sp):
                    if not products:
                        sp.dma_start(w[:], d["w_attend"][e]).then_inc(loaded, 16)
                        sp.dma_start(cols[:], d["cols"][e]).then_inc(loaded, 16)
                        sp.dma_start(lb[:], d["rows"][e, ROWS["lb"]:ROWS["lb"] + 2 * G4].partition_broadcast(P)
                                     ).then_inc(loaded, 16)
                    load_heads(sp, e * B + b, 1)
                    sp.dma_start(vx[:].rearrange("p t h r -> p (t h r)"), d["vx"][e * B + b]).then_inc(vx_in, 16)
                    if products:
                        for n in range(4):
                            store_product(sp, n, e, b - 1)
                    sp.wait_ge(scored_t, BT * NH // 2)
                    load_heads(sp, e * B + b + 1, 0)
                    if products:
                        for n in range(4, 8):
                            store_product(sp, n, e, b - 1)
                        for slot in z_stored:
                            sp.wait_ge(slot, 2 * 16)
                    sp.wait_ge(qk_in[0], HEADS_IN)
                    if not products:
                        sp.wait_ge(loaded, 48)

                @block.tensor
                def _(pe):
                    def score(h, qt):
                        if h == NH // 2 and qt == 0:
                            pe.wait_ge(qk_in[1], HEADS_IN)
                        if BT * h + qt >= 2:
                            pe.wait_ge(maxed, BT * h + qt - 1)
                        nc.tensor.matmul(bank[qt % 2][:], qp[0:KROWS, h, qt * P:(qt + 1) * P], kp[0:KROWS, h],
                                         start=True, stop=True).then_inc(scored, 1)

                    def turn_maxima(h):
                        pe.wait_ge(part3, h + 1)
                        if h > 0:
                            pe.wait_ge(rows_kept, h)
                        for qt in range(BT):
                            last = nc.tensor.matmul(bank[5][KROWS:KROWS + 3, qt * P:(qt + 1) * P],
                                                    maxparts[:, h % 2, qt], ident16[:], start=True, stop=True)
                        last.then_inc(rows_mm, 1)

                    def score_t(h, kt):
                        n = BT * h + kt
                        if kt == 0:
                            pe.wait_ge(rows_kept, h + 1)
                        if products and n == 2:
                            pe.wait_ge(a_kept, KH)
                        if n >= 3:
                            pe.wait_ge(exped, n - 2)
                        nc.tensor.matmul(bank[2 + n % 3][:], kp[:, h, kt * P:(kt + 1) * P], qp[:, h], start=True,
                                         stop=True).then_inc(scored_t, 1)

                    def values(g, kt):
                        if g == 0:
                            pe.wait_ge(vx_in, 16)
                        elif kt == 0:
                            pe.wait_ge(o_kept, g)
                        pe.wait_ge(exped, BT * (4 * g + 3) + kt + 1)
                        for c in range(4):
                            h = 4 * g + c
                            last = nc.tensor.matmul(bank[6][32 * c:32 * c + DH + 1, :], vx[:, kt, h],
                                                    pT[:, h % RING, kt], start=kt == 0, stop=kt == BT - 1)
                        last.then_inc(valued, 1)

                    for h in range(NH + 2):
                        if h < NH:
                            score(h, 0)
                            score(h, 1)
                        if products and h == 0:
                            turn_values(pe)
                        if products and h == 1:
                            turn_divided(pe)
                        if h >= 2:
                            for kt in range(3):
                                score_t(h - 2, kt)
                        if products and h >= 2:
                            product(pe, h - 2, 0, BESIDE)
                        if h < NH:
                            score(h, 2)
                            score(h, 3)
                        if 1 <= h <= NH:
                            turn_maxima(h - 1)
                        if products and h == 1:
                            project(pe)
                        if h >= 2:
                            score_t(h - 2, 3)
                        if h >= 6:
                            values((h - 6) // 4, (h - 6) % 4)
                        if products and h >= 2:
                            product(pe, h - 2, 1, BESIDE)
                    for kt in range(BT):
                        values(3, kt)

                @block.vector
                def _(dve):
                    def largest(h, qt):
                        dve.wait_ge(scored, BT * h + qt + 1)
                        nc.vector.tensor_reduce(negmax[:, h, qt:qt + 1], bank[qt % 2][:], AX.X, ALU.max,
                                                negate=True).then_inc(maxed, 1)

                    def split(h):
                        parts = [maxparts[:, h % 2, :, n] for n in range(3)]
                        dve.wait_ge(maxed, BT * (h + 1))
                        if h >= 2:
                            dve.wait_ge(rows_mm, h - 1)
                        nc.vector.tensor_copy(parts[0], negmax[:, h]).then_inc(part1, 1)
                        dve.wait_ge(part1, h + 1)
                        if h > 0:
                            dve.wait_ge(part3, h)
                        nc.vector.tensor_tensor(rest[:], negmax[:, h], parts[0], ALU.subtract).then_inc(rested, 1)
                        dve.wait_ge(rested, h + 1)
                        nc.vector.tensor_copy(parts[1], rest[:]).then_inc(part2, 1)
                        dve.wait_ge(part2, h + 1)
                        nc.vector.tensor_tensor(parts[2], rest[:], parts[1], ALU.subtract).then_inc(part3, 1)

                    for h in range(NH + 2):
                        if products and h >= 3:
                            keep_product(dve, h - 3, BESIDE)
                        if h < NH:
                            largest(h, 0)
                            largest(h, 1)
                            if products and h == 0:
                                divide(dve)
                            largest(h, 2)
                            largest(h, 3)
                            split(h)
                    if products:
                        keep_product(dve, NH - 1, BESIDE)

                @block.scalar
                def _(act):
                    def keep_rows(h):
                        act.wait_ge(rows_mm, h + 1)
                        nc.scalar.activation(qp[KROWS:KROWS + 3, h], bank[5][KROWS:KROWS + 3, :], ACT.Copy
                                             ).then_inc(rows_kept, 1)

                    def exponent(h, kt):
                        n = BT * h + kt
                        act.wait_ge(scored_t, n + 1)
                        if h >= RING:
                            act.wait_ge(valued, (h - RING) // 4 * 4 + kt + 1)
                        nc.scalar.activation(pT[:, h % RING, kt], bank[2 + n % 3][:], ACT.Exp).then_inc(exped, 1)

                    def keep_values(g):
                        act.wait_ge(valued, 4 * (g + 1))
                        nc.scalar.activation(o[:, g], bank[6][:], ACT.Copy).then_inc(o_kept, 1)

                    if products:
                        keep_divided(act)
                    for h in range(NH + 2):
                        if products and h == 2:
                            keep_projected(act)
                        if h >= 10 and h % 4 == 2:
                            keep_values(h // 4 - 2)
                        if h >= 2:
                            for kt in range(3):
                                exponent(h - 2, kt)
                        if 1 <= h <= NH:
                            keep_rows(h - 1)
                        if h >= 2:
                            exponent(h - 2, 3)
                    keep_values(2)
                    keep_values(3)
            clear_signals(nc, [loaded, scored, maxed, part1, part2, part3, rested, rows_mm, rows_kept, scored_t, exped,
                               valued, o_kept, o_turned, inverted, on_done, on_turned, oT_kept, a_mm, a_kept, z_mm,
                               z_kept, vx_in] + qk_in + z_stored)

        with nc.Block() as block:
            @block.sync
            def _(sp):
                sp.dma_start(d["qk"][E * B], d["qk"][0]).then_inc(filled, 16)
                load_heads(sp, 0, 0)
                sp.wait_ge(qk_in[0], HEADS_IN)
                sp.wait_ge(filled, 16)

            @block.vector
            def _(dve):
                nc.vector.memset(bank[6][:], 0.0)
                nc.vector.memset(kp[KROWS:KROWS + 3], 1.0)
                nc.vector.tensor_copy(ident16[:], core.ident[:])
        clear_signals(nc, qk_in)
        def expert(e, final):
            attend(e, 0, False)
            with nc.Fori(1, B) as b:
                attend(e, b, True)
            with nc.Block() as block:
                @block.scalar
                def _(act):
                    keep_divided(act)
                    keep_projected(act)

                @block.tensor
                def _(pe):
                    turn_values(pe)
                    turn_divided(pe)
                    project(pe)
                    for n in range(NH):
                        product(pe, n, 0, ALONE)
                        product(pe, n, 1, ALONE)

                @block.vector
                def _(dve):
                    divide(dve)
                    for n in range(NH):
                        keep_product(dve, n, ALONE)

                @block.sync
                def _(sp):
                    if final:
                        sp.dma_start(core.wh[:], d["wh"]).then_inc(wh_in, 16)
                    for n in range(8):
                        store_product(sp, n, e, B - 1)
                    for slot in z_stored:
                        sp.wait_ge(slot, 2 * 16)
                    if final:
                        sp.wait_ge(wh_in, 16)
            clear_signals(nc, [o_turned, inverted, on_done, on_turned, oT_kept, a_mm, a_kept, z_mm, z_kept] + z_stored)

        with nc.Fori(0, E - 1) as e:
            expert(e, False)
        expert(E - 1, True)


STEPS = 4
PER_TURN = 2 * STEPS


def recurrence(core, d):
    nc, bank = core.nc, core.bank
    turns = S // PER_TURN
    with ExitStack() as ctx:
        wh = core.wh
        zx = core.sb(ctx, "lzx", [P, 2, 2, STEPS, G4])
        hs = core.sb(ctx, "lhs", [P, 2, 2, STEPS, DM])
        z = core.sb(ctx, "lz", [P, 2, KH, 4, P])
        gate = core.sb(ctx, "lgate", [P, 2, KH, 3, P])
        gc = core.sb(ctx, "lgc", [P, 2, KH, 2, P])
        prod = core.sb(ctx, "lprod", [P, 2, KH, 2, P])
        tc = core.sb(ctx, "ltc", [P, 2, KH, P])
        zeros = core.sb(ctx, "lzeros", [P, G4])
        hT = core.sb(ctx, "lhT", [P, 2, KH, E, B])
        zeros_ready, cleared_v, cleared_a = core.sems("ls", "zeros clearedv cleareda")

        def pair(name):
            return core.sems("ls", f"{name}0 {name}1")

        made, added, gated, celled, tanhed, ready, turned, kept = (
            pair(n) for n in ("made", "added", "gated", "celled", "tanhed", "ready", "turned", "kept"))
        multiplied = pair("multiplied")
        zx_in = [pair("zxin0"), pair("zxin1")]
        hs_out = [pair("hsout0"), pair("hsout1")]

        AHEAD = KH

        def z_bank(way, j):
            return bank[2 * way + j]

        def turn_bank(way, j):
            return bank[4 + 2 * way + j]

        def rows_of(e):
            return slice(32 * e, 32 * e + B)

        def first_time(way, turn, buf):
            n = 2 * turn + buf
            return n * STEPS if way == 0 else n * -STEPS + (S - STEPS)

        def at(way, i):
            return i if way == 0 else STEPS - 1 - i

        def load_zx(sp, way, turn, buf):
            for e in range(E):
                sp.dma_start(zx[rows_of(e), way, buf], d["zx"][way, e, :, bass.ds(first_time(way, turn, buf), STEPS)]
                             ).then_inc(zx_in[way][buf], 16)

        with nc.Block() as block:
            @block.sync
            def _(sp):
                for buf in range(2):
                    for way in range(2):
                        sp.wait_ge((cleared_v, cleared_a)[buf], way + 1)
                        load_zx(sp, way, 0, buf)

            @block.vector
            def _(dve):
                nc.vector.memset(zeros[:], 0.0).then_inc(zeros_ready, 1)
                for way in range(2):
                    nc.vector.memset(zx[:, way, 0], 0.0).then_inc(cleared_v, 1)
                    nc.vector.memset(hs[:, way, 1, at(way, STEPS - 1)], 0.0)
                nc.vector.memset(hT[:], 0.0)
                nc.vector.memset(gc[:], 0.0)
                for way in range(2):
                    dve.sem_inc(added[way], AHEAD)
                    dve.sem_inc(ready[way], AHEAD)
                    for buf in range(2):
                        dve.sem_inc(hs_out[way][buf], 1)

            @block.scalar
            def _(act):
                act.wait_ge(zeros_ready, 1)
                for way in range(2):
                    nc.scalar.activation(zx[:, way, 1], zeros[:].unsqueeze(1).broadcast_to([P, STEPS, G4]),
                                         ACT.Copy).then_inc(cleared_a, 1)
                for n in range(4):
                    nc.scalar.activation(bank[n][:], zeros[:, 0:512], ACT.Copy)

        with nc.Block() as block:
            @block.tensor
            def _(pe):
                def products(way, done, k, j):
                    if j == 0:
                        pe.wait_ge(kept[way], done + k + 1)
                    if k == 0:
                        pe.wait_ge(added[way], done + j + 1)
                    for e in range(E):
                        last = nc.tensor.matmul(z_bank(way, j)[rows_of(e), :], hT[:, way, k, e],
                                                wh[:, way, e, k, j * 512:(j + 1) * 512],
                                                start=k == 0, stop=k == KH - 1)
                    if k == KH - 1:
                        last.then_inc(made[way], 1)

                def transpose(way, i, done, j):
                    pe.wait_ge(ready[way], done + AHEAD + j + 1)
                    nc.tensor.transpose(turn_bank(way, j)[:, 0:P],
                                        hs[:, way, i // STEPS, at(way, i % STEPS), j * P:(j + 1) * P],
                                        core.ident[:]).then_inc(turned[way], 1)

                transpose(0, PER_TURN - 1, -AHEAD, 0)
                with pe.Fori(0, turns) as turn:
                    for i in range(PER_TURN):
                        for way in range(2):
                            done = 2 * PER_TURN * turn + 2 * i
                            products(way, done, 0, 0)
                            transpose(way, (i - 1) % PER_TURN, done - AHEAD, 1)
                            products(way, done, 0, 1)
                            products(way, done, 1, 0)
                            if way == 0:
                                transpose(1, (i - 1) % PER_TURN, done - AHEAD, 0)
                            else:
                                transpose(0, i, done, 0)
                            products(way, done, 1, 1)
                transpose(0, PER_TURN - 1, 2 * S - 2, 1)

            @block.vector
            def _(dve):
                def keep(way, done, j):
                    dve.wait_ge(turned[way], done + AHEAD + j + 1)
                    nc.vector.tensor_copy(hT[:, way, j], turn_bank(way, j)[:, 0:P].rearrange(
                        "p (e b) -> p e b", e=E)[:, :, 0:B]).then_inc(kept[way], 1)

                for j in range(KH):
                    keep(0, -AHEAD, j)
                with dve.Fori(0, turns) as turn:
                    for i in range(PER_TURN):
                        buf, done = i // STEPS, 2 * PER_TURN * turn + 2 * i
                        for way in range(2):
                            here = at(way, i % STEPS)
                            if i % STEPS == 0:
                                dve.wait_ge(zx_in[way][buf], 64 * turn + 64)
                                dve.wait_ge(hs_out[way][buf], 64 * turn + 1)

                            def add(j):
                                dve.wait_ge(made[way], done + j + 1)
                                nc.vector.tensor_tensor(z[:, way, j].rearrange("p g n -> p (g n)"), z_bank(way, j)[:],
                                                        zx[:, way, buf, here, j * 512:(j + 1) * 512],
                                                        ALU.add).then_inc(added[way], 1)

                            def cell(j):
                                dve.wait_ge(gated[way], done + j + 1)
                                nc.vector.tensor_tensor(prod[:, way, j], gate[:, way, j, 0:2], gc[:, way, j],
                                                        ALU.mult).then_inc(multiplied[way], 1)
                                dve.wait_ge(multiplied[way], done + j + 1)
                                nc.vector.tensor_tensor(gc[:, way, j, 1], prod[:, way, j, 0], prod[:, way, j, 1],
                                                        ALU.add).then_inc(celled[way], 1)

                            def state(j):
                                dve.wait_ge(tanhed[way], done + j + 1)
                                nc.vector.tensor_tensor(hs[:, way, buf, here, j * P:(j + 1) * P], gate[:, way, j, 2],
                                                        tc[:, way, j], ALU.mult).then_inc(ready[way], 1)

                            other = done - AHEAD if way == 0 else done
                            keep(1 - way, other, 0)
                            add(0)
                            add(1)
                            cell(0)
                            keep(1 - way, other, 1)
                            cell(1)
                            state(0)
                            state(1)

            @block.scalar
            def _(act):
                with act.Fori(0, turns) as turn:
                    for i in range(PER_TURN):
                        done = 2 * PER_TURN * turn + 2 * i
                        for way in range(2):
                            for j in range(KH):
                                act.wait_ge(added[way], AHEAD + done + j + 1)
                                nc.scalar.activation(gate[:, way, j], z[:, way, j, 0:3], ACT.Sigmoid)
                                nc.scalar.activation(gc[:, way, j, 0], z[:, way, j, 3], ACT.Tanh).then_inc(gated[way], 1)
                            for j in range(KH):
                                act.wait_ge(celled[way], done + j + 1)
                                nc.scalar.activation(tc[:, way, j], gc[:, way, j, 1], ACT.Tanh).then_inc(tanhed[way], 1)

            @block.sync
            def _(sp):
                def store_and_load(turn, more):
                    for buf in range(2):
                        for way in range(2):
                            steps = 2 * PER_TURN * turn + 2 * STEPS * (buf + 1)
                            sp.wait_ge(ready[way], steps + AHEAD)
                            for e in range(E):
                                sp.dma_start(d["hs"][way, e, :, bass.ds(first_time(way, turn, buf), STEPS)],
                                             hs[rows_of(e), way, buf]).then_inc(hs_out[way][buf], 16)
                            if more:
                                load_zx(sp, way, turn + 1, buf)

                with sp.Fori(0, turns - 1) as turn:
                    store_and_load(turn, True)
                store_and_load(turns - 1, False)
                for buf in range(2):
                    for way in range(2):
                        sp.wait_ge(hs_out[way][buf], 64 * turns + 1)

    core.lstm.close()


def experts_after(core, d):
    nc, bank = core.nc, core.bank
    STEPS_IN_TURN = 2 * B
    with ExitStack() as ctx:
        w = core.sb(ctx, "cw", [P, 2, POST_W])
        cols = core.sb(ctx, "ccols", [P, 2, COLS_W])
        rows = core.sb(ctx, "crows", [P, 2, 3 * D])
        mem = core.sb(ctx, "cmem", [P, 2, 2, BT, DM])
        memT = core.sb(ctx, "cmemT", [P, 4, S])
        hid = core.sb(ctx, "chid", [P, 4, S])
        gt = core.sb(ctx, "cgt", [P, 4, S])
        g = core.sb(ctx, "cg", [P, KH, S])
        d1 = core.sb(ctx, "cd1", [P, KH, S])
        y = core.sb(ctx, "cy", [P, BT, D])
        yn = core.sb(ctx, "cyn", [P, BT, D])
        yg = core.sb(ctx, "cyg", [P, BT, D])
        yb = core.sb(ctx, "cyb", [P, BT, D])
        wt = core.sb(ctx, "cwt", [P, 2, TILES])
        stats = core.sb(ctx, "cstats", [P, BT, 6])
        mv = core.sb(ctx, "cmv", [P, BT, 2])
        var = core.sb(ctx, "cvar", [P, BT])
        std = core.sb(ctx, "cstd", [P, BT])
        rstd = core.sb(ctx, "crstd", [P, BT])
        (mem_turned, turn_kept_v, turn_kept_a, hid_mm, hid_kept, gate_mm, gate_kept, product, d1_mm, d1_kept, y_mm,
         y_kept, weighted, stats_done, mv_done, var_done, std_done, rstd_done, normed, gained, shifted, summed
         ) = core.sems(
            "ea", "memturned turnkeptv turnkepta hidmm hidkept gatemm gatekept product d1mm d1kept ymm ykept weighted "
                  "stats mv var std rstd normed gained shifted summed")
        mem_in = [core.sems("ea", "mem0f mem0b"), core.sems("ea", "mem1f mem1b")]
        sw_in, tw_in, rest_in, vectors_in = (core.sems("ea", f"{n}0 {n}1") for n in ("sw", "tw", "rest", "vec"))

        def weight(s, name, part, m):
            width = D if name == "dw2" else DM
            at = POST[name] + part * width + m * P
            return w[:, s // B, at:at + P]

        def col(s, name, part):
            return cols[:, s // B, COLS[name] + part:COLS[name] + part + 1]

        def row(s, name):
            at = ROWS[name] - ROWS["db2"]
            return rows[:, s // B, at:at + D].unsqueeze(1).broadcast_to([P, BT, D])

        with nc.Fori(0, E // 2) as turn:
            with nc.Block() as block:
                @block.sync
                def _(sp):
                    def load_states(s):
                        for way in range(2):
                            sp.dma_start(mem[:, s % 2, way], d["hs"][way, 2 * turn + s // B, s % B]
                                         .rearrange("(t p) u -> p t u", p=P)).then_inc(mem_in[s % 2][way], 16)

                    def load_weights(half, lo, hi, signal):
                        sp.dma_start(w[:, half, lo:hi], d["w_after"][2 * turn + half, :, lo:hi]).then_inc(signal[half], 16)

                    def load_vectors(half):
                        sp.dma_start(cols[:, half], d["cols"][2 * turn + half]).then_inc(vectors_in[half], 16)
                        sp.dma_start(rows[:, half], d["rows"][2 * turn + half, ROWS["db2"]:ROWS_W].partition_broadcast(P)
                                     ).then_inc(vectors_in[half], 16)

                    load_states(0)
                    load_weights(0, 0, POST["tw1"], sw_in)
                    load_vectors(0)
                    load_weights(0, POST["tw1"], POST["sw2"], tw_in)
                    load_weights(0, POST["sw2"], POST_W, rest_in)
                    load_states(1)
                    load_weights(1, 0, POST["tw1"], sw_in)
                    load_weights(1, POST["tw1"], POST["sw2"], tw_in)
                    load_weights(1, POST["sw2"], POST_W, rest_in)
                    load_vectors(1)
                    for s in range(2, STEPS_IN_TURN):
                        sp.wait_ge(mem_turned, 4 * (s - 1))
                        load_states(s)
                    for half in range(2):
                        for signal, amount in ((sw_in, 16), (tw_in, 16), (rest_in, 16), (vectors_in, 32)):
                            sp.wait_ge(signal[half], amount)
                        for way in range(2):
                            sp.wait_ge(mem_in[half][way], 16 * STEPS_IN_TURN // 2)

                @block.tensor
                def _(pe):
                    def transposes(s):
                        for k in range(4):
                            pe.wait_ge(mem_in[s % 2][k // 2], 16 * (s // 2 + 1))
                            if k == 3:
                                pe.wait_ge(turn_kept_v, 2 * s + 1)
                            elif s > 0:
                                pe.wait_ge(hid_kept, 4 * (s - 1) + k + 2)
                            for t in range(BT):
                                last = nc.tensor.transpose(bank[5 + k % 3][:, t * P:(t + 1) * P],
                                                           mem[:, s % 2, k // 2, t, k % 2 * P:(k % 2 + 1) * P],
                                                           core.ident[:])
                            last.then_inc(mem_turned, 1)

                    def hidden(s):
                        pe.wait_ge(turn_kept_v, 2 * s + 2)
                        pe.wait_ge(turn_kept_a, 2 * s + 2)
                        if s > 1:
                            pe.wait_ge(y_kept, s - 1)
                        for m in range(4):
                            if s % B == 0 and m % 2 == 0:
                                pe.wait_ge((sw_in, tw_in)[m // 2][s // B], 16)
                            for k in range(4):
                                last = nc.tensor.matmul(bank[4 + m][:], weight(s, ("sw1", "tw1")[m // 2], k, m % 2),
                                                        memT[:, k], start=k == 0, stop=k == 3)
                            last.then_inc(hid_mm, 1)

                    def gates(s):
                        if s % B == 0:
                            pe.wait_ge(rest_in[s // B], 16)
                        for m in range(4):
                            if m >= 2 and s > 0:
                                pe.wait_ge(d1_kept, 2 * s + m - 3)
                            for k in range(KH):
                                pe.wait_ge(hid_kept, 4 * s + m // 2 * 2 + k + 1)
                                last = nc.tensor.matmul(bank[(m + 2) % 4][:], weight(s, ("sw2", "tw2")[m // 2], k, m % 2),
                                                        hid[:, m // 2 * 2 + k], start=k == 0, stop=k == KH - 1)
                            last.then_inc(gate_mm, 1)

                    def decode1(s):
                        pe.wait_ge(product, KH * (s + 1))
                        for m in range(KH):
                            for k in range(KH):
                                last = nc.tensor.matmul(bank[m][:], weight(s, "dw1", k, m), g[:, k], start=k == 0,
                                                        stop=k == KH - 1)
                            last.then_inc(d1_mm, 1)

                    def decode2(s):
                        pe.wait_ge(hid_kept, min(4 * (s + 1) + 1, 4 * STEPS_IN_TURN))
                        pe.wait_ge(d1_kept, KH * (s + 1))
                        for t in range(BT):
                            for k in range(KH):
                                last = nc.tensor.matmul(bank[4][:, t * D:(t + 1) * D], d1[:, k, t * P:(t + 1) * P],
                                                        weight(s, "dw2", k, 0), start=k == 0, stop=k == KH - 1)
                        last.then_inc(y_mm, 1)

                    transposes(0)
                    for s in range(STEPS_IN_TURN):
                        hidden(s)
                        if s > 0:
                            decode1(s - 1)
                        gates(s)
                        if s > 0:
                            decode2(s - 1)
                        if s < STEPS_IN_TURN - 1:
                            transposes(s + 1)
                    decode1(STEPS_IN_TURN - 1)
                    pe.wait_ge(y_kept, STEPS_IN_TURN - 1)
                    decode2(STEPS_IN_TURN - 1)

                @block.scalar
                def _(act):
                    def keep_turned(s):
                        for k in (1, 3):
                            act.wait_ge(mem_turned, 4 * s + k + 1)
                            nc.scalar.activation(memT[:, k], bank[5 + k % 3][:], ACT.Copy).then_inc(turn_kept_a, 1)

                    def decode1(s):
                        for m in range(KH):
                            act.wait_ge(d1_mm, KH * s + m + 1)
                            nc.scalar.activation(d1[:, m], bank[m][:], ACT.Relu, bias=col(s, "db1", m)).then_inc(d1_kept, 1)

                    def root(s):
                        act.wait_ge(var_done, s + 1)
                        nc.scalar.activation(std[:], var[:], ACT.Sqrt).then_inc(std_done, 1)

                    keep_turned(0)
                    for s in range(STEPS_IN_TURN):
                        if s % B == 0:
                            act.wait_ge(vectors_in[s // B], 32)
                        for m in range(4):
                            act.wait_ge(hid_mm, 4 * s + m + 1)
                            nc.scalar.activation(hid[:, m], bank[4 + m][:], ACT.Relu,
                                                 bias=col(s, ("sb1", "tb1")[m // 2], m % 2)).then_inc(hid_kept, 1)
                        if s > 0:
                            decode1(s - 1)
                        for m in range(4):
                            act.wait_ge(gate_mm, 4 * s + m + 1)
                            nc.scalar.activation(gt[:, m], bank[(m + 2) % 4][:], (ACT.Sigmoid, ACT.Tanh)[m // 2],
                                                 bias=col(s, ("sb2", "tb2")[m // 2], m % 2)).then_inc(gate_kept, 1)
                        if s < STEPS_IN_TURN - 1:
                            keep_turned(s + 1)
                        if s > 0:
                            root(s - 1)
                    decode1(STEPS_IN_TURN - 1)
                    root(STEPS_IN_TURN - 1)

                @block.vector
                def _(dve):
                    def keep_turned(s):
                        for k in (0, 2):
                            dve.wait_ge(mem_turned, 4 * s + k + 1)
                            nc.vector.tensor_copy(memT[:, k], bank[5 + k % 3][:]).then_inc(turn_kept_v, 1)

                    def keep_decoded(s):
                        dve.wait_ge(y_mm, s + 1)
                        if s > 0:
                            dve.wait_ge(normed, BT * s)
                        nc.vector.tensor_tensor(y[:], bank[4][:].rearrange("p (t n) -> p t n", t=BT), row(s, "db2"),
                                                ALU.add).then_inc(y_kept, 1)

                    def norm_and_sum(s):
                        dve.wait_ge(y_kept, s + 1)
                        for t in range(BT):
                            nc.vector.bn_stats(stats[:, t], y[:, t]).then_inc(stats_done, 1)
                        for t in range(BT):
                            dve.wait_ge(stats_done, BT * s + t + 1)
                            nc.vector.bn_aggr(mv[:, t], stats[:, t]).then_inc(mv_done, 1)
                        dve.wait_ge(mv_done, BT * (s + 1))
                        nc.vector.tensor_scalar(var[:], mv[:, :, 1], EPS, None, ALU.add).then_inc(var_done, 1)
                        dve.wait_ge(std_done, s + 1)
                        nc.vector.reciprocal(rstd[:], std[:]).then_inc(rstd_done, 1)
                        dve.wait_ge(rstd_done, s + 1)
                        if s > 0:
                            dve.wait_ge(gained, s)
                        for t in range(BT):
                            nc.vector.tensor_scalar(yn[:, t], y[:, t], mv[:, t, 0:1], rstd[:, t:t + 1],
                                                    ALU.subtract, ALU.mult).then_inc(normed, 1)
                        dve.wait_ge(normed, BT * (s + 1))
                        if s > 0:
                            dve.wait_ge(shifted, s)
                        nc.vector.tensor_tensor(yg[:], yn[:], row(s, "dg"), ALU.mult).then_inc(gained, 1)
                        dve.wait_ge(gained, s + 1)
                        if s > 0:
                            dve.wait_ge(summed, BT * s)
                        nc.vector.tensor_tensor(yb[:], yg[:], row(s, "dbeta"), ALU.add).then_inc(shifted, 1)
                        dve.wait_ge(shifted, s + 1)
                        for t in range(BT):
                            tile = s % B * BT + t
                            if s >= B:
                                dve.wait_ge(summed, BT * (s - B) + t + 1)
                            nc.vector.scalar_tensor_tensor(
                                out=core.h[:, tile], in0=yb[:, t], scalar=wt[:, s // B, tile:tile + 1],
                                in1=core.h[:, tile], op0=ALU.mult, op1=ALU.add).then_inc(summed, 1)

                    for half in range(2):
                        nc.vector.tensor_copy(wt[:, half], core.route[:, :, 2 * turn + half]).then_inc(weighted, 1)
                    keep_turned(0)
                    dve.wait_ge(weighted, 2)
                    for half in range(2):
                        dve.wait_ge(vectors_in[half], 32)
                    for s in range(STEPS_IN_TURN):
                        if s > 0:
                            dve.wait_ge(product, KH * s)
                        for m in range(KH):
                            dve.wait_ge(gate_kept, 4 * s + KH + m + 1)
                            nc.vector.tensor_tensor(g[:, m], gt[:, m], gt[:, KH + m], ALU.mult).then_inc(product, 1)
                        if s > 0:
                            keep_decoded(s - 1)
                        if s < STEPS_IN_TURN - 1:
                            keep_turned(s + 1)
                        if s > 0:
                            norm_and_sum(s - 1)
                    keep_decoded(STEPS_IN_TURN - 1)
                    norm_and_sum(STEPS_IN_TURN - 1)
            clear_signals(nc, [mem_turned, turn_kept_v, turn_kept_a, hid_mm, hid_kept, gate_mm, gate_kept, product, d1_mm,
                               d1_kept, y_mm, y_kept, weighted, stats_done, mv_done, var_done, std_done, rstd_done,
                               normed, gained, shifted, summed] + mem_in[0] + mem_in[1] + sw_in + tw_in + rest_in
                          + vectors_in)


def state_space(core, d):
    nc, bank = core.nc, core.bank
    PAIRS = B // 2
    with ExitStack() as ctx:
        bT = core.sb(ctx, "sbT", [P, NST])
        cT = core.sb(ctx, "scT", [P, D])
        alog = core.sb(ctx, "salog", [P, 1])
        a = core.sb(ctx, "sa", [P, 1])
        nega = core.sb(ctx, "snega", [P, 1])
        dtw = core.sb(ctx, "sdtw", [P, 1])
        dtw_wide = core.sb(ctx, "sdtww", [P, NST])
        dtb = core.sb(ctx, "sdtb", [P, 1])
        drow = core.sb(ctx, "sdrow", [P, D])
        gamma = core.sb(ctx, "sgamma", [P, D])
        beta = core.sb(ctx, "sbeta", [P, D])
        sig = core.sb(ctx, "ssig", [P, PAIRS, S])
        dt = core.sb(ctx, "sdt", [P, PAIRS, S])
        da = core.sb(ctx, "sda", [P, PAIRS, S])
        dbu = core.sb(ctx, "sdbu", [P, PAIRS, S])
        st = core.sb(ctx, "sst", [P, PAIRS, S])
        dx = core.sb(ctx, "sdx", [P, TILES, D])
        y = core.sb(ctx, "sy", [P, TILES, D])
        yn = core.sb(ctx, "syn", [P, TILES, D])
        yg = core.sb(ctx, "syg", [P, TILES, D])
        yb = core.sb(ctx, "syb", [P, TILES, D])
        stats = core.sb(ctx, "sstats", [P, TILES, 6])
        mv = core.sb(ctx, "smv", [P, TILES, 2])
        var = core.sb(ctx, "svar", [P, TILES])
        std = core.sb(ctx, "sstd", [P, TILES])
        rstd = core.sb(ctx, "srstd", [P, TILES])
        (loaded, a_exp, a_ready, wide_ready, dt_mm, u_mm, sig_done, dt_done, da_done, dbu_done, scanned, dx_done, y_mm,
         y_kept, stats_done, mv_done, var_done, std_done, rstd_done, normed, gained, shifted) = core.sems(
            "ss", "loaded aexp aready wide dtmm umm sig dt da dbu scanned dx ymm ykept stats mv var std rstd normed "
                  "gained shifted")
        with nc.Block() as block:
            @block.sync
            def _(sp):
                for dst, src in ((bT, d["B_T"]), (dtw, d["dt_w"]), (alog, d["A_log"]), (cT, d["C_T"]),
                                 (dtb, d["dt_b"].partition_broadcast(P)), (drow, d["D_vec"].partition_broadcast(P)),
                                 (gamma, d["gamma"].partition_broadcast(P)), (beta, d["beta"].partition_broadcast(P))):
                    sp.dma_start(dst[:], src).then_inc(loaded, 16)

            @block.tensor
            def _(pe):
                pe.wait_ge(loaded, 8 * 16)
                pe.wait_ge(wide_ready, 1)
                for p in range(PAIRS):
                    for half in range(2):
                        b = 2 * p + half
                        r = slice(half * NST, (half + 1) * NST)
                        x = core.xT[:, b * S:(b + 1) * S]
                        nc.tensor.matmul(bank[p][r, :], dtw_wide[:], x, start=True, stop=True).then_inc(dt_mm, 1)
                        nc.tensor.matmul(bank[2 + p][r, :], bT[:], x, start=True, stop=True).then_inc(u_mm, 1)
                for t in range(TILES):
                    b = t // BT
                    pe.wait_ge(scanned, b // 2 + 1)
                    r = slice(b % 2 * NST, (b % 2 + 1) * NST)
                    last = nc.tensor.matmul(bank[4 + b][:, t % BT * D:(t % BT + 1) * D],
                                            st[r, b // 2, t % BT * P:(t % BT + 1) * P], cT[r, :], start=True, stop=True)
                    if t % BT == BT - 1:
                        last.then_inc(y_mm, 1)

            @block.scalar
            def _(act):
                act.wait_ge(loaded, 8 * 16)
                nc.scalar.activation(a[:], alog[:], ACT.Exp).then_inc(a_exp, 1)
                for p in range(PAIRS):
                    act.wait_ge(dt_mm, 2 * p + 2)
                    nc.scalar.activation(sig[:, p], bank[p][:], ACT.Sigmoid, bias=dtb[:, 0:1]).then_inc(sig_done, 1)
                act.wait_ge(a_ready, 1)
                for p in range(PAIRS):
                    act.wait_ge(dt_done, p + 1)
                    nc.scalar.activation(da[:, p], dt[:, p], ACT.Exp, scale=nega[:, 0:1]).then_inc(da_done, 1)
                act.wait_ge(var_done, 1)
                nc.scalar.activation(std[:], var[:], ACT.Sqrt).then_inc(std_done, 1)

            @block.vector
            def _(dve):
                def wide(v, n=TILES):
                    return v[:].unsqueeze(1).broadcast_to([P, n, D])

                dve.wait_ge(loaded, 8 * 16)
                nc.vector.tensor_copy(dtw_wide[:], dtw[:, 0:1].broadcast_to([P, NST])).then_inc(wide_ready, 1)
                dve.wait_ge(a_exp, 1)
                nc.vector.tensor_scalar(nega[:], a[:], -1.0, None, ALU.mult).then_inc(a_ready, 1)
                nc.vector.tensor_tensor(dx[:], core.xn[:], wide(drow), ALU.mult).then_inc(dx_done, 1)
                for p in range(PAIRS):
                    dve.wait_ge(sig_done, p + 1)
                    nc.vector.tensor_scalar(dt[:, p], sig[:, p], 0.1 - 0.001, 0.001, ALU.mult, ALU.add).then_inc(dt_done, 1)
                for p in range(PAIRS):
                    dve.wait_ge(dt_done, p + 1)
                    dve.wait_ge(u_mm, 2 * p + 2)
                    nc.vector.tensor_tensor(dbu[:, p], bank[2 + p][:], dt[:, p], ALU.mult).then_inc(dbu_done, 1)
                for p in range(PAIRS):
                    dve.wait_ge(da_done, p + 1)
                    dve.wait_ge(dbu_done, p + 1)
                    nc.vector.tensor_tensor_scan(st[:, p], da[:, p], dbu[:, p], 0.0, ALU.mult, ALU.add
                                                 ).then_inc(scanned, 1)
                dve.wait_ge(dx_done, 1)
                for b in range(B):
                    dve.wait_ge(y_mm, b + 1)
                    nc.vector.tensor_tensor(y[:, b * BT:(b + 1) * BT], bank[4 + b][:].rearrange("p (t d) -> p t d", d=D),
                                            dx[:, b * BT:(b + 1) * BT], ALU.add).then_inc(y_kept, 1)
                for t in range(TILES):
                    dve.wait_ge(y_kept, t // BT + 1)
                    nc.vector.bn_stats(stats[:, t], y[:, t]).then_inc(stats_done, 1)
                for t in range(TILES):
                    dve.wait_ge(stats_done, t + 1)
                    nc.vector.bn_aggr(mv[:, t], stats[:, t]).then_inc(mv_done, 1)
                dve.wait_ge(mv_done, TILES)
                nc.vector.tensor_scalar(var[:], mv[:, :, 1], EPS, None, ALU.add).then_inc(var_done, 1)
                dve.wait_ge(std_done, 1)
                nc.vector.reciprocal(rstd[:], std[:]).then_inc(rstd_done, 1)
                dve.wait_ge(rstd_done, 1)
                for t in range(TILES):
                    nc.vector.tensor_scalar(yn[:, t], y[:, t], mv[:, t, 0:1], rstd[:, t:t + 1],
                                            ALU.subtract, ALU.mult).then_inc(normed, 1)
                dve.wait_ge(normed, TILES)
                nc.vector.tensor_tensor(yg[:], yn[:], wide(gamma), ALU.mult).then_inc(gained, 1)
                dve.wait_ge(gained, 1)
                nc.vector.tensor_tensor(yb[:], yg[:], wide(beta), ALU.add).then_inc(shifted, 1)
                dve.wait_ge(shifted, 1)
                nc.vector.tensor_tensor(core.h[:], core.h[:], yb[:], ALU.add)


def feature_mixer(core, d):
    nc, bank = core.nc, core.bank
    with ExitStack() as ctx:
        w = core.sb(ctx, "fw", [P, 2, P])
        wm = core.sb(ctx, "fwm", [P, 2, P])
        keep = core.sb(ctx, "fkeep", [P, P])
        b1 = core.sb(ctx, "fb1", [P, 1])
        b2 = core.sb(ctx, "fb2", [P, D])
        act_out = core.sb(ctx, "fact", [P, B, S])
        hb = core.sb(ctx, "fhb", [P, TILES, D])
        loaded, masked, mm1, acted, mm2, biased = core.sems("fm", "loaded masked mm1 acted mm2 biased")
        with nc.Block() as block:
            @block.sync
            def _(sp):
                for dst, src in ((w, d["mix_w"]), (keep, d["tril_T"]), (b1, d["mix_b1"]),
                                 (b2, d["mix_b2"].partition_broadcast(P))):
                    sp.dma_start(dst[:], src).then_inc(loaded, 16)

            @block.vector
            def _(dve):
                dve.wait_ge(loaded, 64)
                nc.vector.tensor_tensor(wm[:], w[:], keep[:].unsqueeze(1).broadcast_to([P, 2, P]), ALU.mult
                                        ).then_inc(masked, 1)
                nc.vector.tensor_tensor(hb[:], core.h[:], b2[:].unsqueeze(1).broadcast_to([P, TILES, D]), ALU.add
                                        ).then_inc(biased, 1)
                dve.wait_ge(biased, 1)
                for b in range(B):
                    dve.wait_ge(mm2, b + 1)
                    nc.vector.tensor_tensor(core.h[:, b * BT:(b + 1) * BT],
                                            bank[4 + b][:].rearrange("p (t d) -> p t d", d=D),
                                            hb[:, b * BT:(b + 1) * BT], ALU.add)

            @block.tensor
            def _(pe):
                pe.wait_ge(masked, 1)
                for b in range(B):
                    nc.tensor.matmul(bank[b][:], wm[:, 0], core.xT[:, b * S:(b + 1) * S], start=True,
                                     stop=True).then_inc(mm1, 1)
                for b in range(B):
                    pe.wait_ge(acted, b + 1)
                    for t in range(BT):
                        last = nc.tensor.matmul(bank[4 + b][:, t * D:(t + 1) * D], act_out[:, b, t * P:(t + 1) * P],
                                                wm[:, 1], start=True, stop=True)
                    last.then_inc(mm2, 1)

            @block.scalar
            def _(act):
                act.wait_ge(loaded, 64)
                for b in range(B):
                    act.wait_ge(mm1, b + 1)
                    nc.scalar.activation(act_out[:, b], bank[b][:], ACT.Gelu, bias=b1[:, 0:1]).then_inc(acted, 1)


def store(core, d):
    nc = core.nc
    (stored,) = core.sems("out", "stored")
    with nc.Block() as block:
        @block.sync
        def _(sp):
            sp.dma_start(d["out"].rearrange("(t p) d -> p t d", p=P), core.h[:]).then_inc(stored, 16)
            sp.wait_ge(stored, 16)


def pack(x, **w):
    n = np
    f = n.float32

    def permute_gates(a):
        a = a.reshape(a.shape[:-1] + (4, 2, P))
        return n.ascontiguousarray(n.moveaxis(a[..., [0, 1, 3, 2], :, :], -2, -3)).reshape(a.shape[:-3] + (G4,))

    def rows(a):
        e, k, m = a.shape
        return n.moveaxis(a.reshape(e, k // P, P, m), 1, 2).reshape(e, P, k // P * m)

    def cols(a):
        return n.moveaxis(a.reshape(E, KH, P), 1, 2)

    out = {}
    pos = n.arange(N_FRAMES)[:, None] * N_FFT + n.arange(N_FFT)[None] - N_FFT // 2
    pos = n.abs(pos)
    pos = n.where(pos >= S, 2 * (S - 1) - pos, pos)
    out["ids_frames"] = n.ascontiguousarray(x[:, pos].reshape(BF, N_FFT).T)
    out["ids"] = n.ascontiguousarray(x.reshape(TOK))
    out["vocab_row"] = n.broadcast_to(n.arange(VOCAB, dtype=f), (N_FFT, VOCAB)).copy()
    out["vocab_col"] = n.arange(VOCAB, dtype=f)[:, None].copy()
    j = n.arange(N_FFT, dtype=n.float64)[:, None]
    fr = n.arange(N_FREQ, dtype=n.float64)[None]
    win = 0.5 - 0.5 * n.cos(2 * n.pi * j / N_FFT)
    ang = 2 * n.pi * (j * fr % N_FFT) / N_FFT
    out["dft"] = n.stack([win * n.cos(ang), win * n.sin(ang)], 1).astype(f)
    up = n.zeros((BF, TOK), f)
    for b in range(B):
        up[b * N_FRAMES + n.arange(S) * N_FRAMES // S, b * S + n.arange(S)] = 1
    out["upsample"] = up
    out["ident"] = n.eye(P, dtype=f)
    out["causal"] = n.where(n.arange(P)[None] > n.arange(P)[:, None], f(-1e30), f(0)).astype(f)
    out["emb_table"] = w["L0_tok_emb_table"]
    out["proj_w"] = w["L0_tok_proj_w"].reshape(N_FREQ, VOCAB, D_STFT)
    out["proj_b"] = w["L0_tok_proj_b"]
    qkv = [n.moveaxis(w[f"L0_attn_W_{c}"], 0, 1).reshape(D, AH * ADK) for c in "qkv"]
    wo = n.moveaxis(w["L0_attn_W_o"].reshape(4, P, D), 0, 1).reshape(P, 4 * D)
    out["attn_w"] = n.stack(qkv + [wo], 1)
    for name in ("router_w", "router_b"):
        out[name] = w["L0_ffn_" + name]
    ff = {k[len("L0_ffn_"):]: v for k, v in w.items() if k.startswith("L0_ffn_")}
    out["w_encode"] = n.concatenate([rows(ff[c]) for c in ("enc_w1", "enc_w2", "attn_in_w")], 2)
    out["w_attend"] = n.concatenate(
        [rows(ff["attn_out_w"]), rows(permute_gates(ff["lstm_wi_f"])), rows(permute_gates(ff["lstm_wi_b"]))], 2)
    out["w_after"] = n.concatenate([rows(ff[c]) for c in ("sig_w1", "tan_w1", "sig_w2", "tan_w2", "dec_w1", "dec_w2")], 2)
    inb = ff["attn_in_b"]
    out["cols"] = n.concatenate(
        [cols(a) for a in (ff["enc_b1"], ff["enc_g"], ff["enc_beta"], inb[:, 0:DM], inb[:, DM:2 * DM],
                           ff["attn_out_b"], ff["sig_b1"], ff["tan_b1"], ff["sig_b2"], ff["tan_b2"], ff["dec_b1"])], 2)
    out["rows"] = n.concatenate(
        [ff["enc_b2"], inb[:, 2 * DM:], permute_gates(ff["lstm_b_f"]), permute_gates(ff["lstm_b_b"]), ff["dec_b2"],
         ff["dec_g"], ff["dec_beta"]], 1)
    out["wh"] = n.ascontiguousarray(n.stack([rows(permute_gates(ff["lstm_wh_" + c])) for c in "fb"])
                                    .reshape(2, E, P, KH, G4).transpose(2, 0, 1, 3, 4))
    ss = {k[len("L1_attn_"):]: v for k, v in w.items() if k.startswith("L1_attn_")}
    out["B_T"] = ss["B_mat"].T
    out["C_T"] = n.concatenate([ss["C_mat"].T, ss["C_mat"].T], 0)
    out["A_log"] = n.concatenate([ss["A_log"], ss["A_log"]])[:, None]
    out["dt_w"] = ss["dt_w"].reshape(D, 1)
    for name in ("dt_b", "D_vec", "gamma", "beta"):
        out[name] = ss[name]
    out["mix_w"] = n.stack([w["L1_ffn_W1"].T, w["L1_ffn_W2"].T], 1)
    out["tril_T"] = n.triu(n.ones((P, P), f))
    out["mix_b1"] = w["L1_ffn_b1"][:, None]
    out["mix_b2"] = w["L1_ffn_b2"]
    return out


def build(nc, d):
    with ExitStack() as ctx:
        core = Core(nc, ctx)
        d["zx"] = nc.dram_tensor("zx", (2, E, B, S, G4), F32, kind="Internal").ap()
        d["qk"] = nc.dram_tensor("qk", (E * B + 1, 2, 3, DM, S), BF16, kind="Internal").ap()
        d["vx"] = nc.dram_tensor("vx", (E * B, P, BT * NH * (DH + 1)), F32, kind="Internal").ap()
        d["hs"] = nc.dram_tensor("hs", (2, E, B, S, DM), F32, kind="Internal").ap()
        for phase in PHASES:
            core.run(phase, d)
        core.run(store, d)


PHASES = [
    embed,
    lambda core, d: layer_norm(core, "ln0"),
    causal_attention,
    lambda core, d: layer_norm(core, "ln1"),
    router,
    experts_encode,
    experts_attend,
    recurrence,
    experts_after,
    lambda core, d: layer_norm(core, "ln2"),
    state_space,
    lambda core, d: layer_norm(core, "ln3"),
    feature_mixer,
]


def kernel(**inputs):
    import concourse.bacc as bacc
    from concourse.bass_utils import run_bass_kernel_spmd

    nc = bacc.Bacc("TRN2", target_bir_lowering=False, num_devices=1)
    arrays = pack(**{k: np.asarray(v) for k, v in inputs.items()})
    arrays = {f"in_{k}": np.ascontiguousarray(v) for k, v in arrays.items()}
    d = {k[3:]: nc.dram_tensor(k, a.shape, mybir.dt.from_np(a.dtype), kind="ExternalInput").ap()
         for k, a in arrays.items()}
    d["out"] = nc.dram_tensor("out", (TOK, D), F32, kind="ExternalOutput").ap()
    build(nc, d)
    r = run_bass_kernel_spmd(nc, [arrays], core_ids=[0])
    return r.results[0]["out"].reshape(B, S, D)
```
